# Optimizing a Trainium2 kernel written in Bass

```python
import numpy as np
import jax
import jax.numpy as jnp

def _softmax(x, axis=-1):
    return jax.nn.softmax(x, axis=axis)

def _gelu(x):
    return jax.nn.gelu(x, approximate=True)

def _silu(x):
    return jax.nn.silu(x)

def _sigmoid(x):
    return jax.nn.sigmoid(x)

def _layernorm(x, axis=-1, eps=1e-05):
    m = jnp.mean(x, axis=axis, keepdims=True)
    v = jnp.var(x, axis=axis, keepdims=True)
    return (x - m) / jnp.sqrt(v + eps)

def _scatter_add(tgt, idx, src, axis=0):
    return tgt.at[idx].add(src)

def _segment_sum(src, seg, n):
    return jax.ops.segment_sum(src, seg, n)
kernel_name = 'mk_seq_preln_d2_jaxref_r8_119469'

def setup_inputs(seed: int=0):
    np.random.seed(seed)
    _w = jnp.asarray

    def _L0_attn_setup():
        import jax, jax.numpy as jnp
        import numpy as np
        B, T, E, H = (2, 256, 128, 16)
        D = E // H
        key = jax.random.key(seed)
        k = jax.random.split(key, 6)
        return {'x': jax.random.normal(k[0], (B, T, E), dtype=jnp.float32), 'w_att_val': jax.random.normal(k[1], (H, D, D), dtype=jnp.float32) * (6.0 / D) ** 0.5, 'wv_w': jax.random.normal(k[2], (E, E), dtype=jnp.float32) * E ** (-0.5), 'wv_b': jnp.zeros((E,), dtype=jnp.float32), 'out_w': jax.random.normal(k[3], (E, E), dtype=jnp.float32) * E ** (-0.5), 'out_b': jnp.zeros((E,), dtype=jnp.float32)}
    _L0_attn_in = _L0_attn_setup()

    def _L0_ffn_setup():
        import jax, jax.numpy as jnp
        import numpy as np
        D_MODEL = 128
        N_HEADS = 16
        HEAD_DIM = D_MODEL // N_HEADS
        KV_LATENT = 64
        N_EXPERTS = 4
        D_HIDDEN = 4 * D_MODEL
        B, T = (2, 128)

        def rmsnorm(x, w, eps=1e-06):
            return w * (x * jax.lax.rsqrt(jnp.mean(x * x, axis=-1, keepdims=True) + eps))

        def layernorm(x, g, b, eps=1e-05):
            mu = jnp.mean(x, axis=-1, keepdims=True)
            var = jnp.mean((x - mu) ** 2, axis=-1, keepdims=True)
            return (x - mu) * jax.lax.rsqrt(var + eps) * g + b

        def apply_rope(x):
            t, d = (x.shape[2], x.shape[3])
            half = d // 2
            pos = jnp.arange(t, dtype=x.dtype)[:, None]
            inv_freq = 1.0 / 10000.0 ** (jnp.arange(half, dtype=x.dtype) / half)
            ang = pos * inv_freq[None, :]
            sin, cos = (jnp.sin(ang), jnp.cos(ang))
            x1, x2 = (x[..., :half], x[..., half:])
            return jnp.concatenate([x1 * cos - x2 * sin, x1 * sin + x2 * cos], axis=-1)

        def mla_attention(x, Wq, Wdkv, Wuk, Wuv, Wo, ln_g, ln_b):
            b, t, _ = x.shape
            q = (x @ Wq.T).reshape(b, t, N_HEADS, HEAD_DIM).transpose(0, 2, 1, 3)
            latent = layernorm(x @ Wdkv.T, ln_g, ln_b)
            k = (latent @ Wuk.T).reshape(b, t, N_HEADS, HEAD_DIM).transpose(0, 2, 1, 3)
            v = (latent @ Wuv.T).reshape(b, t, N_HEADS, HEAD_DIM).transpose(0, 2, 1, 3)
            q = apply_rope(q)
            k = apply_rope(k)
            scores = jnp.einsum('bhqd,bhkd->bhqk', q, k) / np.sqrt(HEAD_DIM)
            causal = jnp.tril(jnp.ones((t, t), dtype=bool))
            scores = jnp.where(causal, scores, -jnp.inf)
            attn = jax.nn.softmax(scores, axis=-1)
            out = jnp.einsum('bhqk,bhkd->bhqd', attn, v).transpose(0, 2, 1, 3).reshape(b, t, D_MODEL)
            return out @ Wo.T

        def moe(x, gate_w, gate_b, W1, b1, W2, b2):
            logits = x @ gate_w.T + gate_b
            top = jnp.argmax(logits, axis=-1)
            onehot = jax.nn.one_hot(top, N_EXPERTS, dtype=x.dtype)
            h = jax.nn.relu(jnp.einsum('btd,ehd->bteh', x, W1) + b1)
            y = jnp.einsum('bteh,edh->bted', h, W2) + b2
            return jnp.einsum('bted,bte->btd', y, onehot)
        key = jax.random.key(seed)
        ks = jax.random.split(key, 16)
        s = lambda fan_in: 1.0 / np.sqrt(fan_in)
        return {'x': jax.random.normal(ks[0], (B, T, D_MODEL), jnp.float32), 'norm1_w': jnp.ones((D_MODEL,), jnp.float32), 'norm2_w': jnp.ones((D_MODEL,), jnp.float32), 'Wq': jax.random.normal(ks[1], (D_MODEL, D_MODEL), jnp.float32) * s(D_MODEL), 'Wdkv': jax.random.normal(ks[2], (KV_LATENT, D_MODEL), jnp.float32) * s(D_MODEL), 'Wuk': jax.random.normal(ks[3], (D_MODEL, KV_LATENT), jnp.float32) * s(KV_LATENT), 'Wuv': jax.random.normal(ks[4], (D_MODEL, KV_LATENT), jnp.float32) * s(KV_LATENT), 'Wo': jax.random.normal(ks[5], (D_MODEL, D_MODEL), jnp.float32) * s(D_MODEL), 'ln_g': jnp.ones((KV_LATENT,), jnp.float32), 'ln_b': jnp.zeros((KV_LATENT,), jnp.float32), 'gate_w': jax.random.normal(ks[6], (N_EXPERTS, D_MODEL), jnp.float32) * s(D_MODEL), 'gate_b': jnp.zeros((N_EXPERTS,), jnp.float32), 'W1': jax.random.normal(ks[7], (N_EXPERTS, D_HIDDEN, D_MODEL), jnp.float32) * s(D_MODEL), 'b1': jnp.zeros((N_EXPERTS, D_HIDDEN), jnp.float32), 'W2': jax.random.normal(ks[8], (N_EXPERTS, D_MODEL, D_HIDDEN), jnp.float32) * s(D_HIDDEN), 'b2': jnp.zeros((N_EXPERTS, D_MODEL), jnp.float32)}
    _L0_ffn_in = _L0_ffn_setup()

    def _L1_attn_setup():
        import jax, jax.numpy as jnp
        import numpy as np
        EPS = 1e-08

        def rms_norm(x, scale):
            d = x.shape[-1]
            norm = jnp.linalg.norm(x, ord=2, axis=-1, keepdims=True)
            rms = norm * d ** (-0.5)
            return scale * (x / (rms + EPS))
        key = jax.random.key(seed)
        ks = jax.random.split(key, 4)
        B, N, C, H = (2, 256, 128, 16)
        hd = C // H
        x = jax.random.normal(ks[0], (B, N, C), dtype=jnp.float32)
        Wqkv = jax.random.normal(ks[1], (C, 3 * C), dtype=jnp.float32) * C ** (-0.5)
        Wproj = jax.random.normal(ks[2], (C, C), dtype=jnp.float32) * C ** (-0.5)
        bproj = jnp.zeros((C,), dtype=jnp.float32)
        q_scale = jnp.ones((hd,), dtype=jnp.float32)
        k_scale = jnp.ones((hd,), dtype=jnp.float32)
        return {'x': x, 'Wqkv': Wqkv, 'Wproj': Wproj, 'bproj': bproj, 'q_scale': q_scale, 'k_scale': k_scale}
    _L1_attn_in = _L1_attn_setup()

    def _L1_ffn_setup():
        import jax, jax.numpy as jnp
        import numpy as np
        B, S, D = (4, 256, 128)
        E = 8
        DFF = 512
        CAP_FACTOR = 1.25
        key = jax.random.key(seed)
        ks = jax.random.split(key, 4)
        std_gate = float(np.sqrt(0.1 / D))
        inputs = jax.random.normal(ks[0], (B, S, D), dtype=jnp.float32)
        gate_w = jax.random.normal(ks[1], (E, D), dtype=jnp.float32) * std_gate
        w1 = jax.random.normal(ks[2], (E, D, DFF), dtype=jnp.float32) * (1.0 / np.sqrt(D))
        b1 = jnp.zeros((E, DFF), dtype=jnp.float32)
        w2 = jax.random.normal(ks[3], (E, DFF, D), dtype=jnp.float32) * (1.0 / np.sqrt(DFF))
        b2 = jnp.zeros((E, D), dtype=jnp.float32)
        return {'inputs': inputs, 'gate_w': gate_w, 'w1': w1, 'b1': b1, 'w2': w2, 'b2': b2}
    _L1_ffn_in = _L1_ffn_setup()
    _d = {'L0_attn_x': _L0_attn_in['x'], 'L0_attn_w_att_val': _L0_attn_in['w_att_val'], 'L0_attn_wv_w': _L0_attn_in['wv_w'], 'L0_attn_wv_b': _L0_attn_in['wv_b'], 'L0_attn_out_w': _L0_attn_in['out_w'], 'L0_attn_out_b': _L0_attn_in['out_b'], 'L0_ffn_norm1_w': _L0_ffn_in['norm1_w'], 'L0_ffn_norm2_w': _L0_ffn_in['norm2_w'], 'L0_ffn_Wq': _L0_ffn_in['Wq'], 'L0_ffn_Wdkv': _L0_ffn_in['Wdkv'], 'L0_ffn_Wuk': _L0_ffn_in['Wuk'], 'L0_ffn_Wuv': _L0_ffn_in['Wuv'], 'L0_ffn_Wo': _L0_ffn_in['Wo'], 'L0_ffn_ln_g': _L0_ffn_in['ln_g'], 'L0_ffn_ln_b': _L0_ffn_in['ln_b'], 'L0_ffn_gate_w': _L0_ffn_in['gate_w'], 'L0_ffn_gate_b': _L0_ffn_in['gate_b'], 'L0_ffn_W1': _L0_ffn_in['W1'], 'L0_ffn_b1': _L0_ffn_in['b1'], 'L0_ffn_W2': _L0_ffn_in['W2'], 'L0_ffn_b2': _L0_ffn_in['b2'], 'L1_attn_Wqkv': _L1_attn_in['Wqkv'], 'L1_attn_Wproj': _L1_attn_in['Wproj'], 'L1_attn_bproj': _L1_attn_in['bproj'], 'L1_attn_q_scale': _L1_attn_in['q_scale'], 'L1_attn_k_scale': _L1_attn_in['k_scale'], 'L1_ffn_gate_w': _L1_ffn_in['gate_w'], 'L1_ffn_w1': _L1_ffn_in['w1'], 'L1_ffn_b1': _L1_ffn_in['b1'], 'L1_ffn_w2': _L1_ffn_in['w2'], 'L1_ffn_b2': _L1_ffn_in['b2']}
    _x0 = _d['L0_attn_x']
    _d['L0_attn_x'] = jax.random.normal(jax.random.fold_in(jax.random.key(seed), 1), (32, 256, 128), dtype=_x0.dtype)
    del _x0
    return _d

def reference(L0_attn_x, L0_attn_w_att_val, L0_attn_wv_w, L0_attn_wv_b, L0_attn_out_w, L0_attn_out_b, L0_ffn_norm1_w, L0_ffn_norm2_w, L0_ffn_Wq, L0_ffn_Wdkv, L0_ffn_Wuk, L0_ffn_Wuv, L0_ffn_Wo, L0_ffn_ln_g, L0_ffn_ln_b, L0_ffn_gate_w, L0_ffn_gate_b, L0_ffn_W1, L0_ffn_b1, L0_ffn_W2, L0_ffn_b2, L1_attn_Wqkv, L1_attn_Wproj, L1_attn_bproj, L1_attn_q_scale, L1_attn_k_scale, L1_ffn_gate_w, L1_ffn_w1, L1_ffn_b1, L1_ffn_w2, L1_ffn_b2):

    def _L0_attn_ref(x, w_att_val, wv_w, wv_b, out_w, out_b):
        import jax, jax.numpy as jnp
        import numpy as np
        B, T, E, H = (2, 256, 128, 16)
        D = E // H
        b, t, e = x.shape
        h, d, _ = w_att_val.shape
        x_h = x.reshape(b, t, h, d).transpose(0, 2, 1, 3)
        xw = jnp.einsum('bhtd,hde->bhte', x_h, w_att_val)
        att = jnp.einsum('bhte,bhse->bhts', xw, x_h) / jnp.sqrt(jnp.asarray(d, x.dtype))
        att = jax.nn.softmax(att, axis=-1)
        vx = x @ wv_w.T + wv_b
        vx = vx.reshape(b, t, h, d).transpose(0, 2, 1, 3)
        o = jnp.einsum('bhts,bhsd->bhtd', att, vx)
        o = o.transpose(0, 2, 1, 3).reshape(b, t, e)
        return o @ out_w.T + out_b

    def _L0_ffn_ref(x, norm1_w, norm2_w, Wq, Wdkv, Wuk, Wuv, Wo, ln_g, ln_b, gate_w, gate_b, W1, b1, W2, b2):
        import jax, jax.numpy as jnp
        import numpy as np
        D_MODEL = 128
        N_HEADS = 16
        HEAD_DIM = D_MODEL // N_HEADS
        KV_LATENT = 64
        N_EXPERTS = 4
        D_HIDDEN = 4 * D_MODEL
        B, T = (2, 128)

        def rmsnorm(x, w, eps=1e-06):
            return w * (x * jax.lax.rsqrt(jnp.mean(x * x, axis=-1, keepdims=True) + eps))

        def layernorm(x, g, b, eps=1e-05):
            mu = jnp.mean(x, axis=-1, keepdims=True)
            var = jnp.mean((x - mu) ** 2, axis=-1, keepdims=True)
            return (x - mu) * jax.lax.rsqrt(var + eps) * g + b

        def apply_rope(x):
            t, d = (x.shape[2], x.shape[3])
            half = d // 2
            pos = jnp.arange(t, dtype=x.dtype)[:, None]
            inv_freq = 1.0 / 10000.0 ** (jnp.arange(half, dtype=x.dtype) / half)
            ang = pos * inv_freq[None, :]
            sin, cos = (jnp.sin(ang), jnp.cos(ang))
            x1, x2 = (x[..., :half], x[..., half:])
            return jnp.concatenate([x1 * cos - x2 * sin, x1 * sin + x2 * cos], axis=-1)

        def mla_attention(x, Wq, Wdkv, Wuk, Wuv, Wo, ln_g, ln_b):
            b, t, _ = x.shape
            q = (x @ Wq.T).reshape(b, t, N_HEADS, HEAD_DIM).transpose(0, 2, 1, 3)
            latent = layernorm(x @ Wdkv.T, ln_g, ln_b)
            k = (latent @ Wuk.T).reshape(b, t, N_HEADS, HEAD_DIM).transpose(0, 2, 1, 3)
            v = (latent @ Wuv.T).reshape(b, t, N_HEADS, HEAD_DIM).transpose(0, 2, 1, 3)
            q = apply_rope(q)
            k = apply_rope(k)
            scores = jnp.einsum('bhqd,bhkd->bhqk', q, k) / np.sqrt(HEAD_DIM)
            causal = jnp.tril(jnp.ones((t, t), dtype=bool))
            scores = jnp.where(causal, scores, -jnp.inf)
            attn = jax.nn.softmax(scores, axis=-1)
            out = jnp.einsum('bhqk,bhkd->bhqd', attn, v).transpose(0, 2, 1, 3).reshape(b, t, D_MODEL)
            return out @ Wo.T

        def moe(x, gate_w, gate_b, W1, b1, W2, b2):
            logits = x @ gate_w.T + gate_b
            top = jnp.argmax(logits, axis=-1)
            onehot = jax.nn.one_hot(top, N_EXPERTS, dtype=x.dtype)
            h = jax.nn.relu(jnp.einsum('btd,ehd->bteh', x, W1) + b1)
            y = jnp.einsum('bteh,edh->bted', h, W2) + b2
            return jnp.einsum('bted,bte->btd', y, onehot)
        x = x + mla_attention(rmsnorm(x, norm1_w), Wq, Wdkv, Wuk, Wuv, Wo, ln_g, ln_b)
        x = x + moe(rmsnorm(x, norm2_w), gate_w, gate_b, W1, b1, W2, b2)
        return x

    def _L1_attn_ref(x, Wqkv, Wproj, bproj, q_scale, k_scale):
        import jax, jax.numpy as jnp
        import numpy as np
        EPS = 1e-08

        def rms_norm(x, scale):
            d = x.shape[-1]
            norm = jnp.linalg.norm(x, ord=2, axis=-1, keepdims=True)
            rms = norm * d ** (-0.5)
            return scale * (x / (rms + EPS))
        B, N, C = x.shape
        H = 16
        hd = C // H
        scale = hd ** (-0.5)
        qkv = (x @ Wqkv).reshape(B, N, 3, H, hd)
        qkv = jnp.transpose(qkv, (2, 0, 3, 1, 4))
        q, k, v = (qkv[0], qkv[1], qkv[2])
        q = rms_norm(q, q_scale)
        k = rms_norm(k, k_scale)
        attn = jnp.einsum('bhnc,bhmc->bhnm', q, k) * scale
        attn = jax.nn.softmax(attn, axis=-1)
        out = jnp.einsum('bhnm,bhmc->bhnc', attn, v)
        out = jnp.transpose(out, (0, 2, 1, 3)).reshape(B, N, C)
        return out @ Wproj + bproj

    def _L1_ffn_ref(inputs, gate_w, w1, b1, w2, b2):
        import jax, jax.numpy as jnp
        import numpy as np
        B, S, D = (4, 256, 128)
        E = 8
        DFF = 512
        CAP_FACTOR = 1.25
        d_model = inputs.shape[-1]
        tokens = inputs.reshape(-1, d_model)
        T = tokens.shape[0]
        num_experts = gate_w.shape[0]
        capacity = int(np.ceil(CAP_FACTOR * T / num_experts))
        logits = jnp.einsum('td,ed->te', tokens.astype(jnp.float32), gate_w)
        probs = jax.nn.softmax(logits, axis=-1)
        expert_idx = jnp.argmax(probs, axis=-1)
        mask = jax.nn.one_hot(expert_idx, num_experts, dtype=jnp.float32)
        ranks = jnp.cumsum(mask, axis=0) - 1.0
        keep = (ranks < capacity) * mask
        pos = ranks.astype(jnp.int32)
        sec_mask = jax.nn.one_hot(pos, capacity, dtype=jnp.float32) * keep[:, :, None]
        combine_weights = probs[:, :, None] * sec_mask
        dispatch = jnp.einsum('tec,td->ecd', sec_mask, tokens)
        h = jax.nn.relu(jnp.einsum('ecd,edh->ech', dispatch, w1) + b1[:, None, :])
        expert_out = jnp.einsum('ech,ehd->ecd', h, w2) + b2[:, None, :]
        ans = jnp.einsum('tec,ecd->td', combine_weights, expert_out)
        return ans.reshape(inputs.shape)
    x = L0_attn_x
    x = x + _L0_attn_ref(_layernorm(x, axis=-1), L0_attn_w_att_val, L0_attn_wv_w, L0_attn_wv_b, L0_attn_out_w, L0_attn_out_b)
    x = x + _L0_ffn_ref(_layernorm(x, axis=-1), L0_ffn_norm1_w, L0_ffn_norm2_w, L0_ffn_Wq, L0_ffn_Wdkv, L0_ffn_Wuk, L0_ffn_Wuv, L0_ffn_Wo, L0_ffn_ln_g, L0_ffn_ln_b, L0_ffn_gate_w, L0_ffn_gate_b, L0_ffn_W1, L0_ffn_b1, L0_ffn_W2, L0_ffn_b2)
    x = x + _L1_attn_ref(_layernorm(x, axis=-1), L1_attn_Wqkv, L1_attn_Wproj, L1_attn_bproj, L1_attn_q_scale, L1_attn_k_scale)
    x = x + _L1_ffn_ref(_layernorm(x, axis=-1), L1_ffn_gate_w, L1_ffn_w1, L1_ffn_b1, L1_ffn_w2, L1_ffn_b2)
    return x

_drawn_inputs = setup_inputs


def setup_inputs(seed=0):
    import zlib

    import numpy as np

    out = dict(_drawn_inputs(seed))
    spreads = {'L0_attn_wv_b': (0.0, 0.1),
     'L0_attn_out_b': (0.0, 0.1),
     'L0_ffn_norm1_w': (1.0, 0.2),
     'L0_ffn_norm2_w': (1.0, 0.2),
     'L0_ffn_ln_g': (1.0, 0.2),
     'L0_ffn_ln_b': (0.0, 0.1),
     'L0_ffn_gate_b': (0.0, 0.1),
     'L0_ffn_b1': (0.0, 0.1),
     'L0_ffn_b2': (0.0, 0.1),
     'L1_attn_bproj': (0.0, 0.1),
     'L1_attn_q_scale': (1.0, 0.6),
     'L1_attn_k_scale': (1.0, 0.6),
     'L1_ffn_b1': (0.0, 0.8),
     'L1_ffn_b2': (0.0, 0.8)}
    factors = {}
    for name, (base, spread) in spreads.items():
        noise = np.random.default_rng([zlib.crc32(name.encode()), seed]).standard_normal(out[name].shape)
        drawn = base * np.exp(spread * noise) if base else spread * noise
        out[name] = jnp.asarray(drawn.astype(out[name].dtype))
    for name, factor in factors.items():
        out[name] = (out[name] * factor).astype(out[name].dtype)
    return out
```

```python
from contextlib import ExitStack, contextmanager

import numpy as np

import concourse.bass as bass
import concourse.mybir as mybir

f32 = mybir.dt.float32
bf16 = mybir.dt.bfloat16
i32 = mybir.dt.int32
u32 = mybir.dt.uint32
ALU = mybir.AluOpType
ACT = mybir.ActivationFunctionType
AX = mybir.AxisListType

B, T, D = 32, 256, 128
P = 128
H, HD = 16, 8
NT = B * T // P
TT = T // P
PAIRS = H // 2
ROWS = 6 * 2 * HD
VW = HD + 1
UNITS = 2 * B
UP = PAIRS // 2
LAT = 64
E0, F0 = 4, 512
E1, F1 = 8, 512
CAP = 1280
SLOTS = E1 * CAP
SCALE = float(HD) ** -0.5
MASKED = -1.0e30


@contextmanager
def semaphores(nc):
    taken = []

    def sem(name):
        taken.append(nc.alloc_semaphore(name))
        return taken[-1]

    yield sem
    nc.clear_and_free_semaphores(taken)
    nc.all_engine_barrier()


class Order:

    def __init__(self, per, round_):
        self.per, self.round, self.k = per, round_, 0

    def next(self):
        self.k += 1
        assert self.k <= self.per
        return self.round * self.per + self.k


def past(n):
    return not (isinstance(n, int) and n <= 0)


def layer_stats(nc, name, src, stat, rstd, eps, second_moment=False):
    G = 8
    W = src.shape[2]
    with ExitStack() as ctx:
        sem = ctx.enter_context(semaphores(nc))
        sb = lambda n, s: ctx.enter_context(nc.sbuf_tensor(f"{name}_{n}", s, f32))
        parts, root, apart = sb("parts", [P, NT, 6]), sb("root", [P, NT]), sb("apart", [P, NT])
        split, order, shifted, rooted = (sem(f"{name}_{x}") for x in ("split", "order", "shifted", "rooted"))
        block = ctx.enter_context(nc.Block())

        @block.vector
        def _(dve):
            with dve.Fori(0, NT // G) as j:
                for g in range(G):
                    nc.vector.bn_stats(parts[:, bass.ds(j * G + g, 1), :].rearrange("p o d -> p (o d)"),
                                       src[:, bass.ds(j * G + g, 1), :].rearrange("p o d -> p (o d)")).then_inc(split, 1)
            dve.wait_ge(split, NT)
            mean, var = stat[:, :, 0], stat[:, :, 1]
            nc.vector.tensor_tensor(apart[:, :], parts[:, :, 1], parts[:, :, 4], ALU.subtract).then_inc(order, 1)
            nc.vector.tensor_tensor(mean, parts[:, :, 1], parts[:, :, 4], ALU.add).then_inc(order, 1)
            nc.vector.tensor_tensor(var, parts[:, :, 2], parts[:, :, 5], ALU.add).then_inc(order, 1)
            dve.wait_ge(order, 3)
            nc.vector.tensor_scalar(mean, mean, 0.5, None, ALU.mult).then_inc(order, 1)
            nc.vector.tensor_scalar(var, var, 1.0 / W, None, ALU.mult).then_inc(order, 1)
            nc.vector.scalar_tensor_tensor(out=apart[:, :], in0=apart[:, :], scalar=0.25, in1=apart[:, :],
                                           op0=ALU.mult, op1=ALU.mult).then_inc(order, 1)
            dve.wait_ge(order, 6)
            nc.vector.tensor_tensor(var, var, apart[:, :], ALU.add).then_inc(order, 1)
            dve.wait_ge(order, 7)
            if second_moment:
                nc.vector.tensor_tensor(root[:, :], mean, mean, ALU.mult).then_inc(order, 1)
                dve.wait_ge(order, 8)
                nc.vector.tensor_tensor(root[:, :], root[:, :], var, ALU.add).then_inc(order, 1)
                dve.wait_ge(order, 9)
                nc.vector.tensor_scalar(root[:, :], root[:, :], eps, None, ALU.add).then_inc(shifted, 1)
            else:
                nc.vector.tensor_scalar(root[:, :], var, eps, None, ALU.add).then_inc(shifted, 1)
            dve.wait_ge(rooted, 1)
            nc.vector.reciprocal(rstd[:, :], root[:, :])

        @block.scalar
        def _(act):
            act.wait_ge(shifted, 1)
            nc.scalar.activation(root[:, :], root[:, :], ACT.Sqrt).then_inc(rooted, 1)


def project(nc, kind, m, w):
    plain, cosine, queries, keys = (kind == k for k in ("plain", "cosine", "queries", "keys"))
    rope = queries or keys
    W = LAT if keys else D
    NQ = 1 if rope else 2
    has_v = not queries
    with ExitStack() as ctx:
        sb = lambda n, s, d=f32: ctx.enter_context(nc.sbuf_tensor(f"{kind}_{n}", s, d))
        ps = lambda n, s, d=f32: ctx.enter_context(nc.psum_tensor(f"{kind}_{n}", s, d))
        new_sem = ctx.enter_context(semaphores(nc))
        sem = lambda n: new_sem(f"{kind}_{n}")
        src, stat, rstd = (m.lat, m.lat_stat, m.lat_rstd) if keys else (m.x, m.x_stat, m.x_rstd)
        xn = sb("xn", [P, 2, TT, W])
        qk = sb("qk", [P, 2, NQ, T])
        xT = qk[:, :, 1, :] if plain else sb("xT", [W, 2, T])[:, :, :]
        rest = sb("rest", [P, 2, NQ, T])
        parts = sb("parts", [P, 2, 3, NQ, T], bf16)
        wq = sb("wq", [W, D])
        loads = []
        if has_v:
            wv = sb("wv", [W, D])
            vt = sb("vt", [P, 2, TT, H, VW])
            pv = ps("pv", [P, 512])
            v_ready, v_taken = sem("v_ready"), sem("v_taken")
        turn = [ps(f"turn{u}", [P, 512]) for u in range(2)]
        pq = ps("pq", [P, 512])
        pq2 = None if plain else ps("pq2", [P, 512])
        weights_in, cleared = sem("weights_in"), sem("cleared")
        normed = sem("normed")
        turned = sem("turned")
        x_ready = sem("x_ready")
        q_ready = sem("q_ready")
        q_taken = sem("q_taken")
        qk_ready = sem("qk_ready")
        high, left, middle, low = sem("high"), sem("left"), sem("middle"), sem("low")
        stored = [sem(f"stored{u}") for u in range(2)]
        STORES = 3 * NQ + has_v
        ordered = sem("ordered")

        if plain:
            bv = sb("bv", [P, D])
            loads = [(wq[:, :], w["watt"]), (wv[:, :], w["wvT"]), (bv[:, :], w["bv"].partition_broadcast(P))]
        if cosine:
            wk = sb("wk", [P, D])
            qkscale = sb("qkscale", [P, 2])
            ones = sb("ones", [P, P])
            square = sb("square", [P, 2, NQ, T])
            rms = sb("rms", [P, 2, NQ, T])
            pss = ps("pss", [P, 512])
            squared, summed, rooted = (sem(x) for x in ("squared", "summed", "rooted"))
            loads = [(wq[:, :], w["wqkv"][:, 0:D]), (wk[:, :], w["wqkv"][:, D:2 * D]),
                     (wv[:, :], w["wqkv"][:, 2 * D:3 * D]), (ones[:, :], w["same_head"])]
            loads += [(qkscale[:, n:n + 1], w[x]) for n, x in enumerate(("qs", "ks"))]
        if rope:
            wq2 = sb("wq2", [W, D])
            gain = sb("gain", [W, 1])
            cos_t, sin_t = sb("cos", [P, T]), sb("sin", [P, T])
            a1, a2 = sb("a1", [P, 2, T]), sb("a2", [P, 2, T])
            multiplied = sem("multiplied")
            loads = [(cos_t[:, :], w["cos"]), (sin_t[:, :], w["sin"])]
        if queries:
            rr = sb("rr", [P, NT])
            wd = sb("wd", [P, LAT])
            pl = ps("pl", [P, 512])
            lat_made, lat_kept = sem("lat_made"), sem("lat_kept")
            r_made, r_root = sem("r_made"), sem("r_root")
            loads += [(wq[:, :], w["wqT"]), (wq2[:, :], w["wqrT"]), (wd[:, :], w["wdT"]), (gain[:, :], w["n1"])]
        if keys:
            shift = sb("shift", [W, 1])
            loads += [(wq[:, :], w["wkT"]), (wq2[:, :], w["wkrT"]), (wv[:, :], w["wvT0"]),
                      (gain[:, :], w["lg"]), (shift[:, :], w["lb"])]
        N_LOADS = len(loads)
        block = ctx.enter_context(nc.Block())

        def sequences(eng, step):
            for u in range(2):
                step(0, u)
            with eng.Fori(1, B // 2 - 1) as j:
                for u in range(2):
                    step(j, u)
            for u in range(2):
                step(B // 2 - 1, u)

        def last(j, u):
            return isinstance(j, int) and j * 2 + u == B - 1

        @block.sync
        def _(sp):
            for dst, s in loads:
                sp.dma_start(dst, s).then_inc(weights_in, 16)

            def step(j, u):
                b = j * 2 + u
                sp.wait_ge(low, b + 1)
                picks = {"q": ((0, 3, 0, True), (3, 2, 1, True), (5, 1, 2, True)),
                         "k": ((0, 3, 0, False), (3, 2, 0, False), (5, 1, 0, False))}
                for n, name in enumerate("q" if queries else "k" if keys else "qk"):
                    dram = m.q_dram if name == "q" else m.k_dram
                    for r, count, part, repeated in picks[name]:
                        dst = dram[bass.ds(b, 1), r:r + count, :, :, :, :].rearrange("o r d x p t -> (o d x p) r t")
                        src_ = (parts[:, u, part:part + 1, n, :].broadcast_to([P, count, T]) if repeated else
                                parts[:, u, part:part + count, n, :])
                        sp.dma_start(dst, src_).then_inc(stored[u], 16)
                if has_v:
                    sp.wait_ge(v_taken, b + 1)
                    sp.dma_start(m.v_dram[bass.ds(b, 1), :, :, :].rearrange("o p t c -> (o p) t c"),
                                 vt[:, u, :, :, :].rearrange("p t h c -> p t (h c)")).then_inc(stored[u], 16)

            sequences(sp, step)
            for u in range(2):
                sp.wait_ge(stored[u], STORES * 16 * (B // 2))

        @block.gpsimd
        def _(pool):
            if has_v:
                for u in range(2):
                    nc.gpsimd.memset(vt[:, u, :, :, :], 1.0).then_inc(cleared, 1)

            def step(j, u):
                b = j * 2 + u
                if rope:
                    pool.wait_ge(multiplied, b * 2 + 2)
                    if past(b - 1):
                        pool.wait_ge(left, b - 1)
                        pool.wait_ge(high, b - 1)
                    nc.gpsimd.tensor_tensor(qk[:, u, 0, :], a1[:, u, :], a2[:, u, :], ALU.add).then_inc(qk_ready, 1)
                pool.wait_ge(middle, b + 1)
                nc.gpsimd.tensor_tensor(parts[:, u, 2, :, :], rest[:, u, :, :], parts[:, u, 1, :, :],
                                        ALU.subtract).then_inc(low, 1)
            sequences(pool, step)

        @block.vector
        def _(dve):
            if queries:
                nc.vector.tensor_tensor(rr[:, :], rstd[:, :], rstd[:, :], ALU.mult).then_inc(r_made, 1)
                dve.wait_ge(r_made, 1)
                nc.vector.tensor_tensor(rr[:, :], rr[:, :], stat[:, :, 1], ALU.mult).then_inc(r_made, 1)
                dve.wait_ge(r_made, 2)
                nc.vector.tensor_scalar(rr[:, :], rr[:, :], 1e-6, None, ALU.add).then_inc(r_made, 1)
                dve.wait_ge(r_root, 1)
                nc.vector.reciprocal(rr[:, :], rr[:, :]).then_inc(r_made, 1)
                dve.wait_ge(r_made, 4)

            def normalize(j, u):
                b = j * 2 + u
                if past(b - 1):
                    dve.wait_ge(turned, b - 1)
                for t in range(TT):
                    n = j * (2 * TT) + (u * TT + t)
                    row = src[:, bass.ds(n, 1), :].rearrange("p o d -> p (o d)")
                    mean, inv = stat[:, bass.ds(n, 1), 0], rstd[:, bass.ds(n, 1)]
                    if queries:
                        y = m.y[:, bass.ds(n, 1), :].rearrange("p o d -> p (o d)")
                        nc.vector.tensor_scalar(y, row, mean, inv, ALU.subtract, ALU.mult).then_inc(ordered, 1)
                        dve.wait_ge(ordered, b * TT + t + 1)
                        nc.vector.tensor_scalar(xn[:, u, t, :], y, rr[:, bass.ds(n, 1)], None, ALU.mult)\
                            .then_inc(normed, 1)
                    else:
                        dst = xn[:, u, t, :]
                        if plain:
                            dst, row_ = (v.rearrange(r, **z) for v, r, z in (
                                (dst, "p (d x q) -> p d x q", dict(x=2, d=HD)), (row, "p (q x d) -> p d x q", dict(x=2, d=HD))))
                        nc.vector.tensor_scalar(dst, row_ if plain else row, mean, inv, ALU.subtract, ALU.mult)\
                            .then_inc(normed, 1)
                    if plain or cosine:
                        dve.wait_ge(normed, b * TT + t + 1)
                        nc.vector.tensor_tensor(row, row, (m.out_bias if plain else m.proj_bias)[:, :], ALU.add)

            if plain or cosine:
                dve.wait_ge(weights_in, 16 * N_LOADS)
            if rope:
                dve.wait_ge(weights_in, 16 * N_LOADS)
            if has_v:
                dve.wait_ge(cleared, 2)
            normalize(0, 0)

            def step(j, u):
                b = j * 2 + u
                if not last(j, u):
                    normalize(j + u, 1 - u)
                if rope:
                    if past(b - 1):
                        dve.wait_ge(qk_ready, b - 1)
                    dve.wait_ge(q_ready, b + 1)
                    nc.vector.tensor_tensor(a1[:, u, :], pq[:, 0:T], cos_t[:, :], ALU.mult).then_inc(multiplied, 1)
                    nc.vector.tensor_tensor(a2[:, u, :], pq2[:, 0:T], sin_t[:, :], ALU.mult).then_inc(multiplied, 1)
                if queries:
                    dve.wait_ge(lat_made, b + 1)
                    nc.vector.tensor_copy(m.lat[:, bass.ds(j * (2 * TT) + u * TT, TT), :],
                                          pl[:, 0:TT * LAT].rearrange("p (t c) -> p t c", t=TT)).then_inc(lat_kept, 1)
                if has_v:
                    dve.wait_ge(v_ready, b + 1)
                    if past(j):
                        dve.wait_ge(stored[u], j * (STORES * 16))
                    pv4 = pv[:, 0:TT * D].rearrange("p (t h c) -> p t h c", t=TT, h=H)
                    if plain:
                        for t in range(TT):
                            i = nc.vector.tensor_tensor(vt[:, u, t, :, 0:HD], pv4[:, t, :, :],
                                                        bv[:, :].rearrange("p (h c) -> p h c", h=H), ALU.add)
                        i.then_inc(v_taken, 1)
                    else:
                        for t in range(TT):
                            i = nc.vector.tensor_copy(vt[:, u, t, :, 0:HD], pv4[:, t, :, :])
                        i.then_inc(v_taken, 1)
                if cosine:
                    dve.wait_ge(rooted, b + 1)
                    if past(b - 1):
                        dve.wait_ge(high, b - 1)
                    o = Order(2, b)
                    nc.vector.tensor_scalar(rms[:, u, :, :], rms[:, u, :, :], 1e-8, None, ALU.add).then_inc(ordered, 1)
                    dve.wait_ge(ordered, o.next())
                    nc.vector.reciprocal(rms[:, u, :, :], rms[:, u, :, :]).then_inc(ordered, 1)
                    dve.wait_ge(ordered, o.next())
                    for n, p_ in enumerate((pq, pq2)):
                        i = nc.vector.scalar_tensor_tensor(out=qk[:, u, n, :], in0=p_[:, 0:T],
                                                           scalar=qkscale[:, n:n + 1], in1=rms[:, u, n, :],
                                                           op0=ALU.mult, op1=ALU.mult)
                    i.then_inc(qk_ready, 1)
                dve.wait_ge(high, b + 1)
                if past(b - 1):
                    dve.wait_ge(low, b - 1)
                nc.vector.tensor_tensor(rest[:, u, :, :], qk[:, u, :, :], parts[:, u, 0, :, :],
                                        ALU.subtract).then_inc(left, 1)

            sequences(dve, step)

        @block.tensor
        def _(pe):
            def turns(j, u):
                b = j * 2 + u
                pe.wait_ge(normed, b * TT + TT)
                if past(b - 1):
                    pe.wait_ge(x_ready, b - 1)
                for t in range(TT):
                    if keys:
                        i = nc.tensor.matmul(turn[u][0:W, t * P:(t + 1) * P], xn[:, u, t, :], m.ident[:, :],
                                             start=True, stop=True)
                    else:
                        i = nc.tensor.transpose(turn[u][0:W, t * P:(t + 1) * P], xn[:, u, t, :], m.ident[:, :])
                i.then_inc(turned, 1)

            turns(0, 0)
            pe.wait_ge(weights_in, 16 * N_LOADS)

            def step(j, u):
                b = j * 2 + u
                if not last(j, u):
                    turns(j + u, 1 - u)
                pe.wait_ge(x_ready, b + 1)
                if past(b):
                    if plain:
                        pe.wait_ge(q_taken, b)
                    elif rope:
                        pe.wait_ge(multiplied, b * 2)
                    else:
                        pe.wait_ge(qk_ready, b)
                i = nc.tensor.matmul(pq[:, 0:T], wq[:, :], xT[:, u, :], start=True, stop=True)
                if not plain:
                    i = nc.tensor.matmul(pq2[:, 0:T], (wk if cosine else wq2)[:, :], xT[:, u, :], start=True, stop=True)
                i.then_inc(q_ready, 1)
                if queries:
                    if past(b):
                        pe.wait_ge(lat_kept, b)
                    for t in range(TT):
                        i = nc.tensor.matmul(pl[:, t * LAT:(t + 1) * LAT], xT[:, u, t * P:(t + 1) * P], wd[:, :],
                                             start=True, stop=True)
                    i.then_inc(lat_made, 1)
                if has_v:
                    if past(b):
                        pe.wait_ge(v_taken, b)
                    for t in range(TT):
                        i = nc.tensor.matmul(pv[:, t * D:(t + 1) * D], xT[:, u, t * P:(t + 1) * P], wv[:, :],
                                             start=True, stop=True)
                    i.then_inc(v_ready, 1)
                if cosine:
                    pe.wait_ge(squared, b + 1)
                    if past(b):
                        pe.wait_ge(rooted, b)
                    nc.tensor.matmul(pss[:, 0:NQ * T], ones[:, :], square[:, u, :, :].rearrange("p n t -> p (n t)"),
                                     start=True, stop=True).then_inc(summed, 1)

            sequences(pe, step)

        @block.scalar
        def _(act):
            if queries:
                act.wait_ge(r_made, 3)
                nc.scalar.activation(rr[:, :], rr[:, :], ACT.Sqrt).then_inc(r_root, 1)
            if rope:
                act.wait_ge(weights_in, 16 * N_LOADS)

            def take(j, u):
                b = j * 2 + u
                act.wait_ge(turned, b + 1)
                if past(b - 1):
                    act.wait_ge(q_ready if queries else v_ready, b - 1)
                    if queries:
                        act.wait_ge(lat_made, b - 1)
                    if plain:
                        act.wait_ge(left, b - 1)
                        act.wait_ge(high, b - 1)
                if rope:
                    nc.scalar.activation(xT[:, u, :], turn[u][0:W, 0:T], ACT.Identity, scale=gain[:, :],
                                         bias=shift[:, :] if keys else 0.0).then_inc(x_ready, 1)
                else:
                    nc.scalar.activation(xT[:, u, :], turn[u][0:W, 0:T], ACT.Copy).then_inc(x_ready, 1)

            take(0, 0)

            def step(j, u):
                b = j * 2 + u
                if not last(j, u):
                    take(j + u, 1 - u)
                if plain:
                    act.wait_ge(q_ready, b + 1)
                    if past(b - 1):
                        act.wait_ge(left, b - 1)
                        act.wait_ge(high, b - 1)
                    nc.scalar.activation(qk[:, u, 0, :], pq[:, 0:T], ACT.Copy).then_inc(q_taken, 1)
                    act.wait_ge(q_taken, b + 1)
                    act.wait_ge(x_ready, b + 1)
                if cosine:
                    act.wait_ge(q_ready, b + 1)
                    if past(b - 1):
                        act.wait_ge(summed, b - 1)
                    for n, p_ in enumerate((pq, pq2)):
                        i = nc.scalar.activation(square[:, u, n, :], p_[:, 0:T], ACT.Square)
                    i.then_inc(squared, 1)
                    act.wait_ge(summed, b + 1)
                    if past(b - 1):
                        act.wait_ge(qk_ready, b - 1)
                    nc.scalar.activation(rms[:, u, :, :].rearrange("p n t -> p (n t)"), pss[:, 0:NQ * T], ACT.Sqrt,
                                         scale=1.0 / HD).then_inc(rooted, 1)
                if not plain:
                    act.wait_ge(qk_ready, b + 1)
                if past(j):
                    act.wait_ge(stored[u], j * (STORES * 16))
                nc.scalar.activation(parts[:, u, 0, :, :], qk[:, u, :, :], ACT.Copy).then_inc(high, 1)
                act.wait_ge(left, b + 1)
                nc.scalar.activation(parts[:, u, 1, :, :], rest[:, u, :, :], ACT.Copy).then_inc(middle, 1)

            sequences(act, step)


def attend(nc, kind, m, w):
    causal = kind == "causal"
    RING = 4
    QUAD = 4
    SW = T + (P if causal else T)
    with ExitStack() as ctx:
        sb = lambda n, s, d=f32: ctx.enter_context(nc.sbuf_tensor(f"{kind}{m.serial}_{n}", s, d))
        ps = lambda n, s, d=f32: ctx.enter_context(nc.psum_tensor(f"{kind}{m.serial}_{n}", s, d))
        new_sem = ctx.enter_context(semaphores(nc))
        sem = lambda n: new_sem(f"{kind}{m.serial}_{n}")
        resid = m.y if causal else m.x
        qst, kst = m.qst, m.kst
        vst = sb("vst", [P, RING, TT, H // 2, VW])
        neg = sb("neg", [P, 2, TT, 2, UP])
        msp = sb("msp", [P, 2, TT, 2, 2, UP], bf16)
        mrow = sb("mrow", [2 * 2 * UP, 2, T], bf16)
        prob = sb("prob", [P, UP, 2, SW])
        usb = sb("usb", [P, 2, T])
        rec = sb("rec", [P, TT * H // 2])
        o = sb("o", [P, TT, D])
        oT = sb("oT", [P, T])
        wo = sb("wo", [P, D])
        ps_s = [ps(f"s{t}", [P, 512]) for t in range(2)]
        ps_st = [ps(f"st{t}", [P, 2, 512]) for t in range(2)]
        ps_u = ps("u", [P, 512])
        ps_m = ps("m", [P, 512])

        w_in = sem("w_in")
        stack_in = [sem(f"stack_in{k}") for k in range(RING)]
        mrow_in = [sem(f"mrow_in{k}") for k in range(RING)]
        s_ready, s_read = sem("s_ready"), sem("s_read")
        halved = sem("halved")
        msplit, mturned, mrow_ready = sem("msplit"), sem("mturned"), sem("mrow_ready")
        st_ready, exp_done = sem("st_ready"), sem("exp_done")
        pv_done, u_out = sem("pv_done"), sem("u_out")
        t_ready, inverted, t_read = sem("t_ready"), sem("inverted"), sem("t_read")
        ot_ready, ot_out = sem("ot_ready"), sem("ot_out")
        proj_ready, added = sem("proj_ready"), sem("added")
        cleared = sem("u_cleared")
        STACK_DMAS, MROW_DMAS = 4, 1
        block = ctx.enter_context(nc.Block())

        def steps(eng, step):
            for k in range(RING):
                step(0, k)
            with eng.Fori(1, UNITS // RING - 1) as j:
                for k in range(RING):
                    step(j, k)
            for k in range(RING):
                step(UNITS // RING - 1, k)
            for k in range(2):
                step(UNITS // RING, k)

        def has_unit(j, k, ahead):
            return not isinstance(j, int) or 0 <= j * RING + k + ahead < UNITS

        @block.sync
        def _(sp):
            sp.dma_start(wo[:, :], w["woT"]).then_inc(w_in, 16)

            def load(j, k):
                b, p0 = j * 2 + k // 2, UP * (k % 2)
                rows = m.q_dram[bass.ds(b, 1), :, :, :, p0:p0 + UP, :].rearrange("o r d x p t -> (o r d x) p t")
                sp.dma_start(qst[0:ROWS, k, :, :], rows).then_inc(stack_in[k], 16)
                for x in range(2):
                    rows = m.k_dram[bass.ds(b, 1), :, :, x, p0:p0 + UP, :].rearrange("o r d p t -> (o r d) p t")
                    sp.dma_start(kst[x:ROWS:2, k, x, :, :], rows).then_inc(stack_in[k], 16)
                h0 = (H // 2) * (k % 2)
                v = m.v_dram[bass.ds(b, 1), :, :, h0 * VW:(h0 + H // 2) * VW].rearrange("o p t c -> (o p) t c")
                sp.dma_start(vst[:, k, :, :, :].rearrange("p t h c -> p t (h c)"), v).then_inc(stack_in[k], 16)

            def bring_max(j, k):
                u = j * RING + k
                sp.wait_ge(mrow_ready, u + 1)
                sp.dma_start(qst[ROWS:ROWS + 4, k, :, :].rearrange("c p t -> c (p t)"), mrow[:, k % 2, :])\
                    .then_inc(mrow_in[k], 16)

            for k in range(3):
                load(0, k)
            bring_max(0, 0)

            def step(j, k):
                s = j * RING + k
                if has_unit(j, k, 3):
                    if past(s):
                        sp.wait_ge(pv_done, s * 2)
                    load(j + (k + 3) // RING, (k + 3) % RING)
                if has_unit(j, k, 1):
                    bring_max(j + (k + 1) // RING, (k + 1) % RING)
            steps(sp, step)

        def pass1_columns(t):
            return P if causal and t == 0 else T

        @block.tensor
        def _(pe):
            def scores1(j, k, p, tiles=range(TT)):
                u = j * RING + k
                if p == 0 and 0 in tiles:
                    pe.wait_ge(stack_in[k], (j + 1) * (STACK_DMAS * 16))
                for t in tiles:
                    c = pass1_columns(t)
                    n = (u * UP + p) * TT + t
                    if past(n - 1):
                        pe.wait_ge(s_read, n - 1)
                    q = qst[0:ROWS, k, p, t * P:(t + 1) * P]
                    out = ps_s[t][:, :].rearrange("p (x c) -> p x c", x=2)[:, :, 0:c]
                    i = nc.tensor.matmul(out, q, kst[0:ROWS, k, :, p, 0:c], start=True, stop=not causal)
                    if causal:
                        i = nc.tensor.matmul(out[:, :, c - P:c], m.ident16[:, :], m.mask_qk[:, :, :],
                                             start=False, stop=True)
                    i.then_inc(s_ready, 1)

            def turn_max(j, k):
                u = j * RING + k
                pe.wait_ge(msplit, u + 1)
                if past(u - 1):
                    pe.wait_ge(u_out, (u - 1) * 2)
                if not past(u - 1) and past(u):
                    pe.wait_ge(mrow_ready, 1)
                for t in range(TT):
                    i = nc.tensor.matmul(ps_u[0:4 * UP, T + t * P:T + (t + 1) * P],
                                         msp[:, k % 2, t, :, :, :].rearrange("p x r q -> p (x r q)"),
                                         m.ident16[:, :], start=True, stop=True)
                i.then_inc(mturned, 1)

            def scores2(j, k, p, x):
                u = j * RING + k
                if p == 0 and x == 0:
                    pe.wait_ge(mrow_in[k], (j + 1) * (MROW_DMAS * 16))
                n = u * UP + p
                if x == 0 and past(n - 1):
                    pe.wait_ge(exp_done, n - 1)
                for kt in range(TT):
                    q0 = P if causal and kt else 0
                    c0 = T * kt
                    key = kst[0:ROWS + 4, k, x, p, kt * P:(kt + 1) * P]
                    out = ps_st[p % 2][:, x, c0:c0 + T - q0]
                    i = nc.tensor.matmul(out, key, qst[0:ROWS + 4, k, p, q0:T], start=True, stop=not causal)
                    if causal:
                        i = nc.tensor.matmul(out[:, 0:P], m.ident16[:, :], m.mask_kq[:, :], start=False, stop=True)
                if x == 1:
                    i.then_inc(st_ready, 1)

            def values(j, k, qd):
                u = j * RING + k
                n = u * 2 + qd
                pe.wait_ge(exp_done, u * UP + 2 * qd + 2)
                if past(n):
                    pe.wait_ge(u_out, n)
                if qd == 0 and has_unit(j, k, 1):
                    pe.wait_ge(mrow_ready, u + 2)
                for kt in range(TT):
                    q0 = P if causal and kt else 0
                    for g in range(QUAD):
                        h = QUAD * qd + g
                        i = nc.tensor.matmul(ps_u[32 * g:32 * g + VW, q0:T], vst[:, k, kt, h, :],
                                             prob[:, h // 2, h % 2, T * kt:T * kt + T - q0],
                                             start=kt == 0, stop=kt == TT - 1, tile_position=(0, 32 * g))
                i.then_inc(pv_done, 1)

            def turn_values(j, k):
                pe.wait_ge(u_out, (j * RING + k) * 2 + 2)
                for t in range(TT):
                    for qd in range(2):
                        c = (t * 2 + qd) * P
                        i = nc.tensor.transpose(ps_m[:, c:c + P], usb[:, qd, t * P:(t + 1) * P], m.ident[:, :])
                i.then_inc(t_ready, 1)

            pe.wait_ge(cleared, 1)
            for p in range(UP):
                scores1(0, 0, p)
            for p in range(UP):
                scores1(0, 1, p)
            turn_max(0, 0)
            pe.wait_ge(w_in, 16)

            def step(j, k):
                s = j * RING + k
                jj, kk = (j, k - 1) if k else (j - 1, RING - 1)
                behind = past(s) and has_unit(j, k, -1)
                for p in range(UP):
                    for i in range(2):
                        if has_unit(j, k, 2):
                            scores1(j + (k + 2) // RING, (k + 2) % RING, p, [i])
                        if has_unit(j, k, 0):
                            scores2(j, k, p, i)
                    if p == 0 and behind:
                        values(jj, kk, 1)
                    if p == 1 and has_unit(j, k, 1):
                        turn_max(j + (k + 1) // RING, (k + 1) % RING)
                    if p == 1 and behind:
                        if k % 2 == 1 and past(s - 1):
                            pe.wait_ge(ot_out, j * 2 + (k - 1) // 2)
                        elif k % 2 == 0 and past(s - 2):
                            pe.wait_ge(added, j * 2 + (k - 2) // 2)
                        elif past(s - 1):
                            pe.wait_ge(t_read, 1)
                        turn_values(jj, kk)
                    if p == 2 and has_unit(j, k, 0):
                        values(j, k, 0)
                    if p == 3 and k % 2 == 0 and past(s):
                        pe.wait_ge(t_read, s)
                        for t in range(TT):
                            i = nc.tensor.transpose(ps_m[:, t * P:(t + 1) * P], o[:, t, :], m.ident[:, :])
                        i.then_inc(ot_ready, 1)
                    if p == 3 and k % 2 == 1 and past(s - 1):
                        if behind:
                            pe.wait_ge(t_read, s)
                        pe.wait_ge(ot_out, j * 2 + (k - 1) // 2)
                        for t in range(TT):
                            i = nc.tensor.matmul(ps_m[:, t * P:(t + 1) * P], oT[:, t * P:(t + 1) * P], wo[:, :],
                                                 start=True, stop=True)
                        i.then_inc(proj_ready, 1)
            steps(pe, step)

        @block.vector
        def _(dve):
            nc.vector.memset(ps_u[:, :], 0.0).then_inc(cleared, 1)

            def maxima(j, k, p, tiles=range(TT)):
                u = j * RING + k
                for t in tiles:
                    c = pass1_columns(t)
                    dve.wait_ge(s_ready, (u * UP + p) * TT + t + 1)
                    if p == 0 and t == 0 and past(u - 1):
                        dve.wait_ge(msplit, u - 1)
                    nc.vector.tensor_reduce(neg[:, k % 2, t, :, p],
                                            ps_s[t][:, :].rearrange("p (x c) -> p x c", x=2)[:, :, 0:c],
                                            AX.X, ALU.max, negate=True).then_inc(s_read, 1)

            def split_max(j, k, part):
                u = j * RING + k
                n_ = neg[:, k % 2, :, :, :].rearrange("p t x q -> p (t x) q")
                hi, mid = (msp[:, k % 2, :, :, r, :].rearrange("p t x q -> p (t x) q") for r in range(2))
                if part == 0:
                    dve.wait_ge(s_read, (u + 1) * (UP * TT))
                    if past(u - 1):
                        dve.wait_ge(mturned, u - 1)
                    nc.vector.tensor_copy(hi, n_).then_inc(halved, 1)
                else:
                    dve.wait_ge(halved, u + 1)
                    nc.vector.tensor_tensor(mid, n_, hi, ALU.subtract).then_inc(msplit, 1)

            def normalize(j, k, part):
                u = j * RING + k
                h0 = (H // 2) * (k % 2)
                tv = ps_m[:, :].rearrange("p (g c) -> p g c", c=32)
                if part == 0:
                    dve.wait_ge(t_ready, u + 1)
                    if past(u):
                        dve.wait_ge(t_read, u)
                    nc.vector.reciprocal(rec[:, :], tv[:, :, HD]).then_inc(inverted, 1)
                else:
                    dve.wait_ge(inverted, u + 1)
                    nc.vector.tensor_tensor(o[:, :, h0 * HD:(h0 + H // 2) * HD].rearrange("p t (g c) -> p t g c", c=HD),
                                            tv[:, :, 0:HD].rearrange("p (t g) c -> p t g c", t=TT),
                                            rec[:, :].rearrange("p (t g) -> p t g", t=TT).unsqueeze(3)
                                            .broadcast_to([P, TT, H // 2, HD]), ALU.mult).then_inc(t_read, 1)

            for k in range(2):
                for p in range(UP):
                    for t in range(TT):
                        maxima(0, k, p, [t])
                        if k == 1 and p == 0:
                            split_max(0, 0, t)

            def add_output(before, n0):
                dve.wait_ge(proj_ready, before + 1)
                x = resid[:, bass.ds(n0, TT), :]
                nc.vector.tensor_tensor(x, x, ps_m[:, 0:TT * D].rearrange("p (t c) -> p t c", t=TT),
                                        ALU.add).then_inc(added, 1)

            def step(j, k):
                s = j * RING + k
                jj, kk = (j, k - 1) if k else (j - 1, RING - 1)
                behind = past(s) and has_unit(j, k, -1)
                for p in range(UP):
                    for t in range(TT):
                        if has_unit(j, k, 2):
                            maxima(j + (k + 2) // RING, (k + 2) % RING, p, [t])
                        if p == 0 and has_unit(j, k, 1):
                            split_max(j + (k + 1) // RING, (k + 1) % RING, t)
                        if p == 1 and t == 0 and k % 2 == 0 and past(s - 2):
                            add_output(j * 2 + (k - 4) // 2, (j * 2 + (k - 4) // 2) * TT)
                        if p == 2 and behind:
                            normalize(jj, kk, t)
            steps(dve, step)
            add_output(B - 1, (B - 1) * TT)

        @block.scalar
        def _(act):
            def rows(j, k):
                u = j * RING + k
                act.wait_ge(mturned, u + 1)
                if past(u - 1):
                    act.wait_ge(mrow_in[(k - 2) % RING], (j + 1 - (k < 2)) * (MROW_DMAS * 16))
                nc.scalar.activation(mrow[:, k % 2, :], ps_u[0:4 * UP, T:2 * T], ACT.Copy).then_inc(mrow_ready, 1)

            def exps(j, k, p):
                n = (j * RING + k) * UP + p
                act.wait_ge(st_ready, n + 1)
                if p % 2 == 0 and past(n - UP + 1):
                    act.wait_ge(pv_done, (j * RING + k) * 2 + p // 2 - 1)
                nc.scalar.activation(prob[:, p, :, :], ps_st[p % 2][:, :, 0:SW], ACT.Exp, scale=SCALE)\
                    .then_inc(exp_done, 1)

            def keep_values(j, k, qd):
                n = (j * RING + k) * 2 + qd
                act.wait_ge(pv_done, n + 1)
                if past(j * RING + k):
                    act.wait_ge(t_ready, j * RING + k)
                nc.scalar.activation(usb[:, qd, :], ps_u[:, 0:T], ACT.Copy).then_inc(u_out, 1)

            rows(0, 0)

            def step(j, k):
                s = j * RING + k
                jj, kk = (j, k - 1) if k else (j - 1, RING - 1)
                if has_unit(j, k, 0):
                    exps(j, k, 0)
                if past(s) and has_unit(j, k, -1):
                    keep_values(jj, kk, 1)
                if has_unit(j, k, 0):
                    exps(j, k, 1)
                if has_unit(j, k, 1):
                    rows(j + (k + 1) // RING, (k + 1) % RING)
                if has_unit(j, k, 0):
                    exps(j, k, 2)
                    keep_values(j, k, 0)
                    exps(j, k, 3)
                if k % 2 == 0 and past(s):
                    act.wait_ge(ot_ready, j * 2 + k // 2)
                    nc.scalar.activation(oT[:, :], ps_m[:, 0:T], ACT.Copy).then_inc(ot_out, 1)
            steps(act, step)


def experts0(nc, m, w):
    G = 4
    N = G * P
    C = F0 // P
    GROUPS = NT // G
    with ExitStack() as ctx:
        sb = lambda n, s, d=f32: ctx.enter_context(nc.sbuf_tensor(f"e0_{n}", s, d))
        ps = lambda n, s, d=f32: ctx.enter_context(nc.psum_tensor(f"e0_{n}", s, d))
        new_sem = ctx.enter_context(semaphores(nc))
        sem = lambda n: new_sem(f"e0_{n}")
        w1, w2 = sb("w1", [P, E0, F0]), sb("w2", [P, E0, C, D])
        b1, b2 = sb("b1", [P, E0, C]), sb("b2", [P, E0])
        gw, gb, n2 = sb("gw", [P, E0]), sb("gb", [P, E0]), sb("n2", [P, 1])
        xn = sb("xn", [P, 2, G, D])
        xT = sb("xT", [P, 2, N])
        hid = sb("hid", [P, 4, N])
        yT = sb("yT", [P, 2, N])
        acc = sb("acc", [P, 2, G, D])
        lg, eq, one = sb("lg", [P, G, E0]), sb("eq", [P, G, E0]), sb("one", [P, 2, G, E0])
        top = sb("top", [P, G])
        turn, psl, pst = ps("turn", [P, 512]), ps("psl", [P, 512]), ps("pst", [P, 512])
        psh = [ps(f"h{i}", [P, 512]) for i in range(2)]
        psy = [ps(f"y{i}", [P, 512]) for i in range(2)]
        w_in, normed, turned, x_ready = sem("w_in"), sem("normed"), sem("turned"), sem("x_ready")
        lg_ready, order, chosen = sem("lg_ready"), sem("order"), sem("chosen")
        h_ready, h_act, h_dve = sem("h_ready"), sem("h_act"), sem("h_dve")
        y_done, y_out, t_ready, summed = (sem(x) for x in ("y_done", "y_out", "t_ready", "summed"))
        joined = sem("joined")
        block = ctx.enter_context(nc.Block())
        loads = [(w1, w["w1"]), (w2, w["w2"]), (b1, w["b1"]), (b2, w["b2"]), (gw, w["gw"]), (n2, w["n2"])]
        EC = E0 * C

        def groups(eng, step):
            for u in range(2):
                step(0, u)
            with eng.Fori(1, GROUPS // 2 - 1) as j:
                for u in range(2):
                    step(j, u)
            for u in range(2):
                step(GROUPS // 2 - 1, u)

        def last(j, u):
            return isinstance(j, int) and j * 2 + u == GROUPS - 1

        @block.sync
        def _(sp):
            for dst, s in loads:
                sp.dma_start(dst[:], s).then_inc(w_in, 16)
            sp.dma_start(gb[:, :], w["gb"].partition_broadcast(P)).then_inc(w_in, 16)

        @block.gpsimd
        def _(pool):
            def step(j, u):
                g = j * 2 + u
                pool.wait_ge(summed, g * E0 + E0)
                x = m.x[:, bass.ds(j * (2 * G) + u * G, G), :]
                nc.gpsimd.tensor_tensor(x, x, acc[:, u, :, :], ALU.add).then_inc(joined, 1)
            groups(pool, step)

        @block.vector
        def _(dve):
            def normalize(j, u):
                g = j * 2 + u
                if past(g - 1):
                    dve.wait_ge(turned, g - 1)
                for t in range(G):
                    n = j * (2 * G) + (u * G + t)
                    i = nc.vector.tensor_scalar(xn[:, u, t, :], m.y[:, bass.ds(n, 1), :].rearrange("p o d -> p (o d)"),
                                                m.y_rms[:, bass.ds(n, 1)], None, ALU.mult)
                i.then_inc(normed, 1)

            def choose(j, u):
                g = j * 2 + u
                o = Order(5, g)
                lgp = psl[:, 0:G * E0].rearrange("p (t e) -> p t e", e=E0)
                dve.wait_ge(lg_ready, g + 1)
                nc.vector.tensor_tensor(lg[:, :, :], lgp, gb[:, :].unsqueeze(1).broadcast_to([P, G, E0]),
                                        ALU.add).then_inc(order, 1)
                dve.wait_ge(order, o.next())
                nc.vector.tensor_reduce(top[:, :], lg[:, :, :], AX.X, ALU.max).then_inc(order, 1)
                dve.wait_ge(order, o.next())
                nc.vector.tensor_tensor(eq[:, :, :], lg[:, :, :], top[:, :].unsqueeze(2).broadcast_to([P, G, E0]),
                                        ALU.is_equal).then_inc(order, 1)
                dve.wait_ge(order, o.next())
                nc.vector.tensor_tensor(eq[:, :, :], eq[:, :, :], m.prior[:, 0:E0].unsqueeze(1)
                                        .broadcast_to([P, G, E0]), ALU.mult).then_inc(order, 1)
                dve.wait_ge(order, o.next())
                nc.vector.tensor_reduce(top[:, :], eq[:, :, :], AX.X, ALU.max).then_inc(order, 1)
                dve.wait_ge(order, o.next())
                nc.vector.tensor_tensor(one[:, u, :, :], eq[:, :, :], top[:, :].unsqueeze(2)
                                        .broadcast_to([P, G, E0]), ALU.is_equal).then_inc(chosen, 1)

            dve.wait_ge(w_in, 16 * (len(loads) + 1))
            normalize(0, 0)
            choose(0, 0)

            def add_expert(j, u, e):
                g = j * 2 + u
                dve.wait_ge(t_ready, g * E0 + e + 1)
                dve.wait_ge(chosen, g + 1)
                if e:
                    dve.wait_ge(summed, g * E0 + e)
                elif past(g - 1):
                    dve.wait_ge(joined, g - 1)
                for t in range(G):
                    n = j * (2 * G) + (u * G + t)
                    base = acc[:, u, t, :] if e else m.y[:, bass.ds(n, 1), :].rearrange("p o d -> p (o d)")
                    i = nc.vector.scalar_tensor_tensor(out=acc[:, u, t, :], in0=pst[:, t * P:(t + 1) * P],
                                                       scalar=one[:, u, t, e:e + 1], in1=base,
                                                       op0=ALU.mult, op1=ALU.add)
                i.then_inc(summed, 1)

            def step(j, u):
                g = j * 2 + u
                for q in range(EC + 4):
                    if q < EC and q % 2:
                        dve.wait_ge(h_ready, g * EC + q + 1)
                        if past(g * EC + q - 3):
                            dve.wait_ge(y_done, g * EC + q - 3)
                        nc.vector.tensor_scalar(hid[:, q % 4, :], psh[q % 2][:, :], b1[:, q // C, q % C:q % C + 1], 0.0,
                                                ALU.add, ALU.max).then_inc(h_dve, 1)
                    if q == 8 and not last(j, u):
                        normalize(j + u, 1 - u)
                    if q == 12 and not last(j, u):
                        choose(j + u, 1 - u)
                    if q >= 7 and q % 4 == 3:
                        add_expert(j, u, (q - 7) // 4)
            groups(dve, step)

        @block.scalar
        def _(act):
            act.wait_ge(w_in, 16 * (len(loads) + 1))

            def take(j, u):
                g = j * 2 + u
                act.wait_ge(turned, g + 1)
                if past(g - 1):
                    act.wait_ge(h_ready, (g - 1) * EC)
                    act.wait_ge(lg_ready, g - 1)
                nc.scalar.activation(xT[:, u, :], turn[:, :], ACT.Copy, scale=n2[:, :]).then_inc(x_ready, 1)

            take(0, 0)

            def step(j, u):
                g = j * 2 + u
                for q in range(EC + 4):
                    if q < EC and q % 2 == 0:
                        act.wait_ge(h_ready, g * EC + q + 1)
                        if past(g * EC + q - 3):
                            act.wait_ge(y_done, g * EC + q - 3)
                        nc.scalar.activation(hid[:, q % 4, :], psh[q % 2][:, :], ACT.Relu,
                                             bias=b1[:, q // C, q % C:q % C + 1]).then_inc(h_act, 1)
                    if q == 9 and not last(j, u):
                        take(j + u, 1 - u)
                    if q >= 6 and q % 4 == 2:
                        e = (q - 6) // 4
                        act.wait_ge(y_done, g * EC + e * C + C)
                        if past(g * E0 + e - 1):
                            act.wait_ge(t_ready, g * E0 + e - 1)
                        nc.scalar.activation(yT[:, e % 2, :], psy[e % 2][:, :], ACT.Identity,
                                             bias=b2[:, e:e + 1]).then_inc(y_out, 1)
            groups(act, step)

        @block.tensor
        def _(pe):
            pe.wait_ge(w_in, 16 * (len(loads) + 1))

            def turns(j, u):
                g = j * 2 + u
                pe.wait_ge(normed, g + 1)
                if past(g):
                    pe.wait_ge(x_ready, g)
                for t in range(G):
                    i = nc.tensor.transpose(turn[:, t * P:(t + 1) * P], xn[:, u, t, :], m.ident[:, :])
                i.then_inc(turned, 1)

            def logits(j, u):
                g = j * 2 + u
                pe.wait_ge(x_ready, g + 1)
                if past(g):
                    pe.wait_ge(chosen, g)
                for t in range(G):
                    i = nc.tensor.matmul(psl[:, t * E0:(t + 1) * E0], xT[:, u, t * P:(t + 1) * P], gw[:, :],
                                         start=True, stop=True)
                i.then_inc(lg_ready, 1)

            turns(0, 0)
            logits(0, 0)

            def step(j, u):
                g = j * 2 + u
                for q in range(EC + 4):
                    if q < EC:
                        n = g * EC + q
                        if past(n - 1):
                            half = g * (EC // 2) + (q // 2)
                            pe.wait_ge(h_dve if q % 2 else h_act, half)
                        nc.tensor.matmul(psh[q % 2][:, :], w1[:, q // C, (q % C) * P:(q % C + 1) * P], xT[:, u, :],
                                         start=True, stop=True).then_inc(h_ready, 1)
                    r = q - 2
                    if 0 <= r < EC:
                        e, c = r // C, r % C
                        pe.wait_ge(h_dve if r % 2 else h_act, g * (EC // 2) + r // 2 + 1)
                        if c == 0 and past(g * E0 + e - 1):
                            pe.wait_ge(y_out, g * E0 + e - 1)
                        nc.tensor.matmul(psy[e % 2][:, :], w2[:, e, c, :], hid[:, r % 4, :],
                                         start=c == 0, stop=c == C - 1).then_inc(y_done, 1)
                    if q == 8 and not last(j, u):
                        turns(j + u, 1 - u)
                    if q == 11 and not last(j, u):
                        logits(j + u, 1 - u)
                    if q >= 7 and q % 4 == 3:
                        e = (q - 7) // 4
                        pe.wait_ge(y_out, g * E0 + e + 1)
                        if past(g * E0 + e):
                            pe.wait_ge(summed, g * E0 + e)
                        for t in range(G):
                            i = nc.tensor.transpose(pst[:, t * P:(t + 1) * P], yT[:, e % 2, t * P:(t + 1) * P],
                                                    m.ident[:, :])
                        i.then_inc(t_ready, 1)
            groups(pe, step)


def route1(nc, m, w):
    with ExitStack() as ctx:
        sb = lambda n, s, d=f32: ctx.enter_context(nc.sbuf_tensor(f"r1_{n}", s, d))
        ps = lambda n, s, d=f32: ctx.enter_context(nc.psum_tensor(f"r1_{n}", s, d))
        new_sem = ctx.enter_context(semaphores(nc))
        sem = lambda n: new_sem(f"r1_{n}")
        G, GROUPS = 4, NT // 4
        gw = sb("gw", [P, E1])
        xn = sb("xn", [P, 2, G, D])
        xT = sb("xT", [P, 2, G * P])
        lg, ex, one = sb("lg", [P, NT, E1]), sb("ex", [P, NT, E1]), sb("one", [P, NT, E1])
        one16 = sb("one16", [P, NT, E1], bf16)
        tot, inc = sb("tot", [P, NT, E1]), sb("inc", [P, E1, NT])
        mx, sm, esel = sb("mx", [P, NT]), sb("sm", [P, NT]), sb("esel", [P, NT])
        rank, keep, slot = sb("rank", [P, NT]), sb("keep", [P, NT]), sb("slot", [P, NT])
        onesf = sb("onesf", [P, NT])
        turn = [ps(f"turn{i}", [P, 512]) for i in range(2)]
        psl = [ps(f"l{i}", [P, 512]) for i in range(2)]
        ps_pre, ps_tot = ps("ps_pre", [P, 512]), ps("ps_tot", [P, 512])
        w_in, normed, turned, x_ready, lg_ready, lg_kept = (sem(x) for x in ("w_in", "normed", "turned", "x_ready",
                                                                            "lg_ready", "lg_kept"))
        order, less, exped, counted, one_ready = (sem(x) for x in ("order", "less", "exped", "counted", "one_ready"))
        block = ctx.enter_context(nc.Block())

        def groups(eng, step):
            for u in range(2):
                step(0, u)
            with eng.Fori(1, GROUPS // 2) as j:
                for u in range(2):
                    step(j, u)

        @block.sync
        def _(sp):
            sp.dma_start(gw[:, :], w["gw"]).then_inc(w_in, 16)

        @block.scalar
        def _(act):
            def step(j, u):
                g = j * 2 + u
                act.wait_ge(turned, g + 1)
                if past(g - 1):
                    act.wait_ge(lg_ready, g - 1)
                nc.scalar.activation(xT[:, u, :], turn[u][:, :], ACT.Copy).then_inc(x_ready, 1)
            groups(act, step)
            act.wait_ge(less, 1)
            nc.scalar.activation(ex[:, :, :], lg[:, :, :], ACT.Exp).then_inc(exped, 1)

        @block.tensor
        def _(pe):
            pe.wait_ge(w_in, 16)

            def step(j, u):
                g = j * 2 + u
                pe.wait_ge(normed, g + 1)
                if past(g - 1):
                    pe.wait_ge(x_ready, g - 1)
                for t in range(G):
                    i = nc.tensor.transpose(turn[u][:, t * P:(t + 1) * P], xn[:, u, t, :], m.ident[:, :])
                i.then_inc(turned, 1)
                pe.wait_ge(x_ready, g + 1)
                if past(g - 1):
                    pe.wait_ge(lg_kept, g - 1)
                for t in range(G):
                    i = nc.tensor.matmul(psl[u][:, t * E1:(t + 1) * E1], xT[:, u, t * P:(t + 1) * P], gw[:, :],
                                         start=True, stop=True)
                i.then_inc(lg_ready, 1)
            groups(pe, step)
            pe.wait_ge(one_ready, 1)
            rhs = one16[:, :, :].rearrange("p n e -> p (n e)")
            nc.tensor.matmul(ps_pre[:, :], m.before[:, :], rhs, start=True, stop=True)
            nc.tensor.matmul(ps_tot[:, :], m.ones16[:, :], rhs, start=True, stop=True).then_inc(counted, 1)

        @block.vector
        def _(dve):
            def step(j, u):
                g = j * 2 + u
                if past(g - 1):
                    dve.wait_ge(turned, g - 1)
                for t in range(G):
                    n = j * (2 * G) + (u * G + t)
                    row = m.x[:, bass.ds(n, 1), :].rearrange("p o d -> p (o d)")
                    mean, inv = m.x_stat[:, bass.ds(n, 1), 0], m.x_rstd[:, bass.ds(n, 1)]
                    nc.vector.tensor_scalar(m.y[:, bass.ds(n, 1), :].rearrange("p o d -> p (o d)"), row, mean, inv,
                                            ALU.subtract, ALU.mult)
                    i = nc.vector.tensor_scalar(xn[:, u, t, :], row, mean, inv, ALU.subtract, ALU.mult)
                i.then_inc(normed, 1)
                dve.wait_ge(lg_ready, g + 1)
                nc.vector.tensor_copy(lg[:, bass.ds(j * (2 * G) + u * G, G), :],
                                      psl[u][:, 0:G * E1].rearrange("p (t e) -> p t e", e=E1)).then_inc(lg_kept, 1)

            nc.vector.memset(onesf[:, :], 1.0).then_inc(order, 1)
            groups(dve, step)
            dve.wait_ge(lg_kept, GROUPS)
            o = Order(40, 0)
            o.next()

            def wide(a):
                return a[:, :].unsqueeze(2).broadcast_to([P, NT, E1])

            def flat(a):
                return a[:, :].unsqueeze(1).broadcast_to([P, NT, E1])

            nc.vector.tensor_reduce(mx[:, :], lg[:, :, :], AX.X, ALU.max).then_inc(order, 1)
            dve.wait_ge(order, o.next())
            nc.vector.tensor_tensor(lg[:, :, :], lg[:, :, :], wide(mx), ALU.subtract).then_inc(less, 1)
            dve.wait_ge(exped, 1)
            nc.vector.tensor_reduce(sm[:, :], ex[:, :, :], AX.X, ALU.add).then_inc(order, 1)
            dve.wait_ge(order, o.next())
            nc.vector.reciprocal(sm[:, :], sm[:, :]).then_inc(order, 1)
            dve.wait_ge(order, o.next())
            nc.vector.tensor_reduce(mx[:, :], ex[:, :, :], AX.X, ALU.max).then_inc(order, 1)
            dve.wait_ge(order, o.next())
            nc.vector.tensor_tensor(m.gate[:, :], mx[:, :], sm[:, :], ALU.mult).then_inc(order, 1)
            dve.wait_ge(order, o.next())
            nc.vector.tensor_tensor(one[:, :, :], ex[:, :, :], wide(mx), ALU.is_equal).then_inc(order, 1)
            dve.wait_ge(order, o.next())
            nc.vector.tensor_tensor(one[:, :, :], one[:, :, :], flat(m.prior), ALU.mult).then_inc(order, 1)
            dve.wait_ge(order, o.next())
            nc.vector.tensor_reduce(mx[:, :], one[:, :, :], AX.X, ALU.max).then_inc(order, 1)
            dve.wait_ge(order, o.next())
            nc.vector.tensor_tensor(one[:, :, :], one[:, :, :], wide(mx), ALU.is_equal).then_inc(order, 1)
            dve.wait_ge(order, o.next())
            nc.vector.tensor_copy(one16[:, :, :], one[:, :, :]).then_inc(one_ready, 1)
            dve.wait_ge(counted, 1)
            nc.vector.tensor_copy(tot[:, :, :].rearrange("p n e -> p (n e)"), ps_tot[:, :]).then_inc(order, 1)
            dve.wait_ge(order, o.next())
            for e in range(E1):
                i = nc.vector.tensor_tensor_scan(inc[:, e, :], onesf[:, :], tot[:, :, e], 0.0, ALU.mult, ALU.add)
            i.then_inc(order, 1)
            dve.wait_ge(order, o.next())
            by_tile = inc[:, :, :].rearrange("p e n -> p n e")
            nc.vector.tensor_tensor(tot[:, :, :], by_tile, tot[:, :, :], ALU.subtract).then_inc(order, 1)
            dve.wait_ge(order, o.next())
            nc.vector.tensor_tensor(tot[:, :, :], tot[:, :, :], ps_pre[:, :].rearrange("p (n e) -> p n e", e=E1),
                                    ALU.add).then_inc(order, 1)
            dve.wait_ge(order, o.next())
            nc.vector.tensor_tensor(tot[:, :, :], tot[:, :, :], one[:, :, :], ALU.mult).then_inc(order, 1)
            dve.wait_ge(order, o.next())
            nc.vector.tensor_reduce(rank[:, :], tot[:, :, :], AX.X, ALU.add).then_inc(order, 1)
            dve.wait_ge(order, o.next())
            nc.vector.tensor_tensor(tot[:, :, :], one[:, :, :], flat(m.prior), ALU.mult).then_inc(order, 1)
            dve.wait_ge(order, o.next())
            nc.vector.tensor_reduce(esel[:, :], tot[:, :, :], AX.X, ALU.add).then_inc(order, 1)
            dve.wait_ge(order, o.next())
            nc.vector.tensor_scalar(esel[:, :], esel[:, :], float(-CAP), float(E1 * CAP), ALU.mult, ALU.add)\
                .then_inc(order, 1)
            dve.wait_ge(order, o.next())
            nc.vector.tensor_tensor(slot[:, :], esel[:, :], rank[:, :], ALU.add).then_inc(order, 1)
            dve.wait_ge(order, o.next())
            nc.vector.tensor_scalar(keep[:, :], rank[:, :], float(CAP), None, ALU.is_lt).then_inc(order, 1)
            dve.wait_ge(order, o.next())
            nc.vector.tensor_tensor(m.gate[:, :], m.gate[:, :], keep[:, :], ALU.mult).then_inc(order, 1)
            nc.vector.tensor_scalar(rank[:, :], keep[:, :], -1.0e6, 1.0e6, ALU.mult, ALU.add).then_inc(order, 1)
            o.next()
            dve.wait_ge(order, o.next())
            nc.vector.tensor_tensor(rank[:, :], rank[:, :], slot[:, :], ALU.add).then_inc(order, 1)
            nc.vector.tensor_tensor(slot[:, :], keep[:, :], slot[:, :], ALU.mult).then_inc(order, 1)
            o.next()
            dve.wait_ge(order, o.next())
            nc.vector.tensor_copy(m.to_slot[:, :], rank[:, :])
            nc.vector.tensor_copy(m.from_slot[:, :], slot[:, :])


def experts1(nc, m, w, out):
    S = 2 * P
    BL = CAP // S
    C = F1 // P
    R = BL
    with ExitStack() as ctx:
        sb = lambda n, s, d=f32: ctx.enter_context(nc.sbuf_tensor(f"e1_{n}", s, d))
        ps = lambda n, s, d=f32: ctx.enter_context(nc.psum_tensor(f"e1_{n}", s, d))
        new_sem = ctx.enter_context(semaphores(nc))
        sem = lambda n: new_sem(f"e1_{n}")
        w1, w2 = sb("w1", [P, 2, F1]), sb("w2", [P, 2, C, D])
        b1, b2 = sb("b1", [P, 2, C]), sb("b2", [P, 2])
        tok = sb("tok", [P, R, 2, D])
        xT = sb("xT", [P, 2, S])
        hid = sb("hid", [P, 2, C, S])
        yT = sb("yT", [P, 2, S])
        res = sb("res", [P, R, 2, D])
        turn, psy, pst = ps("turn", [P, 512]), ps("y", [P, 512]), ps("t", [P, 512])
        psh = [ps(f"h{i}", [P, 512]) for i in range(4)]
        scattered = sem("scattered")
        w_in = [sem(f"w_in{u}") for u in range(2)]
        tok_in = [sem(f"tok_in{r}") for r in range(R)]
        turned, x_ready, h_ready, h_act, h_dve = (sem(x) for x in ("turned", "x_ready", "h_ready", "h_act", "h_dve"))
        y_ready, y_out, t_ready, res_ready = (sem(x) for x in ("y_ready", "y_out", "t_ready", "res_ready"))
        sent = [sem(f"sent{r}") for r in range(R)]
        stored_all = sem("stored_all")
        NG = 8
        fetched = [sem(f"fetched{n}") for n in range(NG)]
        summed, done = sem("summed"), sem("done")
        block = ctx.enter_context(nc.Block())
        slots = m.slots.rearrange("(b t p) d -> b p t d", t=2, p=P)
        outs = m.slot_out.rearrange("(b t p) d -> b p t d", t=2, p=P)

        def experts(eng, step):
            def both(j):
                for u in range(2):
                    for r in range(BL):
                        step(j, u, r)
            both(0)
            with eng.Fori(1, E1 // 2 - 1) as j:
                both(j)
            both(E1 // 2 - 1)

        def number(j, u, r):
            return j * (2 * BL) + (u * BL + r)

        def ahead(j, u, r):
            if r + 1 < BL:
                return j, u, r + 1
            return (j, 1, 0) if u == 0 else (j + 1, 0, 0)

        def last(j, u, r):
            return isinstance(j, int) and number(j, u, r) == E1 * BL - 1

        @block.gpsimd
        def _(pool):
            for n in range(NT):
                nc.gpsimd.indirect_dma_start(out=m.slots, out_offset=bass.IndirectOffsetOnAxis(
                    ap=m.to_slot[:, n:n + 1], axis=0), in_=m.y[:, n, :], in_offset=None,
                    bounds_check=SLOTS - 1, oob_is_err=False).then_inc(scattered, 16)
            pool.wait_ge(stored_all, 1)
            for n in range(NT):
                nc.gpsimd.indirect_dma_start(out=m.y[:, n, :], out_offset=None, in_=m.slot_out,
                                             in_offset=bass.IndirectOffsetOnAxis(ap=m.from_slot[:, n:n + 1], axis=0),
                                             bounds_check=SLOTS - 1, oob_is_err=False)\
                    .then_inc(fetched[n // (NT // NG)], 16)

        @block.sync
        def _(sp):
            def weights(j, u):
                e = j * 2 + u
                sp.dma_start(w1[:, u, :], w["w1"][bass.ds(e, 1), :, :].rearrange("o d h -> (o d) h")).then_inc(w_in[u], 16)
                sp.dma_start(w2[:, u, :, :], w["w2"][bass.ds(e, 1), :, :].rearrange("o (c p) d -> (o p) c d", p=P))\
                    .then_inc(w_in[u], 16)
                sp.dma_start(b1[:, u, :], w["b1"][bass.ds(e, 1), :, :].rearrange("o p c -> (o p) c")).then_inc(w_in[u], 16)
                sp.dma_start(b2[:, u:u + 1], w["b2"][bass.ds(e, 1), :, :].rearrange("o p c -> (o p) c"))\
                    .then_inc(w_in[u], 16)

            for u in range(2):
                weights(0, u)
            sp.wait_ge(scattered, 16 * NT)

            def fetch(j, u, r):
                i = number(j, u, r)
                if past(i - R + 1):
                    sp.wait_ge(turned, i - R + 1)
                sp.dma_start(tok[:, r, :, :], slots[bass.ds(i, 1), :, :, :].rearrange("o p t d -> (o p) t d"))\
                    .then_inc(tok_in[r], 16)

            for r in range(3):
                fetch(0, 0, r)

            def step(j, u, r):
                i = number(j, u, r)
                if not (isinstance(j, int) and i + 3 >= E1 * BL):
                    if r + 3 < BL:
                        fetch(j, u, r + 3)
                    else:
                        fetch(j + u, 1 - u, r + 3 - BL)
                if r == 1 and not (isinstance(j, int) and (j * 2 + u < 1 or j * 2 + u + 1 >= E1)):
                    sp.wait_ge(y_out, (j * 2 + u) * BL)
                    weights(j + u, 1 - u)
                sp.wait_ge(res_ready, i + 1)
                sp.dma_start(outs[bass.ds(i, 1), :, :, :].rearrange("o p t d -> (o p) t d"), res[:, r, :, :])\
                    .then_inc(sent[r], 16)
            experts(sp, step)
            for r in range(R):
                sp.wait_ge(sent[r], 16 * E1)
            sp.nop().then_inc(stored_all, 1)
            view = out.rearrange("b (t p) d -> p (b t) d", p=P)
            K = NT // NG
            for n in range(NG):
                sp.wait_ge(summed, (n + 1) * K)
                sp.dma_start(view[:, n * K:(n + 1) * K, :], m.x[:, n * K:(n + 1) * K, :]).then_inc(done, 16)
            sp.wait_ge(done, 16 * NG)

        @block.scalar
        def _(act):
            def take(j, u, r):
                i = number(j, u, r)
                act.wait_ge(turned, i + 1)
                if past(i - 1):
                    act.wait_ge(h_ready, (i - 1) * 2)
                nc.scalar.activation(xT[:, (u * BL + r) % 2, :], turn[:, 0:S], ACT.Copy).then_inc(x_ready, 1)

            take(0, 0, 0)

            def step(j, u, r):
                i = number(j, u, r)
                v = (u * BL + r) % 2
                if not last(j, u, r):
                    take(*ahead(j, u, r))
                if r == 0:
                    act.wait_ge(w_in[u], (j + 1) * 64)
                act.wait_ge(h_ready, i * 2 + 1)
                if past(i - 1):
                    act.wait_ge(y_ready, i - 1)
                for c in (0, 1):
                    k = nc.scalar.activation(hid[:, v, c, :], psh[2 * v][:, c * S:(c + 1) * S], ACT.Relu,
                                             bias=b1[:, u, c:c + 1])
                k.then_inc(h_act, 1)
                act.wait_ge(y_ready, i + 1)
                if past(i - 1):
                    act.wait_ge(t_ready, i - 1)
                nc.scalar.activation(yT[:, v, :], psy[:, 0:S], ACT.Identity, bias=b2[:, u:u + 1])\
                    .then_inc(y_out, 1)
            experts(act, step)

        @block.vector
        def _(dve):
            def give(j, u, r):
                i = number(j, u, r)
                dve.wait_ge(t_ready, i + 1)
                if not (isinstance(j, int) and j * 2 + u < 1):
                    dve.wait_ge(sent[r], (j * 2 + u) * 16)
                nc.vector.tensor_copy(res[:, r, :, :], pst[:, 0:S].rearrange("p (t d) -> p t d", t=2)).then_inc(res_ready, 1)

            def step(j, u, r):
                i = number(j, u, r)
                v = (u * BL + r) % 2
                if r == 0:
                    dve.wait_ge(w_in[u], (j + 1) * 64)
                dve.wait_ge(h_ready, i * 2 + 2)
                if past(i - 1):
                    dve.wait_ge(y_ready, i - 1)
                for c in (2, 3):
                    k = nc.vector.tensor_scalar(hid[:, v, c, :], psh[2 * v + 1][:, (c - 2) * S:(c - 1) * S],
                                                b1[:, u, c:c + 1], 0.0, ALU.add, ALU.max)
                k.then_inc(h_dve, 1)
                give(j, u, r)
            experts(dve, step)

            for n in range(NT):
                if n % (NT // NG) == 0:
                    dve.wait_ge(fetched[n // (NT // NG)], 16 * (NT // NG))
                nc.vector.scalar_tensor_tensor(out=m.x[:, n, :], in0=m.y[:, n, :], scalar=m.gate[:, n:n + 1],
                                               in1=m.x[:, n, :], op0=ALU.mult, op1=ALU.add).then_inc(summed, 1)

        @block.tensor
        def _(pe):
            def turns(j, u, r):
                i = number(j, u, r)
                pe.wait_ge(tok_in[r], (j * 2 + u + 1) * 16)
                if past(i):
                    pe.wait_ge(x_ready, i)
                for t in range(2):
                    k = nc.tensor.transpose(turn[:, t * P:(t + 1) * P], tok[:, r, t, :], m.ident[:, :])
                k.then_inc(turned, 1)

            turns(0, 0, 0)

            def step(j, u, r):
                i = number(j, u, r)
                v = (u * BL + r) % 2
                if r == 0:
                    pe.wait_ge(w_in[u], (j + 1) * 64)
                pe.wait_ge(x_ready, i + 1)
                for c in range(C):
                    if c % 2 == 0 and past(i - 1):
                        pe.wait_ge(h_dve if c else h_act, i - 1)
                    k = nc.tensor.matmul(psh[2 * v + c // 2][:, (c % 2) * S:(c % 2 + 1) * S],
                                         w1[:, u, c * P:(c + 1) * P], xT[:, v, :], start=True, stop=True)
                    if c % 2:
                        k.then_inc(h_ready, 1)
                if not last(j, u, r):
                    turns(*ahead(j, u, r))
                pe.wait_ge(h_act, i + 1)
                if past(i):
                    pe.wait_ge(y_out, i)
                for c in range(C):
                    if c == 2:
                        pe.wait_ge(h_dve, i + 1)
                    k = nc.tensor.matmul(psy[:, 0:S], w2[:, u, c, :], hid[:, v, c, :], start=c == 0, stop=c == C - 1)
                k.then_inc(y_ready, 1)
                pe.wait_ge(y_out, i + 1)
                if past(i):
                    pe.wait_ge(res_ready, i)
                for t in range(2):
                    k = nc.tensor.transpose(pst[:, t * P:(t + 1) * P], yT[:, v, t * P:(t + 1) * P], m.ident[:, :])
                k.then_inc(t_ready, 1)
            experts(pe, step)


class Kept:
    pass


def two_layers(nc, x, a, out):
    with ExitStack() as ctx:
        m = Kept()
        sb = lambda n, s, d=f32: ctx.enter_context(nc.sbuf_tensor(f"kept_{n}", s, d))
        dram = lambda n, s, d=f32: nc.dram_tensor(n, s, d, kind="Internal").ap()
        m.x, m.y = sb("x", [P, NT, D]), sb("y", [P, NT, D])
        m.lat = sb("lat", [P, NT, LAT])
        m.x_stat, m.x_rstd = sb("x_stat", [P, NT, 2]), sb("x_rstd", [P, NT])
        m.lat_stat, m.lat_rstd = sb("lat_stat", [P, NT, 2]), sb("lat_rstd", [P, NT])
        m.y_stat, m.y_rms = sb("y_stat", [P, NT, 2]), sb("y_rms", [P, NT])
        m.qst, m.kst = sb("qst", [P, 4, UP, T], bf16), sb("kst", [P, 4, 2, UP, T], bf16)
        m.ident, m.ident16 = sb("ident", [P, P]), sb("ident16", [P, P], bf16)
        m.mask_qk, m.mask_kq = sb("mask_qk", [P, 2, P], bf16), sb("mask_kq", [P, P], bf16)
        m.before, m.ones16 = sb("before", [P, P], bf16), sb("ones16", [P, P], bf16)
        m.zero = sb("zero", [P, 2 * UP * T], bf16)
        m.prior = sb("prior", [P, E1])
        m.proj_bias = sb("proj_bias", [P, D])
        m.out_bias = sb("out_bias", [P, D])
        m.gate = sb("gate", [P, NT])
        m.to_slot, m.from_slot = sb("to_slot", [P, NT], u32), sb("from_slot", [P, NT], u32)
        m.q_dram = dram("q_stacks", (B, 6, HD, 2, PAIRS, T), bf16)
        m.k_dram = dram("k_stacks", (B, 6, HD, 2, PAIRS, T), bf16)
        m.v_dram = dram("v_rows", (B, P, TT, H * VW))
        m.slots, m.slot_out = dram("slots", (SLOTS, D)), dram("slot_out", (SLOTS, D))
        m.serial = 0

        with ExitStack() as c:
            sem = c.enter_context(semaphores(nc))
            x_in, filled, made, zeroed, slots_zero = (sem(n) for n in ("x_in", "filled", "made", "zeroed", "slots_zero"))
            block = c.enter_context(nc.Block())

            @block.sync
            def _(sp):
                view = x.rearrange("b (t p) d -> p (b t) d", p=P)
                K = NT // 8
                for n in range(8):
                    sp.dma_start(m.x[:, n * K:(n + 1) * K, :], view[:, n * K:(n + 1) * K, :]).then_inc(x_in, 16)
                sp.dma_start(m.proj_bias[:, :], a["L1_attn_bproj"].partition_broadcast(P)).then_inc(x_in, 16)
                sp.dma_start(m.out_bias[:, :], a["L0_attn_out_b"].partition_broadcast(P)).then_inc(x_in, 16)
                sp.wait_ge(zeroed, 1)
                K = 2 * UP * T // 2 // D
                zero = m.zero[:, :].bitcast(f32)
                n_rows = P * K
                for n in range(SLOTS // n_rows):
                    sp.dma_start(m.slots[n * n_rows:(n + 1) * n_rows, :].rearrange("(p k) d -> p (k d)", k=K),
                                 zero).then_inc(slots_zero, 16)
                sp.wait_ge(x_in, 160)
                sp.wait_ge(slots_zero, 16 * (SLOTS // n_rows))

            @block.vector
            def _(dve):
                nc.vector.memset(m.zero[:, :], 0.0).then_inc(zeroed, 1)
                nc.vector.memset(m.ones16[:, :], 1.0)

            @block.gpsimd
            def _(pool):
                p = nc.gpsimd
                n = 0

                def fill(tile, value):
                    p.memset(tile, value).then_inc(filled, 1)

                kst = m.kst[:, :, :, :, :]
                fill(m.ident[:, :], 0.0)
                fill(m.ident16[:, :], 0.0)
                fill(m.mask_qk[:, :, :], 0.0)
                fill(m.mask_kq[:, :], 0.0)
                fill(m.before[:, :], 1.0)
                fill(kst, 0.0)
                for e in range(E1):
                    fill(m.prior[:, e:e + 1], float(E1 - e))
                pool.wait_ge(filled, 6 + E1)
                for t in (m.ident, m.ident16):
                    p.affine_select(out=t[:, :], in_=t[:, :], compare_op=ALU.not_equal, fill=1.0, base=0,
                                    pattern=[[-1, P]], channel_multiplier=1)
                p.affine_select(out=m.mask_qk[:, :, :], in_=m.mask_qk[:, :, :], compare_op=ALU.is_ge, fill=MASKED,
                                base=0, pattern=[[0, 2], [-1, P]], channel_multiplier=1)
                p.affine_select(out=m.mask_kq[:, :], in_=m.mask_kq[:, :], compare_op=ALU.is_ge, fill=MASKED,
                                base=0, pattern=[[1, P]], channel_multiplier=-1)
                p.affine_select(out=m.before[:, :], in_=m.before[:, :], compare_op=ALU.is_gt, fill=0.0,
                                base=0, pattern=[[1, P]], channel_multiplier=-1)
                for x_ in range(2):
                    for r in range(2):
                        part = m.kst[:, :, x_, :, :].rearrange("p k q t -> p k (q t)")
                        n += 1
                        p.affine_select(out=part, in_=part, compare_op=ALU.not_equal, fill=1.0,
                                        base=-(ROWS + 2 * x_ + r), pattern=[[0, 4], [0, UP * T]],
                                        channel_multiplier=1).then_inc(made, 1)
                        pool.wait_ge(made, n)

        layer_stats(nc, "first", m.x, m.x_stat, m.x_rstd, 1e-5)
        m.serial = 1
        project(nc, "plain", m, dict(watt=a["watt"], wvT=a["wvT"], bv=a["L0_attn_wv_b"]))
        attend(nc, "plain", m, dict(woT=a["outT"]))
        layer_stats(nc, "second", m.x, m.x_stat, m.x_rstd, 1e-5)
        project(nc, "queries", m, dict(cos=a["cos"], sin=a["sin"], wqT=a["wqT"], wqrT=a["wqrT"], wdT=a["wdkvT"],
                                       n1=a["n1"]))
        layer_stats(nc, "latent", m.lat, m.lat_stat, m.lat_rstd, 1e-5)
        project(nc, "keys", m, dict(cos=a["cos"], sin=a["sin"], wkT=a["wukT"], wkrT=a["wukrT"], wvT0=a["wuvT"],
                                    lg=a["ln_g"], lb=a["ln_b"]))
        m.serial = 2
        attend(nc, "causal", m, dict(woT=a["woT"]))
        layer_stats(nc, "third", m.y, m.y_stat, m.y_rms, 1e-6, second_moment=True)
        experts0(nc, m, dict(w1=a["w1T"], w2=a["w2T"], b1=a["b1T"], b2=a["b2T"], gw=a["gwT"], gb=a["L0_ffn_gate_b"],
                             n2=a["n2"]))
        layer_stats(nc, "fourth", m.x, m.x_stat, m.x_rstd, 1e-5)
        project(nc, "cosine", m, dict(wqkv=a["L1_attn_Wqkv"], qs=a["q_scale"], ks=a["k_scale"], same_head=a["same_head"]))
        m.serial = 3
        attend(nc, "plain", m, dict(woT=a["L1_attn_Wproj"]))
        layer_stats(nc, "fifth", m.x, m.x_stat, m.x_rstd, 1e-5)
        route1(nc, m, dict(gw=a["gate1T"]))
        experts1(nc, m, dict(w1=a["L1_ffn_w1"], w2=a["L1_ffn_w2"], b1=a["b11T"], b2=a["b21T"]), out)


def rope_tables():
    half = HD // 2
    inv = (np.float32(1.0) / np.float32(10000.0) ** (np.arange(half, dtype=np.float32) / np.float32(half)))
    ang = np.arange(T, dtype=np.float32)[:, None] * inv[None, :].astype(np.float32)
    sin, cos = np.sin(ang).T, np.cos(ang).T
    return (np.ascontiguousarray(np.tile(np.concatenate([cos, cos]), (H, 1)), np.float32),
            np.ascontiguousarray(np.tile(np.concatenate([-sin, sin]), (H, 1)), np.float32))


def kernel(**inputs):
    import concourse.bacc as bacc
    from concourse.bass_utils import run_bass_kernel_spmd as run

    i = {k: np.asarray(v) for k, v in inputs.items()}
    swap = np.arange(D).reshape(H, 2, HD // 2)[:, ::-1].reshape(D)
    order = np.arange(D).reshape(PAIRS, 2, HD).transpose(2, 1, 0).reshape(D)
    cos, sin = (t[order] for t in rope_tables())
    head = order // HD
    blocks = np.zeros((D, D), np.float32)
    for h in range(H):
        blocks[HD * h:HD * h + HD, HD * h:HD * h + HD] = i["L0_attn_w_att_val"][h]
    wqkv = np.concatenate([i["L1_attn_Wqkv"][:, :D][:, order], i["L1_attn_Wqkv"][:, D:2 * D][:, order],
                           i["L1_attn_Wqkv"][:, 2 * D:]], 1)
    arrays = {
        "watt": blocks[order][:, order],
        "same_head": (head[:, None] == head[None, :]).astype(np.float32),
        "wvT": i["L0_attn_wv_w"].T[order], "L0_attn_wv_b": i["L0_attn_wv_b"],
        "outT": i["L0_attn_out_w"].T, "L0_attn_out_b": i["L0_attn_out_b"],
        "cos": cos, "sin": sin,
        "wqT": i["L0_ffn_Wq"].T[:, order], "wqrT": i["L0_ffn_Wq"][swap].T[:, order], "wdkvT": i["L0_ffn_Wdkv"].T,
        "wukT": i["L0_ffn_Wuk"].T[:, order], "wukrT": i["L0_ffn_Wuk"][swap].T[:, order], "wuvT": i["L0_ffn_Wuv"].T,
        "woT": i["L0_ffn_Wo"].T,
        "n1": i["L0_ffn_norm1_w"].reshape(D, 1), "n2": i["L0_ffn_norm2_w"].reshape(D, 1),
        "ln_g": i["L0_ffn_ln_g"].reshape(LAT, 1), "ln_b": i["L0_ffn_ln_b"].reshape(LAT, 1),
        "gwT": i["L0_ffn_gate_w"].T, "L0_ffn_gate_b": i["L0_ffn_gate_b"],
        "w1T": i["L0_ffn_W1"].transpose(2, 0, 1),
        "b1T": i["L0_ffn_b1"].reshape(E0, F0 // P, P).transpose(2, 0, 1),
        "w2T": i["L0_ffn_W2"].reshape(E0, D, F0 // P, P).transpose(3, 0, 2, 1),
        "b2T": i["L0_ffn_b2"].T,
        "L1_attn_Wqkv": wqkv, "L1_attn_Wproj": i["L1_attn_Wproj"], "L1_attn_bproj": i["L1_attn_bproj"],
        "q_scale": i["L1_attn_q_scale"][order % HD].reshape(D, 1), "k_scale": i["L1_attn_k_scale"][order % HD].reshape(D, 1),
        "gate1T": i["L1_ffn_gate_w"].T,
        "L1_ffn_w1": i["L1_ffn_w1"], "L1_ffn_w2": i["L1_ffn_w2"],
        "b11T": i["L1_ffn_b1"].reshape(E1, F1 // P, P).transpose(0, 2, 1),
        "b21T": i["L1_ffn_b2"].reshape(E1, D, 1),
    }
    nc = bacc.Bacc("TRN2", target_bir_lowering=False, num_devices=1)
    feeds, aps = {"x": np.ascontiguousarray(i["L0_attn_x"])}, {}
    x = nc.dram_tensor("x", (B, T, D), f32, kind="ExternalInput").ap()
    for name, v in arrays.items():
        feeds["w_" + name] = np.ascontiguousarray(v)
        aps[name] = nc.dram_tensor("w_" + name, v.shape, f32, kind="ExternalInput").ap()
    out = nc.dram_tensor("out", (B, T, D), f32, kind="ExternalOutput").ap()
    two_layers(nc, x, aps, out)
    r = run(nc, [feeds], core_ids=[0])
    return r.results[0]["out"]
```

```python
from contextlib import ExitStack, contextmanager

import numpy as np

import concourse.bass as bass
import concourse.mybir as mybir

f32 = mybir.dt.float32
bf16 = mybir.dt.bfloat16
i32 = mybir.dt.int32
u32 = mybir.dt.uint32
ALU = mybir.AluOpType
ACT = mybir.ActivationFunctionType
AX = mybir.AxisListType

B, T, D = 32, 256, 128
P = 128
H, HD = 16, 8
NT = B * T // P
TT = T // P
PAIRS = H // 2
ROWS = 6 * 2 * HD
VW = HD + 1
UNITS = 2 * B
UP = PAIRS // 2
LAT = 64
E0, F0 = 4, 512
E1, F1 = 8, 512
CAP = 1280
SLOTS = E1 * CAP
SCALE = float(HD) ** -0.5
MASKED = -1.0e30


@contextmanager
def semaphores(nc):
    taken = []

    def sem(name):
        taken.append(nc.alloc_semaphore(name))
        return taken[-1]

    yield sem
    nc.clear_and_free_semaphores(taken)
    nc.all_engine_barrier()


class Order:

    def __init__(self, per, round_):
        self.per, self.round, self.k = per, round_, 0

    def next(self):
        self.k += 1
        assert self.k <= self.per
        return self.round * self.per + self.k


def past(n):
    return not (isinstance(n, int) and n <= 0)


def take_moments(nc, m, src, n0, count):
    for t in range(count):
        i = nc.vector.bn_stats(m.moments[:, bass.ds(n0 + t, 1), :].rearrange("p o d -> p (o d)"),
                               src[:, bass.ds(n0 + t, 1), :].rearrange("p o d -> p (o d)"))
    return i


def layer_stats(nc, name, m, W, stat, rstd, eps, second_moment=False):
    with ExitStack() as ctx:
        sem = ctx.enter_context(semaphores(nc))
        sb = lambda n, s: ctx.enter_context(nc.sbuf_tensor(f"{name}_{n}", s, f32))
        parts, root, apart = m.moments, sb("root", [P, NT]), sb("apart", [P, NT])
        order, shifted, rooted = (sem(f"{name}_{x}") for x in ("order", "shifted", "rooted"))
        block = ctx.enter_context(nc.Block())

        @block.vector
        def _(dve):
            mean, var = stat[:, :, 0], stat[:, :, 1]
            nc.vector.tensor_tensor(apart[:, :], parts[:, :, 1], parts[:, :, 4], ALU.subtract).then_inc(order, 1)
            nc.vector.tensor_tensor(mean, parts[:, :, 1], parts[:, :, 4], ALU.add).then_inc(order, 1)
            nc.vector.tensor_tensor(var, parts[:, :, 2], parts[:, :, 5], ALU.add).then_inc(order, 1)
            dve.wait_ge(order, 3)
            nc.vector.tensor_scalar(mean, mean, 0.5, None, ALU.mult).then_inc(order, 1)
            nc.vector.tensor_scalar(var, var, 1.0 / W, None, ALU.mult).then_inc(order, 1)
            nc.vector.scalar_tensor_tensor(out=apart[:, :], in0=apart[:, :], scalar=0.25, in1=apart[:, :],
                                           op0=ALU.mult, op1=ALU.mult).then_inc(order, 1)
            dve.wait_ge(order, 6)
            nc.vector.tensor_tensor(var, var, apart[:, :], ALU.add).then_inc(order, 1)
            dve.wait_ge(order, 7)
            if second_moment:
                nc.vector.tensor_tensor(root[:, :], mean, mean, ALU.mult).then_inc(order, 1)
                dve.wait_ge(order, 8)
                nc.vector.tensor_tensor(root[:, :], root[:, :], var, ALU.add).then_inc(order, 1)
                dve.wait_ge(order, 9)
                nc.vector.tensor_scalar(root[:, :], root[:, :], eps, None, ALU.add).then_inc(shifted, 1)
            else:
                nc.vector.tensor_scalar(root[:, :], var, eps, None, ALU.add).then_inc(shifted, 1)
            dve.wait_ge(rooted, 1)
            nc.vector.reciprocal(rstd[:, :], root[:, :])

        @block.scalar
        def _(act):
            act.wait_ge(shifted, 1)
            nc.scalar.activation(root[:, :], root[:, :], ACT.Sqrt).then_inc(rooted, 1)


def project(nc, kind, m, w):
    plain, cosine, queries, keys = (kind == k for k in ("plain", "cosine", "queries", "keys"))
    rope = queries or keys
    W = LAT if keys else D
    NQ = 1 if rope else 2
    has_v = not queries
    LAG = 2 if cosine else 1
    RING = 4
    with ExitStack() as ctx:
        sb = lambda n, s, d=f32: ctx.enter_context(nc.sbuf_tensor(f"{kind}_{n}", s, d))
        ps = lambda n, s, d=f32: ctx.enter_context(nc.psum_tensor(f"{kind}_{n}", s, d))
        new_sem = ctx.enter_context(semaphores(nc))
        sem = lambda n: new_sem(f"{kind}_{n}")
        src, stat, rstd = (m.lat, m.lat_stat, m.lat_rstd) if keys else (m.x, m.x_stat, m.x_rstd)
        xn = sb("xn", [P, 2, TT, W])
        qk = sb("qk", [P, RING, NQ, T])
        if plain:
            xT = [qk[:, u, 1, :] for u in range(RING)]
        else:
            x_turned = sb("xT", [W, 2, T])
            xT = [x_turned[:, u % 2, :] for u in range(RING)]
        rest = sb("rest", [P, 2, NQ, T])
        parts = sb("parts", [P, RING, 3, NQ, T], bf16)
        if has_v:
            vt = sb("vt", [P, RING, TT, H, VW])
            v_ready, v_taken = sem("v_ready"), sem("v_taken")
        turn = [ps(f"turn{u}", [P, 512]) for u in range(2)]
        weights_in, cleared = sem("weights_in"), sem("cleared")
        normed = sem("normed")
        turned = sem("turned")
        x_ready = sem("x_ready")
        q_ready = sem("q_ready")
        qk_ready = sem("qk_ready")
        high, left, middle, low = sem("high"), sem("left"), sem("middle"), sem("low")
        stored = [sem(f"stored{u}") for u in range(RING)]
        STORES = 3 * NQ + has_v
        ordered = sem("ordered")

        if plain or rope:
            wq = sb("wq", [W, D])
        if plain or keys:
            wv = sb("wv", [W, D])
            pv = ps("pv", [P, 512])
        if plain:
            pq = ps("pq", [P, 512])
            bv = sb("bv", [P, D])
            q_copied = sem("q_copied")
            loads = [(wq[:, :], w["watt"]), (wv[:, :], w["wvT"]), (bv[:, :], w["bv"].partition_broadcast(P))]
        if cosine:
            wqkv = sb("wqkv", [P, 3 * D])
            qkscale = sb("qkscale", [P, 2])
            square = sb("square", [P, 2, TT, 2 * D])
            norm = sb("norm", [P, 2, TT, 2, H])
            unit = sb("unit", [P, 2, TT, 2 * D])
            pqkv = [[ps(f"qkv{u}{t}", [P, 512]) for t in range(TT)] for u in range(2)]
            pturn = ps("pturn", [P, 512])
            squared, summed, rooted, shifted, inverted, unit_ready, unit_turned = (sem(x) for x in (
                "squared", "summed", "rooted", "shifted", "inverted", "unit_ready", "unit_turned"))
            loads = [(wqkv[:, :], w["wqkv"])] + [(qkscale[:, n:n + 1], w[x]) for n, x in enumerate(("qs", "ks"))]
        if rope:
            pq, pq2 = [ps(f"pq{u}", [P, 512]) for u in range(2)], [ps(f"pqr{u}", [P, 512]) for u in range(2)]
            wq2 = sb("wq2", [W, D])
            gain = sb("gain", [W, 1])
            cos_t, sin_t = sb("cos", [P, T]), sb("sin", [P, T])
            a1, a2 = sb("a1", [P, 2, T]), sb("a2", [P, 2, T])
            multiplied = sem("multiplied")
            loads = [(cos_t[:, :], w["cos"]), (sin_t[:, :], w["sin"])]
        if queries:
            rr = sb("rr", [P, NT])
            wd = sb("wd", [P, LAT])
            pl = ps("pl", [P, 512])
            lat_made, lat_kept = sem("lat_made"), sem("lat_kept")
            r_made, r_root = sem("r_made"), sem("r_root")
            loads += [(wq[:, :], w["wqT"]), (wq2[:, :], w["wqrT"]), (wd[:, :], w["wdT"]), (gain[:, :], w["n1"])]
        if keys:
            shift = sb("shift", [W, 1])
            loads += [(wq[:, :], w["wkT"]), (wq2[:, :], w["wkrT"]), (wv[:, :], w["wvT0"]),
                      (gain[:, :], w["lg"]), (shift[:, :], w["lb"])]
        N_LOADS = len(loads)
        block = ctx.enter_context(nc.Block())

        def steps(eng, step):
            for u in range(RING):
                step(0, u)
            with eng.Fori(1, B // RING - 1) as j:
                for u in range(RING):
                    step(j, u)
            for n in range(B - RING, B + LAG):
                step(n // RING, n % RING)

        def run(stage, j, u, d):
            j, u = j + (u + d) // RING, (u + d) % RING
            if not isinstance(j, int) or 0 <= j * RING + u < B:
                stage(j, u)

        @block.sync
        def _(sp):
            for dst, s in loads:
                sp.dma_start(dst, s).then_inc(weights_in, 16)

            def store(j, u):
                b = j * RING + u
                if has_v:
                    sp.wait_ge(v_taken, b + 1)
                    sp.dma_start(m.v_dram[bass.ds(b, 1), :, :, :].rearrange("o p t c -> (o p) t c"),
                                 vt[:, u, :, :, :].rearrange("p t h c -> p t (h c)")).then_inc(stored[u], 16)
                sp.wait_ge(low, b + 1)
                picks = {"q": ((0, 3, 0, True), (3, 2, 1, True), (5, 1, 2, True)),
                         "k": ((0, 3, 0, False), (3, 2, 0, False), (5, 1, 0, False))}
                for n, name in enumerate("q" if queries else "k" if keys else "qk"):
                    dram = m.q_dram if name == "q" else m.k_dram
                    for r, count, part, repeated in picks[name]:
                        dst = dram[bass.ds(b, 1), r:r + count, :, :, :, :].rearrange("o r d x p t -> (o d x p) r t")
                        src_ = (parts[:, u, part:part + 1, n, :].broadcast_to([P, count, T]) if repeated else
                                parts[:, u, part:part + count, n, :])
                        sp.dma_start(dst, src_).then_inc(stored[u], 16)

            steps(sp, lambda j, u: run(store, j, u, -LAG))
            for u in range(RING):
                sp.wait_ge(stored[u], STORES * 16 * (B // RING))

        @block.gpsimd
        def _(pool):
            if has_v:
                for u in range(RING):
                    nc.gpsimd.memset(vt[:, u, :, :, :], 1.0).then_inc(cleared, 1)

            def rotated(j, u):
                b = j * RING + u
                if past(b - RING + 1):
                    pool.wait_ge(left, b - RING + 1)
                pool.wait_ge(multiplied, b * 2 + 2)
                nc.gpsimd.tensor_tensor(qk[:, u, 0, :], a1[:, u % 2, :], a2[:, u % 2, :], ALU.add).then_inc(qk_ready, 1)

            def lowest(j, u):
                b = j * RING + u
                pool.wait_ge(middle, b + 1)
                nc.gpsimd.tensor_tensor(parts[:, u, 2, :, :], rest[:, u % 2, :, :], parts[:, u, 1, :, :],
                                        ALU.subtract).then_inc(low, 1)

            def step(j, u):
                if rope:
                    run(rotated, j, u, 0)
                run(lowest, j, u, -LAG)
            steps(pool, step)

        @block.vector
        def _(dve):
            if queries:
                nc.vector.tensor_tensor(rr[:, :], rstd[:, :], rstd[:, :], ALU.mult).then_inc(r_made, 1)
                dve.wait_ge(r_made, 1)
                nc.vector.tensor_tensor(rr[:, :], rr[:, :], stat[:, :, 1], ALU.mult).then_inc(r_made, 1)
                dve.wait_ge(r_made, 2)
                nc.vector.tensor_scalar(rr[:, :], rr[:, :], 1e-6, None, ALU.add).then_inc(r_made, 1)
                dve.wait_ge(r_root, 1)
                nc.vector.reciprocal(rr[:, :], rr[:, :]).then_inc(r_made, 1)
                dve.wait_ge(r_made, 4)

            def row_of(a, n):
                return a[:, bass.ds(n, 1), :].rearrange("p o d -> p (o d)")

            def normalize(j, u):
                b = j * RING + u
                n0 = j * (RING * TT) + u * TT
                if past(b - 1):
                    dve.wait_ge(turned, b - 1)
                for t in range(TT):
                    n = n0 + t
                    mean, inv = stat[:, bass.ds(n, 1), 0], rstd[:, bass.ds(n, 1)]
                    dst, row = row_of(m.y, n) if queries else xn[:, u % 2, t, :], row_of(src, n)
                    if plain:
                        dst = dst.rearrange("p (d x q) -> p d x q", x=2, d=HD)
                        row = row.rearrange("p (q x d) -> p d x q", x=2, d=HD)
                    nc.vector.tensor_scalar(dst, row, mean, inv, ALU.subtract, ALU.mult)\
                        .then_inc(ordered if queries else normed, 1)
                if queries:
                    for t in range(TT):
                        n = n0 + t
                        dve.wait_ge(ordered, b * TT + t + 1)
                        nc.vector.tensor_scalar(xn[:, u % 2, t, :], row_of(m.y, n), rr[:, bass.ds(n, 1)], None, ALU.mult)\
                            .then_inc(normed, 1)
                if plain or cosine:
                    dve.wait_ge(normed, b * TT + TT)
                    two = m.x[:, bass.ds(n0, TT), :]
                    bias = (m.out_bias if plain else m.proj_bias)[:, :]
                    nc.vector.tensor_tensor(two, two, bias.unsqueeze(1).broadcast_to([P, TT, D]), ALU.add)

            def multiplied_rope(j, u):
                b = j * RING + u
                if past(b - 1):
                    dve.wait_ge(qk_ready, b - 1)
                dve.wait_ge(q_ready, b + 1)
                nc.vector.tensor_tensor(a1[:, u % 2, :], pq[u % 2][:, 0:T], cos_t[:, :], ALU.mult).then_inc(multiplied, 1)
                nc.vector.tensor_tensor(a2[:, u % 2, :], pq2[u % 2][:, 0:T], sin_t[:, :], ALU.mult).then_inc(multiplied, 1)

            def keep_latent(j, u):
                dve.wait_ge(lat_made, j * RING + u + 1)
                n0 = j * (RING * TT) + u * TT
                nc.vector.tensor_copy(m.lat[:, bass.ds(n0, TT), :],
                                      pl[:, 0:TT * LAT].rearrange("p (t c) -> p t c", t=TT))
                for t in range(TT):
                    i = nc.vector.bn_stats(m.moments[:, bass.ds(n0 + t, 1), :].rearrange("p o d -> p (o d)"),
                                           pl[:, t * LAT:(t + 1) * LAT])
                i.then_inc(lat_kept, 1)

            def take_v(j, u):
                if cosine:
                    dve.wait_ge(squared, j * RING + u + 1)
                else:
                    dve.wait_ge(v_ready, j * RING + u + 1)
                if past(j):
                    dve.wait_ge(stored[u], j * (STORES * 16))
                for t in range(TT):
                    v = pqkv[u % 2][t][:, 2 * D:3 * D] if cosine else pv[:, t * D:(t + 1) * D]
                    v = v.rearrange("p (h c) -> p h c", h=H)
                    if plain:
                        i = nc.vector.tensor_tensor(vt[:, u, t, :, 0:HD], v, bv[:, :].rearrange("p (h c) -> p h c", h=H),
                                                    ALU.add)
                    else:
                        i = nc.vector.tensor_copy(vt[:, u, t, :, 0:HD], v)
                i.then_inc(v_taken, 1)

            def sum_squares(j, u):
                b = j * RING + u
                dve.wait_ge(squared, b + 1)
                if past(b - 1):
                    dve.wait_ge(unit_ready, (b - 1) * TT)
                nc.vector.tensor_reduce(norm[:, u % 2, :, :, :].rearrange("p t n h -> p (t n) h"),
                                        square[:, u % 2, :, :].rearrange("p t (n d g) -> p (t n) g d", n=2, d=HD),
                                        AX.X, ALU.add).then_inc(summed, 1)

            def to_unit(j, u):
                b = j * RING + u
                nn = norm[:, u % 2, :, :, :].rearrange("p t n h -> p (t n h)")
                dve.wait_ge(rooted, b + 1)
                nc.vector.tensor_scalar(nn, nn, 1e-8, None, ALU.add).then_inc(shifted, 1)
                dve.wait_ge(shifted, b + 1)
                nc.vector.reciprocal(nn, nn).then_inc(inverted, 1)
                dve.wait_ge(inverted, b + 1)
                if past(b - 1):
                    dve.wait_ge(unit_turned, b - 1)
                for t in range(TT):
                    nc.vector.tensor_tensor(unit[:, u % 2, t, :].rearrange("p (n d g) -> p n d g", n=2, d=HD),
                                            pqkv[u % 2][t][:, 0:2 * D].rearrange("p (n d g) -> p n d g", n=2, d=HD),
                                            norm[:, u % 2, t, :, :].unsqueeze(2).broadcast_to([P, 2, HD, H]),
                                            ALU.mult).then_inc(unit_ready, 1)

            def subtract_high(j, u):
                b = j * RING + u
                dve.wait_ge(high, b + 1)
                if past(b - 1):
                    dve.wait_ge(low, b - 1)
                nc.vector.tensor_tensor(rest[:, u % 2, :, :], qk[:, u, :, :], parts[:, u, 0, :, :],
                                        ALU.subtract).then_inc(left, 1)

            dve.wait_ge(weights_in, 16 * N_LOADS)
            if has_v:
                dve.wait_ge(cleared, RING)
            normalize(0, 0)
            normalize(0, 1)

            def step(j, u):
                run(normalize, j, u, 2)
                if cosine:
                    run(to_unit, j, u, -1)
                if rope:
                    run(multiplied_rope, j, u, 0)
                if queries:
                    run(keep_latent, j, u, 0)
                run(subtract_high, j, u, -LAG)
                if has_v:
                    run(take_v, j, u, 0)
                if cosine:
                    run(sum_squares, j, u, 0)
            steps(dve, step)

        @block.tensor
        def _(pe):
            def turns(j, u):
                b = j * RING + u
                pe.wait_ge(normed, b * TT + TT)
                if past(b - 1):
                    pe.wait_ge(x_ready, b - 1)
                for t in range(TT):
                    if keys:
                        i = nc.tensor.matmul(turn[u % 2][0:W, t * P:(t + 1) * P], xn[:, u % 2, t, :], m.ident[:, :],
                                             start=True, stop=True)
                    else:
                        i = nc.tensor.transpose(turn[u % 2][0:W, t * P:(t + 1) * P], xn[:, u % 2, t, :], m.ident[:, :])
                i.then_inc(turned, 1)

            turns(0, 0)
            pe.wait_ge(weights_in, 16 * N_LOADS)

            def products(j, u):
                b = j * RING + u
                pe.wait_ge(x_ready, b + 1)
                if plain:
                    if past(b):
                        pe.wait_ge(q_copied, b)
                    nc.tensor.matmul(pq[:, 0:T], wq[:, :], xT[u], start=True, stop=True).then_inc(q_ready, 1)
                if rope:
                    if past(b - 1):
                        pe.wait_ge(multiplied, (b - 1) * 2)
                    nc.tensor.matmul(pq[u % 2][:, 0:T], wq[:, :], xT[u], start=True, stop=True)
                    nc.tensor.matmul(pq2[u % 2][:, 0:T], wq2[:, :], xT[u], start=True, stop=True).then_inc(q_ready, 1)
                if queries:
                    if past(b):
                        pe.wait_ge(lat_kept, b)
                    for t in range(TT):
                        i = nc.tensor.matmul(pl[:, t * LAT:(t + 1) * LAT], xT[u][:, t * P:(t + 1) * P], wd[:, :],
                                             start=True, stop=True)
                    i.then_inc(lat_made, 1)
                if plain or keys:
                    if past(b):
                        pe.wait_ge(v_taken, b)
                    for t in range(TT):
                        i = nc.tensor.matmul(pv[:, t * D:(t + 1) * D], xT[u][:, t * P:(t + 1) * P], wv[:, :],
                                             start=True, stop=True)
                    i.then_inc(v_ready, 1)
                if cosine:
                    if past(b - 1):
                        pe.wait_ge(unit_ready, (b - 1) * TT)
                        pe.wait_ge(v_taken, b - 1)
                    for t in range(TT):
                        i = nc.tensor.matmul(pqkv[u % 2][t][:, 0:3 * D], xT[u][:, t * P:(t + 1) * P], wqkv[:, :],
                                             start=True, stop=True)
                    i.then_inc(q_ready, 1)

            def turn_unit(j, u):
                b = j * RING + u
                pe.wait_ge(unit_ready, b * TT + TT)
                if past(b):
                    pe.wait_ge(qk_ready, b)
                for n in range(2):
                    for t in range(TT):
                        c = n * T + t * P
                        i = nc.tensor.transpose(pturn[:, c:c + P], unit[:, u % 2, t, n * D:(n + 1) * D], m.ident[:, :])
                i.then_inc(unit_turned, 1)

            def step(j, u):
                run(turns, j, u, 1)
                run(products, j, u, 0)
                if cosine:
                    run(turn_unit, j, u, -1)
            steps(pe, step)

        @block.scalar
        def _(act):
            if queries:
                act.wait_ge(r_made, 3)
                nc.scalar.activation(rr[:, :], rr[:, :], ACT.Sqrt).then_inc(r_root, 1)
            if not plain:
                act.wait_ge(weights_in, 16 * N_LOADS)

            def take(j, u):
                b = j * RING + u
                act.wait_ge(turned, b + 1)
                if plain:
                    if past(b - RING + 1):
                        act.wait_ge(v_ready, b - RING + 1)
                        act.wait_ge(left, b - RING + 1)
                elif past(b - 1):
                    act.wait_ge(lat_made if queries else q_ready if cosine else v_ready, b - 1)
                if rope:
                    nc.scalar.activation(xT[u], turn[u % 2][0:W, 0:T], ACT.Identity, scale=gain[:, :],
                                         bias=shift[:, :] if keys else 0.0).then_inc(x_ready, 1)
                else:
                    nc.scalar.activation(xT[u], turn[u % 2][0:W, 0:T], ACT.Copy).then_inc(x_ready, 1)

            def copy_q(j, u):
                b = j * RING + u
                act.wait_ge(q_ready, b + 1)
                if past(b - RING + 1):
                    act.wait_ge(left, b - RING + 1)
                nc.scalar.activation(qk[:, u, 0, :], pq[:, 0:T], ACT.Copy).then_inc(q_copied, 1)

            def squares(j, u):
                b = j * RING + u
                act.wait_ge(q_ready, b + 1)
                if past(b - 1):
                    act.wait_ge(summed, b - 1)
                for t in range(TT):
                    i = nc.scalar.activation(square[:, u % 2, t, :], pqkv[u % 2][t][:, 0:2 * D], ACT.Square)
                i.then_inc(squared, 1)

            def roots(j, u):
                nn = norm[:, u % 2, :, :, :].rearrange("p t n h -> p (t n h)")
                act.wait_ge(summed, j * RING + u + 1)
                nc.scalar.activation(nn, nn, ACT.Sqrt, scale=1.0 / HD).then_inc(rooted, 1)

            def scaled_unit(j, u):
                b = j * RING + u
                act.wait_ge(unit_turned, b + 1)
                if past(b - RING + 1):
                    act.wait_ge(left, b - RING + 1)
                for n in range(2):
                    i = nc.scalar.activation(qk[:, u, n, :], pturn[:, n * T:(n + 1) * T], ACT.Copy,
                                             scale=qkscale[:, n:n + 1])
                i.then_inc(qk_ready, 1)

            def split_high(j, u):
                b = j * RING + u
                if plain:
                    act.wait_ge(q_copied, b + 1)
                else:
                    act.wait_ge(qk_ready, b + 1)
                if past(j):
                    act.wait_ge(stored[u], j * (STORES * 16))
                nc.scalar.activation(parts[:, u, 0, :, :], qk[:, u, :, :], ACT.Copy).then_inc(high, 1)

            def split_middle(j, u):
                act.wait_ge(left, j * RING + u + 1)
                nc.scalar.activation(parts[:, u, 1, :, :], rest[:, u % 2, :, :], ACT.Copy).then_inc(middle, 1)

            take(0, 0)

            def step(j, u):
                if cosine:
                    run(roots, j, u, -1)
                run(split_high, j, u, -LAG)
                run(take, j, u, 1)
                if cosine:
                    run(squares, j, u, 0)
                if plain:
                    run(copy_q, j, u, 0)
                run(split_middle, j, u, -LAG)
                if cosine:
                    run(scaled_unit, j, u, -1)
            steps(act, step)


def attend(nc, kind, m, w):
    causal = kind == "causal"
    RING = 4
    QUAD = 4
    SW = T + (P if causal else T)
    with ExitStack() as ctx:
        sb = lambda n, s, d=f32: ctx.enter_context(nc.sbuf_tensor(f"{kind}{m.serial}_{n}", s, d))
        ps = lambda n, s, d=f32: ctx.enter_context(nc.psum_tensor(f"{kind}{m.serial}_{n}", s, d))
        new_sem = ctx.enter_context(semaphores(nc))
        sem = lambda n: new_sem(f"{kind}{m.serial}_{n}")
        resid = m.y if causal else m.x
        qst, kst = m.qst, m.kst
        vst = sb("vst", [P, RING, TT, H // 2, VW])
        neg = sb("neg", [P, 2, TT, 2, UP])
        msp = sb("msp", [P, 2, TT, 2, 2, UP], bf16)
        mrow = sb("mrow", [2 * 2 * UP, 2, T], bf16)
        prob = sb("prob", [P, UP, 2, SW])
        usb = sb("usb", [P, 2, T])
        rec = sb("rec", [P, TT * H // 2])
        o = sb("o", [P, TT, D])
        oT = sb("oT", [P, T])
        wo = sb("wo", [P, D])
        ps_s = [ps(f"s{t}", [P, 512]) for t in range(2)]
        ps_st = [ps(f"st{t}", [P, 2, 512]) for t in range(2)]
        ps_u = ps("u", [P, 512])
        ps_m = ps("m", [P, 512])

        w_in = sem("w_in")
        stack_in = [sem(f"stack_in{k}") for k in range(RING)]
        mrow_in = [sem(f"mrow_in{k}") for k in range(RING)]
        s_ready, s_read = sem("s_ready"), sem("s_read")
        halved = sem("halved")
        msplit, mturned, mrow_ready = sem("msplit"), sem("mturned"), sem("mrow_ready")
        st_ready, exp_done = sem("st_ready"), sem("exp_done")
        pv_done, u_out = sem("pv_done"), sem("u_out")
        t_ready, inverted, t_read = sem("t_ready"), sem("inverted"), sem("t_read")
        ot_ready, ot_out = sem("ot_ready"), sem("ot_out")
        proj_ready, added = sem("proj_ready"), sem("added")
        cleared = sem("u_cleared")
        STACK_DMAS, MROW_DMAS = 4, 1
        block = ctx.enter_context(nc.Block())

        def steps(eng, step):
            for k in range(RING):
                step(0, k)
            with eng.Fori(1, UNITS // RING - 1) as j:
                for k in range(RING):
                    step(j, k)
            for k in range(RING):
                step(UNITS // RING - 1, k)
            for k in range(2):
                step(UNITS // RING, k)

        def has_unit(j, k, ahead):
            return not isinstance(j, int) or 0 <= j * RING + k + ahead < UNITS

        @block.sync
        def _(sp):
            sp.dma_start(wo[:, :], w["woT"]).then_inc(w_in, 16)

            def load(j, k):
                b, p0 = j * 2 + k // 2, UP * (k % 2)
                rows = m.q_dram[bass.ds(b, 1), :, :, :, p0:p0 + UP, :].rearrange("o r d x p t -> (o r d x) p t")
                sp.dma_start(qst[0:ROWS, k, :, :], rows).then_inc(stack_in[k], 16)
                for x in range(2):
                    rows = m.k_dram[bass.ds(b, 1), :, :, x, p0:p0 + UP, :].rearrange("o r d p t -> (o r d) p t")
                    sp.dma_start(kst[x:ROWS:2, k, x, :, :], rows).then_inc(stack_in[k], 16)
                h0 = (H // 2) * (k % 2)
                v = m.v_dram[bass.ds(b, 1), :, :, h0 * VW:(h0 + H // 2) * VW].rearrange("o p t c -> (o p) t c")
                sp.dma_start(vst[:, k, :, :, :].rearrange("p t h c -> p t (h c)"), v).then_inc(stack_in[k], 16)

            def bring_max(j, k):
                u = j * RING + k
                sp.wait_ge(mrow_ready, u + 1)
                sp.dma_start(qst[ROWS:ROWS + 4, k, :, :].rearrange("c p t -> c (p t)"), mrow[:, k % 2, :])\
                    .then_inc(mrow_in[k], 16)

            for k in range(3):
                load(0, k)
            bring_max(0, 0)

            def step(j, k):
                s = j * RING + k
                if has_unit(j, k, 3):
                    if past(s):
                        sp.wait_ge(pv_done, s * 2)
                    load(j + (k + 3) // RING, (k + 3) % RING)
                if has_unit(j, k, 1):
                    bring_max(j + (k + 1) // RING, (k + 1) % RING)
            steps(sp, step)

        def pass1_columns(t):
            return P if causal and t == 0 else T

        @block.tensor
        def _(pe):
            def scores1(j, k, p, tiles=range(TT)):
                u = j * RING + k
                if p == 0 and 0 in tiles:
                    pe.wait_ge(stack_in[k], (j + 1) * (STACK_DMAS * 16))
                for t in tiles:
                    c = pass1_columns(t)
                    n = (u * UP + p) * TT + t
                    if past(n - 1):
                        pe.wait_ge(s_read, n - 1)
                    q = qst[0:ROWS, k, p, t * P:(t + 1) * P]
                    out = ps_s[t][:, :].rearrange("p (x c) -> p x c", x=2)[:, :, 0:c]
                    i = nc.tensor.matmul(out, q, kst[0:ROWS, k, :, p, 0:c], start=True, stop=not causal)
                    if causal:
                        i = nc.tensor.matmul(out[:, :, c - P:c], m.ident16[:, :], m.mask_qk[:, :, :],
                                             start=False, stop=True)
                    i.then_inc(s_ready, 1)

            def turn_max(j, k):
                u = j * RING + k
                pe.wait_ge(msplit, u + 1)
                if past(u - 1):
                    pe.wait_ge(u_out, (u - 1) * 2)
                if not past(u - 1) and past(u):
                    pe.wait_ge(mrow_ready, 1)
                for t in range(TT):
                    i = nc.tensor.matmul(ps_u[0:4 * UP, T + t * P:T + (t + 1) * P],
                                         msp[:, k % 2, t, :, :, :].rearrange("p x r q -> p (x r q)"),
                                         m.ident16[:, :], start=True, stop=True)
                i.then_inc(mturned, 1)

            def scores2(j, k, p, x):
                u = j * RING + k
                if p == 0 and x == 0:
                    pe.wait_ge(mrow_in[k], (j + 1) * (MROW_DMAS * 16))
                n = u * UP + p
                if x == 0 and past(n - 1):
                    pe.wait_ge(exp_done, n - 1)
                for kt in range(TT):
                    q0 = P if causal and kt else 0
                    c0 = T * kt
                    key = kst[0:ROWS + 4, k, x, p, kt * P:(kt + 1) * P]
                    out = ps_st[p % 2][:, x, c0:c0 + T - q0]
                    i = nc.tensor.matmul(out, key, qst[0:ROWS + 4, k, p, q0:T], start=True, stop=not causal)
                    if causal:
                        i = nc.tensor.matmul(out[:, 0:P], m.ident16[:, :], m.mask_kq[:, :], start=False, stop=True)
                if x == 1:
                    i.then_inc(st_ready, 1)

            def values(j, k, qd):
                u = j * RING + k
                n = u * 2 + qd
                pe.wait_ge(exp_done, u * UP + 2 * qd + 2)
                if past(n):
                    pe.wait_ge(u_out, n)
                if qd == 0 and has_unit(j, k, 1):
                    pe.wait_ge(mrow_ready, u + 2)
                for kt in range(TT):
                    q0 = P if causal and kt else 0
                    for g in range(QUAD):
                        h = QUAD * qd + g
                        i = nc.tensor.matmul(ps_u[32 * g:32 * g + VW, q0:T], vst[:, k, kt, h, :],
                                             prob[:, h // 2, h % 2, T * kt:T * kt + T - q0],
                                             start=kt == 0, stop=kt == TT - 1, tile_position=(0, 32 * g))
                i.then_inc(pv_done, 1)

            def turn_values(j, k):
                pe.wait_ge(u_out, (j * RING + k) * 2 + 2)
                for t in range(TT):
                    for qd in range(2):
                        c = (t * 2 + qd) * P
                        i = nc.tensor.transpose(ps_m[:, c:c + P], usb[:, qd, t * P:(t + 1) * P], m.ident[:, :])
                i.then_inc(t_ready, 1)

            pe.wait_ge(cleared, 1)
            for p in range(UP):
                scores1(0, 0, p)
            for p in range(UP):
                scores1(0, 1, p)
            turn_max(0, 0)
            pe.wait_ge(w_in, 16)

            def step(j, k):
                s = j * RING + k
                jj, kk = (j, k - 1) if k else (j - 1, RING - 1)
                behind = past(s) and has_unit(j, k, -1)
                for p in range(UP):
                    for i in range(2):
                        if has_unit(j, k, 2):
                            scores1(j + (k + 2) // RING, (k + 2) % RING, p, [i])
                        if has_unit(j, k, 0):
                            scores2(j, k, p, i)
                    if p == 0 and behind:
                        values(jj, kk, 1)
                    if p == 1 and has_unit(j, k, 1):
                        turn_max(j + (k + 1) // RING, (k + 1) % RING)
                    if p == 1 and behind:
                        if k % 2 == 1 and past(s - 1):
                            pe.wait_ge(ot_out, j * 2 + (k - 1) // 2)
                        elif k % 2 == 0 and past(s - 2):
                            pe.wait_ge(added, j * 2 + (k - 2) // 2)
                        elif past(s - 1):
                            pe.wait_ge(t_read, 1)
                        turn_values(jj, kk)
                    if p == 2 and has_unit(j, k, 0):
                        values(j, k, 0)
                    if p == 3 and k % 2 == 0 and past(s):
                        pe.wait_ge(t_read, s)
                        for t in range(TT):
                            i = nc.tensor.transpose(ps_m[:, t * P:(t + 1) * P], o[:, t, :], m.ident[:, :])
                        i.then_inc(ot_ready, 1)
                    if p == 3 and k % 2 == 1 and past(s - 1):
                        if behind:
                            pe.wait_ge(t_read, s)
                        pe.wait_ge(ot_out, j * 2 + (k - 1) // 2)
                        for t in range(TT):
                            i = nc.tensor.matmul(ps_m[:, t * P:(t + 1) * P], oT[:, t * P:(t + 1) * P], wo[:, :],
                                                 start=True, stop=True)
                        i.then_inc(proj_ready, 1)
            steps(pe, step)

        @block.vector
        def _(dve):
            nc.vector.memset(ps_u[:, :], 0.0).then_inc(cleared, 1)

            def maxima(j, k, p, tiles=range(TT)):
                u = j * RING + k
                for t in tiles:
                    c = pass1_columns(t)
                    dve.wait_ge(s_ready, (u * UP + p) * TT + t + 1)
                    if p == 0 and t == 0 and past(u - 1):
                        dve.wait_ge(msplit, u - 1)
                    nc.vector.tensor_reduce(neg[:, k % 2, t, :, p],
                                            ps_s[t][:, :].rearrange("p (x c) -> p x c", x=2)[:, :, 0:c],
                                            AX.X, ALU.max, negate=True).then_inc(s_read, 1)

            def split_max(j, k, part):
                u = j * RING + k
                n_ = neg[:, k % 2, :, :, :].rearrange("p t x q -> p (t x) q")
                hi, mid = (msp[:, k % 2, :, :, r, :].rearrange("p t x q -> p (t x) q") for r in range(2))
                if part == 0:
                    dve.wait_ge(s_read, (u + 1) * (UP * TT))
                    if past(u - 1):
                        dve.wait_ge(mturned, u - 1)
                    nc.vector.tensor_copy(hi, n_).then_inc(halved, 1)
                else:
                    dve.wait_ge(halved, u + 1)
                    nc.vector.tensor_tensor(mid, n_, hi, ALU.subtract).then_inc(msplit, 1)

            def normalize(j, k, part):
                u = j * RING + k
                h0 = (H // 2) * (k % 2)
                tv = ps_m[:, :].rearrange("p (g c) -> p g c", c=32)
                if part == 0:
                    dve.wait_ge(t_ready, u + 1)
                    if past(u):
                        dve.wait_ge(t_read, u)
                    nc.vector.reciprocal(rec[:, :], tv[:, :, HD]).then_inc(inverted, 1)
                else:
                    dve.wait_ge(inverted, u + 1)
                    nc.vector.tensor_tensor(o[:, :, h0 * HD:(h0 + H // 2) * HD].rearrange("p t (g c) -> p t g c", c=HD),
                                            tv[:, :, 0:HD].rearrange("p (t g) c -> p t g c", t=TT),
                                            rec[:, :].rearrange("p (t g) -> p t g", t=TT).unsqueeze(3)
                                            .broadcast_to([P, TT, H // 2, HD]), ALU.mult).then_inc(t_read, 1)

            for k in range(2):
                for p in range(UP):
                    for t in range(TT):
                        maxima(0, k, p, [t])
                        if k == 1 and p == 0:
                            split_max(0, 0, t)

            def add_output(before, n0):
                dve.wait_ge(proj_ready, before + 1)
                x = resid[:, bass.ds(n0, TT), :]
                nc.vector.tensor_tensor(x, x, ps_m[:, 0:TT * D].rearrange("p (t c) -> p t c", t=TT),
                                        ALU.add).then_inc(added, 1)

            def step(j, k):
                s = j * RING + k
                jj, kk = (j, k - 1) if k else (j - 1, RING - 1)
                behind = past(s) and has_unit(j, k, -1)
                for p in range(UP):
                    for t in range(TT):
                        summed = k % 2 == 0 and past(s - 2)
                        if p == 2 and t == 0 and summed:
                            dve.wait_ge(added, j * 2 + (k - 4) // 2 + 1)
                        if has_unit(j, k, 2):
                            maxima(j + (k + 2) // RING, (k + 2) % RING, p, [t])
                        if p == 2 and t == 0 and summed:
                            take_moments(nc, m, resid, (j * 2 + (k - 4) // 2) * TT, TT)
                        if p == 0 and has_unit(j, k, 1):
                            split_max(j + (k + 1) // RING, (k + 1) % RING, t)
                        if p == 1 and t == 0 and summed:
                            add_output(j * 2 + (k - 4) // 2, (j * 2 + (k - 4) // 2) * TT)
                        if p == 2 and behind:
                            normalize(jj, kk, t)
            steps(dve, step)
            add_output(B - 1, (B - 1) * TT)
            dve.wait_ge(added, B)
            take_moments(nc, m, resid, (B - 1) * TT, TT)

        @block.scalar
        def _(act):
            def rows(j, k):
                u = j * RING + k
                act.wait_ge(mturned, u + 1)
                if past(u - 1):
                    act.wait_ge(mrow_in[(k - 2) % RING], (j + 1 - (k < 2)) * (MROW_DMAS * 16))
                nc.scalar.activation(mrow[:, k % 2, :], ps_u[0:4 * UP, T:2 * T], ACT.Copy).then_inc(mrow_ready, 1)

            def exps(j, k, p):
                n = (j * RING + k) * UP + p
                act.wait_ge(st_ready, n + 1)
                if p % 2 == 0 and past(n - UP + 1):
                    act.wait_ge(pv_done, (j * RING + k) * 2 + p // 2 - 1)
                nc.scalar.activation(prob[:, p, :, :], ps_st[p % 2][:, :, 0:SW], ACT.Exp, scale=SCALE)\
                    .then_inc(exp_done, 1)

            def keep_values(j, k, qd):
                n = (j * RING + k) * 2 + qd
                act.wait_ge(pv_done, n + 1)
                if past(j * RING + k):
                    act.wait_ge(t_ready, j * RING + k)
                nc.scalar.activation(usb[:, qd, :], ps_u[:, 0:T], ACT.Copy).then_inc(u_out, 1)

            rows(0, 0)

            def step(j, k):
                s = j * RING + k
                jj, kk = (j, k - 1) if k else (j - 1, RING - 1)
                if has_unit(j, k, 0):
                    exps(j, k, 0)
                if past(s) and has_unit(j, k, -1):
                    keep_values(jj, kk, 1)
                if has_unit(j, k, 0):
                    exps(j, k, 1)
                if has_unit(j, k, 1):
                    rows(j + (k + 1) // RING, (k + 1) % RING)
                if has_unit(j, k, 0):
                    exps(j, k, 2)
                    keep_values(j, k, 0)
                    exps(j, k, 3)
                if k % 2 == 0 and past(s):
                    act.wait_ge(ot_ready, j * 2 + k // 2)
                    nc.scalar.activation(oT[:, :], ps_m[:, 0:T], ACT.Copy).then_inc(ot_out, 1)
            steps(act, step)


def experts0(nc, m, w):
    G = 4
    N = G * P
    C = F0 // P
    GROUPS = NT // G
    with ExitStack() as ctx:
        sb = lambda n, s, d=f32: ctx.enter_context(nc.sbuf_tensor(f"e0_{n}", s, d))
        ps = lambda n, s, d=f32: ctx.enter_context(nc.psum_tensor(f"e0_{n}", s, d))
        new_sem = ctx.enter_context(semaphores(nc))
        sem = lambda n: new_sem(f"e0_{n}")
        w1, w2 = sb("w1", [P, E0, F0]), sb("w2", [P, E0, C, D])
        b1, b2 = sb("b1", [P, E0, C]), sb("b2", [P, E0])
        gw, gb, n2 = sb("gw", [P, E0]), sb("gb", [P, E0]), sb("n2", [P, 1])
        xn = sb("xn", [P, 2, G, D])
        xT = sb("xT", [P, 2, N])
        hid = sb("hid", [P, 4, N])
        yT = sb("yT", [P, 2, N])
        acc = sb("acc", [P, 2, G, D])
        lg, eq, one = sb("lg", [P, G, E0]), sb("eq", [P, G, E0]), sb("one", [P, 2, G, E0])
        top = sb("top", [P, G])
        turn, psl, pst = ps("turn", [P, 512]), ps("psl", [P, 512]), ps("pst", [P, 512])
        psh = [ps(f"h{i}", [P, 512]) for i in range(2)]
        psy = [ps(f"y{i}", [P, 512]) for i in range(2)]
        w_in, normed, turned, x_ready = sem("w_in"), sem("normed"), sem("turned"), sem("x_ready")
        lg_ready, order, chosen = sem("lg_ready"), sem("order"), sem("chosen")
        h_ready, h_act, h_dve = sem("h_ready"), sem("h_act"), sem("h_dve")
        y_done, y_out, t_ready, summed = (sem(x) for x in ("y_done", "y_out", "t_ready", "summed"))
        joined = sem("joined")
        block = ctx.enter_context(nc.Block())
        loads = [(w1, w["w1"]), (w2, w["w2"]), (b1, w["b1"]), (b2, w["b2"]), (gw, w["gw"]), (n2, w["n2"])]
        EC = E0 * C

        def groups(eng, step):
            for u in range(2):
                step(0, u)
            with eng.Fori(1, GROUPS // 2 - 1) as j:
                for u in range(2):
                    step(j, u)
            for u in range(2):
                step(GROUPS // 2 - 1, u)

        def last(j, u):
            return isinstance(j, int) and j * 2 + u == GROUPS - 1

        @block.sync
        def _(sp):
            for dst, s in loads:
                sp.dma_start(dst[:], s).then_inc(w_in, 16)
            sp.dma_start(gb[:, :], w["gb"].partition_broadcast(P)).then_inc(w_in, 16)

        @block.gpsimd
        def _(pool):
            def step(j, u):
                g = j * 2 + u
                pool.wait_ge(summed, g * E0 + E0)
                x = m.x[:, bass.ds(j * (2 * G) + u * G, G), :]
                nc.gpsimd.tensor_tensor(x, x, acc[:, u, :, :], ALU.add).then_inc(joined, 1)
            groups(pool, step)

        @block.vector
        def _(dve):
            def normalize(j, u):
                g = j * 2 + u
                if past(g - 1):
                    dve.wait_ge(turned, g - 1)
                for t in range(G):
                    n = j * (2 * G) + (u * G + t)
                    i = nc.vector.tensor_scalar(xn[:, u, t, :], m.y[:, bass.ds(n, 1), :].rearrange("p o d -> p (o d)"),
                                                m.y_rms[:, bass.ds(n, 1)], None, ALU.mult)
                i.then_inc(normed, 1)

            def choose(j, u):
                g = j * 2 + u
                o = Order(5, g)
                lgp = psl[:, 0:G * E0].rearrange("p (t e) -> p t e", e=E0)
                dve.wait_ge(lg_ready, g + 1)
                nc.vector.tensor_tensor(lg[:, :, :], lgp, gb[:, :].unsqueeze(1).broadcast_to([P, G, E0]),
                                        ALU.add).then_inc(order, 1)
                dve.wait_ge(order, o.next())
                nc.vector.tensor_reduce(top[:, :], lg[:, :, :], AX.X, ALU.max).then_inc(order, 1)
                dve.wait_ge(order, o.next())
                nc.vector.tensor_tensor(eq[:, :, :], lg[:, :, :], top[:, :].unsqueeze(2).broadcast_to([P, G, E0]),
                                        ALU.is_equal).then_inc(order, 1)
                dve.wait_ge(order, o.next())
                nc.vector.tensor_tensor(eq[:, :, :], eq[:, :, :], m.prior[:, 0:E0].unsqueeze(1)
                                        .broadcast_to([P, G, E0]), ALU.mult).then_inc(order, 1)
                dve.wait_ge(order, o.next())
                nc.vector.tensor_reduce(top[:, :], eq[:, :, :], AX.X, ALU.max).then_inc(order, 1)
                dve.wait_ge(order, o.next())
                nc.vector.tensor_tensor(one[:, u, :, :], eq[:, :, :], top[:, :].unsqueeze(2)
                                        .broadcast_to([P, G, E0]), ALU.is_equal).then_inc(chosen, 1)

            dve.wait_ge(w_in, 16 * (len(loads) + 1))
            normalize(0, 0)
            choose(0, 0)

            def add_expert(j, u, e):
                g = j * 2 + u
                dve.wait_ge(t_ready, g * E0 + e + 1)
                dve.wait_ge(chosen, g + 1)
                if e:
                    dve.wait_ge(summed, g * E0 + e)
                elif past(g - 1):
                    dve.wait_ge(joined, g - 1)
                for t in range(G):
                    n = j * (2 * G) + (u * G + t)
                    base = acc[:, u, t, :] if e else m.y[:, bass.ds(n, 1), :].rearrange("p o d -> p (o d)")
                    i = nc.vector.scalar_tensor_tensor(out=acc[:, u, t, :], in0=pst[:, t * P:(t + 1) * P],
                                                       scalar=one[:, u, t, e:e + 1], in1=base,
                                                       op0=ALU.mult, op1=ALU.add)
                i.then_inc(summed, 1)

            def step(j, u):
                g = j * 2 + u
                for q in range(EC + 4):
                    if q == 3 and past(g):
                        dve.wait_ge(joined, g)
                    if q < EC and q % 2:
                        dve.wait_ge(h_ready, g * EC + q + 1)
                        if past(g * EC + q - 3):
                            dve.wait_ge(y_done, g * EC + q - 3)
                        nc.vector.tensor_scalar(hid[:, q % 4, :], psh[q % 2][:, :], b1[:, q // C, q % C:q % C + 1], 0.0,
                                                ALU.add, ALU.max).then_inc(h_dve, 1)
                    if q == 3 and past(g):
                        take_moments(nc, m, m.x, j * (2 * G) + (u - 1) * G, G)
                    if q == 8 and not last(j, u):
                        normalize(j + u, 1 - u)
                    if q == 12 and not last(j, u):
                        choose(j + u, 1 - u)
                    if q >= 7 and q % 4 == 3:
                        add_expert(j, u, (q - 7) // 4)
            groups(dve, step)
            dve.wait_ge(joined, GROUPS)
            take_moments(nc, m, m.x, NT - G, G)

        @block.scalar
        def _(act):
            act.wait_ge(w_in, 16 * (len(loads) + 1))

            def take(j, u):
                g = j * 2 + u
                act.wait_ge(turned, g + 1)
                if past(g - 1):
                    act.wait_ge(h_ready, (g - 1) * EC)
                    act.wait_ge(lg_ready, g - 1)
                nc.scalar.activation(xT[:, u, :], turn[:, :], ACT.Copy, scale=n2[:, :]).then_inc(x_ready, 1)

            take(0, 0)

            def step(j, u):
                g = j * 2 + u
                for q in range(EC + 4):
                    if q < EC and q % 2 == 0:
                        act.wait_ge(h_ready, g * EC + q + 1)
                        if past(g * EC + q - 3):
                            act.wait_ge(y_done, g * EC + q - 3)
                        nc.scalar.activation(hid[:, q % 4, :], psh[q % 2][:, :], ACT.Relu,
                                             bias=b1[:, q // C, q % C:q % C + 1]).then_inc(h_act, 1)
                    if q == 9 and not last(j, u):
                        take(j + u, 1 - u)
                    if q >= 6 and q % 4 == 2:
                        e = (q - 6) // 4
                        act.wait_ge(y_done, g * EC + e * C + C)
                        if past(g * E0 + e - 1):
                            act.wait_ge(t_ready, g * E0 + e - 1)
                        nc.scalar.activation(yT[:, e % 2, :], psy[e % 2][:, :], ACT.Identity,
                                             bias=b2[:, e:e + 1]).then_inc(y_out, 1)
            groups(act, step)

        @block.tensor
        def _(pe):
            pe.wait_ge(w_in, 16 * (len(loads) + 1))

            def turns(j, u):
                g = j * 2 + u
                pe.wait_ge(normed, g + 1)
                if past(g):
                    pe.wait_ge(x_ready, g)
                for t in range(G):
                    i = nc.tensor.transpose(turn[:, t * P:(t + 1) * P], xn[:, u, t, :], m.ident[:, :])
                i.then_inc(turned, 1)

            def logits(j, u):
                g = j * 2 + u
                pe.wait_ge(x_ready, g + 1)
                if past(g):
                    pe.wait_ge(chosen, g)
                for t in range(G):
                    i = nc.tensor.matmul(psl[:, t * E0:(t + 1) * E0], xT[:, u, t * P:(t + 1) * P], gw[:, :],
                                         start=True, stop=True)
                i.then_inc(lg_ready, 1)

            turns(0, 0)
            logits(0, 0)

            def step(j, u):
                g = j * 2 + u
                for q in range(EC + 4):
                    if q < EC:
                        n = g * EC + q
                        if past(n - 1):
                            half = g * (EC // 2) + (q // 2)
                            pe.wait_ge(h_dve if q % 2 else h_act, half)
                        nc.tensor.matmul(psh[q % 2][:, :], w1[:, q // C, (q % C) * P:(q % C + 1) * P], xT[:, u, :],
                                         start=True, stop=True).then_inc(h_ready, 1)
                    r = q - 2
                    if 0 <= r < EC:
                        e, c = r // C, r % C
                        pe.wait_ge(h_dve if r % 2 else h_act, g * (EC // 2) + r // 2 + 1)
                        if c == 0 and past(g * E0 + e - 1):
                            pe.wait_ge(y_out, g * E0 + e - 1)
                        nc.tensor.matmul(psy[e % 2][:, :], w2[:, e, c, :], hid[:, r % 4, :],
                                         start=c == 0, stop=c == C - 1).then_inc(y_done, 1)
                    if q == 8 and not last(j, u):
                        turns(j + u, 1 - u)
                    if q == 11 and not last(j, u):
                        logits(j + u, 1 - u)
                    if q >= 7 and q % 4 == 3:
                        e = (q - 7) // 4
                        pe.wait_ge(y_out, g * E0 + e + 1)
                        if past(g * E0 + e):
                            pe.wait_ge(summed, g * E0 + e)
                        for t in range(G):
                            i = nc.tensor.transpose(pst[:, t * P:(t + 1) * P], yT[:, e % 2, t * P:(t + 1) * P],
                                                    m.ident[:, :])
                        i.then_inc(t_ready, 1)
            groups(pe, step)


def route1(nc, m, w):
    G, GROUPS = 4, NT // 4
    PARTS = 2
    PT = NT // PARTS
    with ExitStack() as ctx:
        sb = lambda n, s, d=f32: ctx.enter_context(nc.sbuf_tensor(f"r1_{n}", s, d))
        ps = lambda n, s, d=f32: ctx.enter_context(nc.psum_tensor(f"r1_{n}", s, d))
        new_sem = ctx.enter_context(semaphores(nc))
        sem = lambda n: new_sem(f"r1_{n}")
        gw = sb("gw", [P, E1])
        xn = sb("xn", [P, 2, G, D])
        xT = sb("xT", [P, 2, G * P])
        lg, ex, one = sb("lg", [P, NT, E1]), sb("ex", [P, NT, E1]), sb("one", [P, NT, E1])
        one16 = sb("one16", [P, NT, E1], bf16)
        tot = sb("tot", [P, NT, E1])
        inc = [sb(f"inc{c}", [P, E1, PT]) for c in range(PARTS)]
        mx, sm, esel = sb("mx", [P, NT]), sb("sm", [P, NT]), sb("esel", [P, NT])
        rank, keep, slot = sb("rank", [P, NT]), sb("keep", [P, NT]), sb("slot", [P, NT])
        onesf = sb("onesf", [P, PT])
        turn = [ps(f"turn{i}", [P, 512]) for i in range(2)]
        psl = [ps(f"l{i}", [P, 512]) for i in range(2)]
        ps_pre = [ps(f"ps_pre{c}", [P, 512]) for c in range(PARTS)]
        ps_tot = [ps(f"ps_tot{c}", [P, 512]) for c in range(PARTS)]
        w_in, normed, turned, x_ready, lg_ready, lg_kept = (sem(x) for x in ("w_in", "normed", "turned", "x_ready",
                                                                            "lg_ready", "lg_kept"))
        order, less, exped, counted, one_ready = (sem(x) for x in ("order", "less", "exped", "counted", "one_ready"))
        slot_ready, scattered = sem("slot_ready"), sem("scattered")
        block = ctx.enter_context(nc.Block())

        def groups(eng, step, c):
            first, end = c * GROUPS // PARTS // 2, (c + 1) * GROUPS // PARTS // 2
            for u in range(2):
                step(first, u)
            with eng.Fori(first + 1, end) as j:
                for u in range(2):
                    step(j, u)

        @block.sync
        def _(sp):
            sp.dma_start(gw[:, :], w["gw"]).then_inc(w_in, 16)

        @block.gpsimd
        def _(pool):
            for n in range(NT):
                if n % PT == 0:
                    pool.wait_ge(slot_ready, n // PT + 1)
                nc.gpsimd.indirect_dma_start(out=m.slots, out_offset=bass.IndirectOffsetOnAxis(
                    ap=m.to_slot[:, n:n + 1], axis=0), in_=m.y[:, n, :], in_offset=None,
                    bounds_check=SLOTS - 1, oob_is_err=False).then_inc(scattered, 16)
            pool.wait_ge(scattered, 16 * NT)

        @block.scalar
        def _(act):
            def step(j, u):
                g = j * 2 + u
                act.wait_ge(turned, g + 1)
                if past(g - 1):
                    act.wait_ge(lg_ready, g - 1)
                nc.scalar.activation(xT[:, u, :], turn[u][:, :], ACT.Copy).then_inc(x_ready, 1)

            for c in range(PARTS):
                groups(act, step, c)
                part = slice(c * PT, (c + 1) * PT)
                act.wait_ge(less, c + 1)
                nc.scalar.activation(ex[:, part, :], lg[:, part, :], ACT.Exp).then_inc(exped, 1)

        @block.tensor
        def _(pe):
            pe.wait_ge(w_in, 16)

            def step(j, u):
                g = j * 2 + u
                pe.wait_ge(normed, g + 1)
                if past(g - 1):
                    pe.wait_ge(x_ready, g - 1)
                for t in range(G):
                    i = nc.tensor.transpose(turn[u][:, t * P:(t + 1) * P], xn[:, u, t, :], m.ident[:, :])
                i.then_inc(turned, 1)
                pe.wait_ge(x_ready, g + 1)
                if past(g - 1):
                    pe.wait_ge(lg_kept, g - 1)
                for t in range(G):
                    i = nc.tensor.matmul(psl[u][:, t * E1:(t + 1) * E1], xT[:, u, t * P:(t + 1) * P], gw[:, :],
                                         start=True, stop=True)
                i.then_inc(lg_ready, 1)

            for c in range(PARTS):
                groups(pe, step, c)
                pe.wait_ge(one_ready, c + 1)
                rhs = one16[:, c * PT:(c + 1) * PT, :].rearrange("p n e -> p (n e)")
                nc.tensor.matmul(ps_pre[c][:, 0:PT * E1], m.before[:, :], rhs, start=True, stop=True)
                nc.tensor.matmul(ps_tot[c][:, 0:PT * E1], m.ones16[:, :], rhs, start=True, stop=True)\
                    .then_inc(counted, 1)

        @block.vector
        def _(dve):
            def normalize(j, u):
                g = j * 2 + u
                if past(g - 1):
                    dve.wait_ge(turned, g - 1)
                for t in range(G):
                    n = j * (2 * G) + (u * G + t)
                    row = m.x[:, bass.ds(n, 1), :].rearrange("p o d -> p (o d)")
                    mean, inv = m.x_stat[:, bass.ds(n, 1), 0], m.x_rstd[:, bass.ds(n, 1)]
                    nc.vector.tensor_scalar(m.y[:, bass.ds(n, 1), :].rearrange("p o d -> p (o d)"), row, mean, inv,
                                            ALU.subtract, ALU.mult)
                    i = nc.vector.tensor_scalar(xn[:, u, t, :], row, mean, inv, ALU.subtract, ALU.mult)
                i.then_inc(normed, 1)

            def keep_logits(j, u):
                dve.wait_ge(lg_ready, j * 2 + u + 1)
                nc.vector.tensor_copy(lg[:, bass.ds(j * (2 * G) + u * G, G), :],
                                      psl[u][:, 0:G * E1].rearrange("p (t e) -> p t e", e=E1)).then_inc(lg_kept, 1)

            nc.vector.memset(onesf[:, :], 1.0).then_inc(order, 1)

            def wide(a):
                return a.unsqueeze(2).broadcast_to([P, PT, E1])

            def flat(a):
                return a.unsqueeze(1).broadcast_to([P, PT, E1])

            o = Order(100, 0)
            o.next()
            for c in range(PARTS):
                first = c * GROUPS // PARTS // 2

                def step(j, u):
                    normalize(j, u)
                    if not (isinstance(j, int) and j == first and u == 0):
                        keep_logits(j if u else j - 1, 1 - u)
                groups(dve, step, c)
                keep_logits((c + 1) * GROUPS // PARTS // 2 - 1, 1)
                dve.wait_ge(lg_kept, (c + 1) * GROUPS // PARTS)

                part = slice(c * PT, (c + 1) * PT)
                lg_, ex_, one_, tot_ = (a[:, part, :] for a in (lg, ex, one, tot))
                mx_, sm_, esel_, rank_, keep_, slot_ = (a[:, part] for a in (mx, sm, esel, rank, keep, slot))
                gate_ = m.gate[:, part]

                def ordered(i):
                    i.then_inc(order, 1)
                    dve.wait_ge(order, o.next())

                ordered(nc.vector.tensor_reduce(mx_, lg_, AX.X, ALU.max))
                nc.vector.tensor_tensor(lg_, lg_, wide(mx_), ALU.subtract).then_inc(less, 1)
                dve.wait_ge(exped, c + 1)
                ordered(nc.vector.tensor_reduce(mx_, ex_, AX.X, ALU.max))
                ordered(nc.vector.tensor_tensor(one_, ex_, wide(mx_), ALU.is_equal))
                ordered(nc.vector.tensor_tensor(one_, one_, flat(m.prior[:, :]), ALU.mult))
                ordered(nc.vector.tensor_reduce(sm_, one_, AX.X, ALU.max))
                ordered(nc.vector.tensor_tensor(one_, one_, wide(sm_), ALU.is_equal))
                nc.vector.tensor_copy(one16[:, part, :], one_).then_inc(one_ready, 1)
                ordered(nc.vector.tensor_reduce(sm_, ex_, AX.X, ALU.add))
                ordered(nc.vector.reciprocal(sm_, sm_))
                ordered(nc.vector.tensor_tensor(gate_, mx_, sm_, ALU.mult))
                ordered(nc.vector.tensor_tensor(lg_, one_, flat(m.prior[:, :]), ALU.mult))
                ordered(nc.vector.tensor_reduce(esel_, lg_, AX.X, ALU.add))
                ordered(nc.vector.tensor_scalar(esel_, esel_, float(-CAP), float(E1 * CAP), ALU.mult, ALU.add))
                dve.wait_ge(counted, c + 1)
                ordered(nc.vector.tensor_copy(tot_.rearrange("p n e -> p (n e)"), ps_tot[c][:, 0:PT * E1]))
                for e in range(E1):
                    start = inc[c - 1][:, e, PT - 1:PT] if c else 0.0
                    i = nc.vector.tensor_tensor_scan(inc[c][:, e, :], onesf[:, :], tot_[:, :, e], start,
                                                     ALU.mult, ALU.add)
                ordered(i)
                by_tile = inc[c][:, :, :].rearrange("p e n -> p n e")
                ordered(nc.vector.tensor_tensor(tot_, by_tile, tot_, ALU.subtract))
                ordered(nc.vector.tensor_tensor(tot_, tot_, ps_pre[c][:, 0:PT * E1].rearrange("p (n e) -> p n e", e=E1),
                                                ALU.add))
                ordered(nc.vector.tensor_tensor(tot_, tot_, one_, ALU.mult))
                ordered(nc.vector.tensor_reduce(rank_, tot_, AX.X, ALU.add))
                ordered(nc.vector.tensor_tensor(slot_, esel_, rank_, ALU.add))
                ordered(nc.vector.tensor_scalar(keep_, rank_, float(CAP), None, ALU.is_lt))
                ordered(nc.vector.tensor_scalar(rank_, keep_, -1.0e6, 1.0e6, ALU.mult, ALU.add))
                ordered(nc.vector.tensor_tensor(rank_, rank_, slot_, ALU.add))
                nc.vector.tensor_copy(m.to_slot[:, part], rank_).then_inc(slot_ready, 1)
                nc.vector.tensor_tensor(gate_, gate_, keep_, ALU.mult)
                ordered(nc.vector.tensor_tensor(slot_, keep_, slot_, ALU.mult))
                nc.vector.tensor_copy(m.from_slot[:, part], slot_)


def experts1(nc, m, w, out):
    S = 2 * P
    BL = CAP // S
    C = F1 // P
    R = BL
    with ExitStack() as ctx:
        sb = lambda n, s, d=f32: ctx.enter_context(nc.sbuf_tensor(f"e1_{n}", s, d))
        ps = lambda n, s, d=f32: ctx.enter_context(nc.psum_tensor(f"e1_{n}", s, d))
        new_sem = ctx.enter_context(semaphores(nc))
        sem = lambda n: new_sem(f"e1_{n}")
        w1, w2 = sb("w1", [P, 2, F1]), sb("w2", [P, 2, C, D])
        b1, b2 = sb("b1", [P, 2, C]), sb("b2", [P, 2])
        tok = sb("tok", [P, R, 2, D])
        xT = sb("xT", [P, 2, S])
        hid = sb("hid", [P, 2, C, S])
        yT = sb("yT", [P, 2, S])
        res = sb("res", [P, R, 2, D])
        turn, psy, pst = ps("turn", [P, 512]), ps("y", [P, 512]), ps("t", [P, 512])
        psh = [ps(f"h{i}", [P, 512]) for i in range(4)]
        w_in = [sem(f"w_in{u}") for u in range(2)]
        tok_in = [sem(f"tok_in{r}") for r in range(R)]
        turned, x_ready, h_ready, h_act, h_dve = (sem(x) for x in ("turned", "x_ready", "h_ready", "h_act", "h_dve"))
        y_ready, y_out, t_ready, res_ready = (sem(x) for x in ("y_ready", "y_out", "t_ready", "res_ready"))
        sent = [sem(f"sent{r}") for r in range(R)]
        stored_all = sem("stored_all")
        NG = 8
        fetched = [sem(f"fetched{n}") for n in range(NG)]
        summed, done = sem("summed"), sem("done")
        block = ctx.enter_context(nc.Block())
        slots = m.slots.rearrange("(b t p) d -> b p t d", t=2, p=P)
        outs = m.slot_out.rearrange("(b t p) d -> b p t d", t=2, p=P)

        def experts(eng, step):
            def both(j):
                for u in range(2):
                    for r in range(BL):
                        step(j, u, r)
            both(0)
            with eng.Fori(1, E1 // 2 - 1) as j:
                both(j)
            both(E1 // 2 - 1)
            for r in range(2):
                step(E1 // 2, 0, r)

        def number(j, u, r):
            return j * (2 * BL) + (u * BL + r)

        def run(stage, j, u, r, d):
            k = u * BL + r + d
            j, u, r = j + k // (2 * BL), k // BL % 2, k % BL
            if not isinstance(j, int) or 0 <= number(j, u, r) < E1 * BL:
                stage(j, u, r)

        @block.gpsimd
        def _(pool):
            pool.wait_ge(stored_all, 1)
            for n in range(NT):
                nc.gpsimd.indirect_dma_start(out=m.y[:, n, :], out_offset=None, in_=m.slot_out,
                                             in_offset=bass.IndirectOffsetOnAxis(ap=m.from_slot[:, n:n + 1], axis=0),
                                             bounds_check=SLOTS - 1, oob_is_err=False)\
                    .then_inc(fetched[n // (NT // NG)], 16)

        @block.sync
        def _(sp):
            def weights(j, u):
                e = j * 2 + u
                sp.dma_start(w1[:, u, :], w["w1"][bass.ds(e, 1), :, :].rearrange("o d h -> (o d) h")).then_inc(w_in[u], 16)
                sp.dma_start(w2[:, u, :, :], w["w2"][bass.ds(e, 1), :, :].rearrange("o (c p) d -> (o p) c d", p=P))\
                    .then_inc(w_in[u], 16)
                sp.dma_start(b1[:, u, :], w["b1"][bass.ds(e, 1), :, :].rearrange("o p c -> (o p) c")).then_inc(w_in[u], 16)
                sp.dma_start(b2[:, u:u + 1], w["b2"][bass.ds(e, 1), :, :].rearrange("o p c -> (o p) c"))\
                    .then_inc(w_in[u], 16)

            for u in range(2):
                weights(0, u)

            def fetch(j, u, r):
                i = number(j, u, r)
                if past(i - R + 1):
                    sp.wait_ge(turned, i - R + 1)
                sp.dma_start(tok[:, r, :, :], slots[bass.ds(i, 1), :, :, :].rearrange("o p t d -> (o p) t d"))\
                    .then_inc(tok_in[r], 16)

            for r in range(R - 1):
                fetch(0, 0, r)

            def step(j, u, r):
                run(fetch, j, u, r, R - 1)
                if r == 2 and not (isinstance(j, int) and not 1 <= j * 2 + u < E1 - 1):
                    sp.wait_ge(y_out, (j * 2 + u) * BL)
                    weights(j + u, 1 - u)
                run(store, j, u, r, -2)

            def store(j, u, r):
                i = number(j, u, r)
                sp.wait_ge(res_ready, i + 1)
                sp.dma_start(outs[bass.ds(i, 1), :, :, :].rearrange("o p t d -> (o p) t d"), res[:, r, :, :])\
                    .then_inc(sent[r], 16)
            experts(sp, step)
            for r in range(R):
                sp.wait_ge(sent[r], 16 * E1)
            sp.nop().then_inc(stored_all, 1)
            view = out.rearrange("b (t p) d -> p (b t) d", p=P)
            K = NT // NG
            for n in range(NG):
                sp.wait_ge(summed, (n + 1) * K)
                sp.dma_start(view[:, n * K:(n + 1) * K, :], m.x[:, n * K:(n + 1) * K, :]).then_inc(done, 16)
            sp.wait_ge(done, 16 * NG)

        @block.scalar
        def _(act):
            def take(j, u, r):
                i = number(j, u, r)
                act.wait_ge(turned, i + 1)
                if past(i - 1):
                    act.wait_ge(h_ready, (i - 1) * 2)
                nc.scalar.activation(xT[:, (u * BL + r) % 2, :], turn[:, 0:S], ACT.Copy).then_inc(x_ready, 1)

            def hidden(j, u, r):
                i = number(j, u, r)
                v = (u * BL + r) % 2
                if r == 0:
                    act.wait_ge(w_in[u], (j + 1) * 64)
                act.wait_ge(h_ready, i * 2 + 1)
                if past(i - 1):
                    act.wait_ge(y_ready, i - 1)
                for c in (0, 1):
                    k = nc.scalar.activation(hid[:, v, c, :], psh[2 * v][:, c * S:(c + 1) * S], ACT.Relu,
                                             bias=b1[:, u, c:c + 1])
                k.then_inc(h_act, 1)

            def keep_outputs(j, u, r):
                i = number(j, u, r)
                v = (u * BL + r) % 2
                act.wait_ge(y_ready, i + 1)
                if past(i - 1):
                    act.wait_ge(t_ready, i - 1)
                nc.scalar.activation(yT[:, v, :], psy[:, 0:S], ACT.Identity, bias=b2[:, u:u + 1])\
                    .then_inc(y_out, 1)

            take(0, 0, 0)

            def step(j, u, r):
                run(hidden, j, u, r, 0)
                run(take, j, u, r, 1)
                run(keep_outputs, j, u, r, -1)
            experts(act, step)

        @block.vector
        def _(dve):
            def give(j, u, r):
                i = number(j, u, r)
                dve.wait_ge(t_ready, i + 1)
                if not (isinstance(j, int) and j * 2 + u < 1):
                    dve.wait_ge(sent[r], (j * 2 + u) * 16)
                nc.vector.tensor_copy(res[:, r, :, :], pst[:, 0:S].rearrange("p (t d) -> p t d", t=2)).then_inc(res_ready, 1)

            def hidden(j, u, r):
                i = number(j, u, r)
                v = (u * BL + r) % 2
                if r == 0:
                    dve.wait_ge(w_in[u], (j + 1) * 64)
                dve.wait_ge(h_ready, i * 2 + 2)
                if past(i - 1):
                    dve.wait_ge(y_ready, i - 1)
                for c in (2, 3):
                    k = nc.vector.tensor_scalar(hid[:, v, c, :], psh[2 * v + 1][:, (c - 2) * S:(c - 1) * S],
                                                b1[:, u, c:c + 1], 0.0, ALU.add, ALU.max)
                k.then_inc(h_dve, 1)

            def step(j, u, r):
                run(hidden, j, u, r, 0)
                run(give, j, u, r, -2)
            experts(dve, step)

            for n in range(NT):
                if n % (NT // NG) == 0:
                    dve.wait_ge(fetched[n // (NT // NG)], 16 * (NT // NG))
                nc.vector.scalar_tensor_tensor(out=m.x[:, n, :], in0=m.y[:, n, :], scalar=m.gate[:, n:n + 1],
                                               in1=m.x[:, n, :], op0=ALU.mult, op1=ALU.add).then_inc(summed, 1)

        @block.tensor
        def _(pe):
            def turns(j, u, r):
                i = number(j, u, r)
                pe.wait_ge(tok_in[r], (j * 2 + u + 1) * 16)
                if past(i):
                    pe.wait_ge(x_ready, i)
                for t in range(2):
                    k = nc.tensor.transpose(turn[:, t * P:(t + 1) * P], tok[:, r, t, :], m.ident[:, :])
                k.then_inc(turned, 1)

            def hidden(j, u, r):
                i = number(j, u, r)
                v = (u * BL + r) % 2
                if r == 0:
                    pe.wait_ge(w_in[u], (j + 1) * 64)
                pe.wait_ge(x_ready, i + 1)
                for c in range(C):
                    if c % 2 == 0 and past(i - 1):
                        pe.wait_ge(h_dve if c else h_act, i - 1)
                    k = nc.tensor.matmul(psh[2 * v + c // 2][:, (c % 2) * S:(c % 2 + 1) * S],
                                         w1[:, u, c * P:(c + 1) * P], xT[:, v, :], start=True, stop=True)
                    if c % 2:
                        k.then_inc(h_ready, 1)

            def outputs(j, u, r):
                i = number(j, u, r)
                v = (u * BL + r) % 2
                pe.wait_ge(h_act, i + 1)
                if past(i):
                    pe.wait_ge(y_out, i)
                for c in range(C):
                    if c == 2:
                        pe.wait_ge(h_dve, i + 1)
                    k = nc.tensor.matmul(psy[:, 0:S], w2[:, u, c, :], hid[:, v, c, :], start=c == 0, stop=c == C - 1)
                k.then_inc(y_ready, 1)

            def turn_outputs(j, u, r):
                i = number(j, u, r)
                v = (u * BL + r) % 2
                pe.wait_ge(y_out, i + 1)
                if past(i):
                    pe.wait_ge(res_ready, i)
                for t in range(2):
                    k = nc.tensor.transpose(pst[:, t * P:(t + 1) * P], yT[:, v, t * P:(t + 1) * P], m.ident[:, :])
                k.then_inc(t_ready, 1)

            turns(0, 0, 0)

            def step(j, u, r):
                run(hidden, j, u, r, 0)
                run(turn_outputs, j, u, r, -2)
                run(turns, j, u, r, 1)
                run(outputs, j, u, r, -1)
            experts(pe, step)


class Kept:
    pass


def two_layers(nc, x, a, out):
    with ExitStack() as ctx:
        m = Kept()
        sb = lambda n, s, d=f32: ctx.enter_context(nc.sbuf_tensor(f"kept_{n}", s, d))
        dram = lambda n, s, d=f32: nc.dram_tensor(n, s, d, kind="Internal").ap()
        m.x, m.y = sb("x", [P, NT, D]), sb("y", [P, NT, D])
        m.lat = sb("lat", [P, NT, LAT])
        m.x_stat, m.x_rstd = sb("x_stat", [P, NT, 2]), sb("x_rstd", [P, NT])
        m.moments = sb("moments", [P, NT, 6])
        m.lat_stat, m.lat_rstd = sb("lat_stat", [P, NT, 2]), sb("lat_rstd", [P, NT])
        m.y_stat, m.y_rms = sb("y_stat", [P, NT, 2]), sb("y_rms", [P, NT])
        m.qst, m.kst = sb("qst", [P, 4, UP, T], bf16), sb("kst", [P, 4, 2, UP, T], bf16)
        m.ident, m.ident16 = sb("ident", [P, P]), sb("ident16", [P, P], bf16)
        m.mask_qk, m.mask_kq = sb("mask_qk", [P, 2, P], bf16), sb("mask_kq", [P, P], bf16)
        m.before, m.ones16 = sb("before", [P, P], bf16), sb("ones16", [P, P], bf16)
        m.zero = sb("zero", [P, 2 * UP * T], bf16)
        m.prior = sb("prior", [P, E1])
        m.proj_bias = sb("proj_bias", [P, D])
        m.out_bias = sb("out_bias", [P, D])
        m.gate = sb("gate", [P, NT])
        m.to_slot, m.from_slot = sb("to_slot", [P, NT], u32), sb("from_slot", [P, NT], u32)
        m.q_dram = dram("q_stacks", (B, 6, HD, 2, PAIRS, T), bf16)
        m.k_dram = dram("k_stacks", (B, 6, HD, 2, PAIRS, T), bf16)
        m.v_dram = dram("v_rows", (B, P, TT, H * VW))
        m.slots, m.slot_out = dram("slots", (SLOTS, D)), dram("slot_out", (SLOTS, D))
        m.serial = 0

        with ExitStack() as c:
            sem = c.enter_context(semaphores(nc))
            PIECES = 8
            x_in = [sem(f"x_in{n}") for n in range(PIECES)]
            bias_in, filled, made, zeroed, slots_zero = (sem(n) for n in ("bias_in", "filled", "made", "zeroed",
                                                                          "slots_zero"))
            block = c.enter_context(nc.Block())

            @block.sync
            def _(sp):
                view = x.rearrange("b (t p) d -> p (b t) d", p=P)
                K = NT // PIECES
                for n in range(PIECES):
                    sp.dma_start(m.x[:, n * K:(n + 1) * K, :], view[:, n * K:(n + 1) * K, :]).then_inc(x_in[n], 16)
                sp.dma_start(m.proj_bias[:, :], a["L1_attn_bproj"].partition_broadcast(P)).then_inc(bias_in, 16)
                sp.dma_start(m.out_bias[:, :], a["L0_attn_out_b"].partition_broadcast(P)).then_inc(bias_in, 16)
                sp.wait_ge(zeroed, 1)
                K = 2 * UP * T // 2 // D
                zero = m.zero[:, :].bitcast(f32)
                n_rows = P * K
                for n in range(SLOTS // n_rows):
                    sp.dma_start(m.slots[n * n_rows:(n + 1) * n_rows, :].rearrange("(p k) d -> p (k d)", k=K),
                                 zero).then_inc(slots_zero, 16)
                sp.wait_ge(bias_in, 32)
                sp.wait_ge(slots_zero, 16 * (SLOTS // n_rows))

            @block.vector
            def _(dve):
                nc.vector.memset(m.zero[:, :], 0.0).then_inc(zeroed, 1)
                nc.vector.memset(m.ones16[:, :], 1.0)
                for n in range(PIECES):
                    dve.wait_ge(x_in[n], 16)
                    take_moments(nc, m, m.x, n * (NT // PIECES), NT // PIECES)

            @block.gpsimd
            def _(pool):
                p = nc.gpsimd
                n = 0

                def fill(tile, value):
                    p.memset(tile, value).then_inc(filled, 1)

                kst = m.kst[:, :, :, :, :]
                fill(m.ident[:, :], 0.0)
                fill(m.ident16[:, :], 0.0)
                fill(m.mask_qk[:, :, :], 0.0)
                fill(m.mask_kq[:, :], 0.0)
                fill(m.before[:, :], 1.0)
                fill(kst, 0.0)
                for e in range(E1):
                    fill(m.prior[:, e:e + 1], float(E1 - e))
                pool.wait_ge(filled, 6 + E1)
                for t in (m.ident, m.ident16):
                    p.affine_select(out=t[:, :], in_=t[:, :], compare_op=ALU.not_equal, fill=1.0, base=0,
                                    pattern=[[-1, P]], channel_multiplier=1)
                p.affine_select(out=m.mask_qk[:, :, :], in_=m.mask_qk[:, :, :], compare_op=ALU.is_ge, fill=MASKED,
                                base=0, pattern=[[0, 2], [-1, P]], channel_multiplier=1)
                p.affine_select(out=m.mask_kq[:, :], in_=m.mask_kq[:, :], compare_op=ALU.is_ge, fill=MASKED,
                                base=0, pattern=[[1, P]], channel_multiplier=-1)
                p.affine_select(out=m.before[:, :], in_=m.before[:, :], compare_op=ALU.is_gt, fill=0.0,
                                base=0, pattern=[[1, P]], channel_multiplier=-1)
                for x_ in range(2):
                    for r in range(2):
                        part = m.kst[:, :, x_, :, :].rearrange("p k q t -> p k (q t)")
                        n += 1
                        p.affine_select(out=part, in_=part, compare_op=ALU.not_equal, fill=1.0,
                                        base=-(ROWS + 2 * x_ + r), pattern=[[0, 4], [0, UP * T]],
                                        channel_multiplier=1).then_inc(made, 1)
                        pool.wait_ge(made, n)

        layer_stats(nc, "first", m, D, m.x_stat, m.x_rstd, 1e-5)
        m.serial = 1
        project(nc, "plain", m, dict(watt=a["watt"], wvT=a["wvT"], bv=a["L0_attn_wv_b"]))
        attend(nc, "plain", m, dict(woT=a["outT"]))
        layer_stats(nc, "second", m, D, m.x_stat, m.x_rstd, 1e-5)
        project(nc, "queries", m, dict(cos=a["cos"], sin=a["sin"], wqT=a["wqT"], wqrT=a["wqrT"], wdT=a["wdkvT"],
                                       n1=a["n1"]))
        layer_stats(nc, "latent", m, LAT, m.lat_stat, m.lat_rstd, 1e-5)
        project(nc, "keys", m, dict(cos=a["cos"], sin=a["sin"], wkT=a["wukT"], wkrT=a["wukrT"], wvT0=a["wuvT"],
                                    lg=a["ln_g"], lb=a["ln_b"]))
        m.serial = 2
        attend(nc, "causal", m, dict(woT=a["woT"]))
        layer_stats(nc, "third", m, D, m.y_stat, m.y_rms, 1e-6, second_moment=True)
        experts0(nc, m, dict(w1=a["w1T"], w2=a["w2T"], b1=a["b1T"], b2=a["b2T"], gw=a["gwT"], gb=a["L0_ffn_gate_b"],
                             n2=a["n2"]))
        layer_stats(nc, "fourth", m, D, m.x_stat, m.x_rstd, 1e-5)
        project(nc, "cosine", m, dict(wqkv=a["L1_attn_Wqkv"], qs=a["q_scale"], ks=a["k_scale"]))
        m.serial = 3
        attend(nc, "plain", m, dict(woT=a["L1_attn_Wproj"]))
        layer_stats(nc, "fifth", m, D, m.x_stat, m.x_rstd, 1e-5)
        route1(nc, m, dict(gw=a["gate1T"]))
        experts1(nc, m, dict(w1=a["L1_ffn_w1"], w2=a["L1_ffn_w2"], b1=a["b11T"], b2=a["b21T"]), out)


def rope_tables():
    half = HD // 2
    inv = (np.float32(1.0) / np.float32(10000.0) ** (np.arange(half, dtype=np.float32) / np.float32(half)))
    ang = np.arange(T, dtype=np.float32)[:, None] * inv[None, :].astype(np.float32)
    sin, cos = np.sin(ang).T, np.cos(ang).T
    return (np.ascontiguousarray(np.tile(np.concatenate([cos, cos]), (H, 1)), np.float32),
            np.ascontiguousarray(np.tile(np.concatenate([-sin, sin]), (H, 1)), np.float32))


def kernel(**inputs):
    import concourse.bacc as bacc
    from concourse.bass_utils import run_bass_kernel_spmd as run

    i = {k: np.asarray(v) for k, v in inputs.items()}
    swap = np.arange(D).reshape(H, 2, HD // 2)[:, ::-1].reshape(D)
    order = np.arange(D).reshape(PAIRS, 2, HD).transpose(2, 1, 0).reshape(D)
    cos, sin = (t[order] for t in rope_tables())
    blocks = np.zeros((D, D), np.float32)
    for h in range(H):
        blocks[HD * h:HD * h + HD, HD * h:HD * h + HD] = i["L0_attn_w_att_val"][h]
    wqkv = np.concatenate([i["L1_attn_Wqkv"][:, :D][:, order], i["L1_attn_Wqkv"][:, D:2 * D][:, order],
                           i["L1_attn_Wqkv"][:, 2 * D:]], 1)
    arrays = {
        "watt": blocks[order][:, order],
        "wvT": i["L0_attn_wv_w"].T[order], "L0_attn_wv_b": i["L0_attn_wv_b"],
        "outT": i["L0_attn_out_w"].T, "L0_attn_out_b": i["L0_attn_out_b"],
        "cos": cos, "sin": sin,
        "wqT": i["L0_ffn_Wq"].T[:, order], "wqrT": i["L0_ffn_Wq"][swap].T[:, order], "wdkvT": i["L0_ffn_Wdkv"].T,
        "wukT": i["L0_ffn_Wuk"].T[:, order], "wukrT": i["L0_ffn_Wuk"][swap].T[:, order], "wuvT": i["L0_ffn_Wuv"].T,
        "woT": i["L0_ffn_Wo"].T,
        "n1": i["L0_ffn_norm1_w"].reshape(D, 1), "n2": i["L0_ffn_norm2_w"].reshape(D, 1),
        "ln_g": i["L0_ffn_ln_g"].reshape(LAT, 1), "ln_b": i["L0_ffn_ln_b"].reshape(LAT, 1),
        "gwT": i["L0_ffn_gate_w"].T, "L0_ffn_gate_b": i["L0_ffn_gate_b"],
        "w1T": i["L0_ffn_W1"].transpose(2, 0, 1),
        "b1T": i["L0_ffn_b1"].reshape(E0, F0 // P, P).transpose(2, 0, 1),
        "w2T": i["L0_ffn_W2"].reshape(E0, D, F0 // P, P).transpose(3, 0, 2, 1),
        "b2T": i["L0_ffn_b2"].T,
        "L1_attn_Wqkv": wqkv, "L1_attn_Wproj": i["L1_attn_Wproj"], "L1_attn_bproj": i["L1_attn_bproj"],
        "q_scale": i["L1_attn_q_scale"][order % HD].reshape(D, 1), "k_scale": i["L1_attn_k_scale"][order % HD].reshape(D, 1),
        "gate1T": i["L1_ffn_gate_w"].T,
        "L1_ffn_w1": i["L1_ffn_w1"], "L1_ffn_w2": i["L1_ffn_w2"],
        "b11T": i["L1_ffn_b1"].reshape(E1, F1 // P, P).transpose(0, 2, 1),
        "b21T": i["L1_ffn_b2"].reshape(E1, D, 1),
    }
    nc = bacc.Bacc("TRN2", target_bir_lowering=False, num_devices=1)
    feeds, aps = {"x": np.ascontiguousarray(i["L0_attn_x"])}, {}
    x = nc.dram_tensor("x", (B, T, D), f32, kind="ExternalInput").ap()
    for name, v in arrays.items():
        feeds["w_" + name] = np.ascontiguousarray(v)
        aps[name] = nc.dram_tensor("w_" + name, v.shape, f32, kind="ExternalInput").ap()
    out = nc.dram_tensor("out", (B, T, D), f32, kind="ExternalOutput").ap()
    two_layers(nc, x, aps, out)
    r = run(nc, [feeds], core_ids=[0])
    return r.results[0]["out"]
```

```python
from contextlib import ExitStack, contextmanager

import numpy as np

import concourse.bass as bass
import concourse.mybir as mybir

f32 = mybir.dt.float32
bf16 = mybir.dt.bfloat16
u32 = mybir.dt.uint32
ALU = mybir.AluOpType
ACT = mybir.ActivationFunctionType
AX = mybir.AxisListType

B, T, D = 32, 256, 128
P = 128
H, HD = 16, 8
NT = B * T // P
TT = T // P
PAIRS = H // 2
ROWS = 6 * 2 * HD
VW = HD + 1
UNITS = 2 * B
UP = PAIRS // 2
LAT = 64
E0, F0 = 4, 512
E1, F1 = 8, 512
CAP = 1280
SLOTS = E1 * CAP
GATE, NUMBER = 2 * D, 2 * D + 1
ROW = 2 * D + 2
NO_TOKEN = 1 << 20
SCALE = float(HD) ** -0.5
MASKED = -1.0e30


@contextmanager
def semaphores(nc):
    taken = []

    def sem(name):
        taken.append(nc.alloc_semaphore(name))
        return taken[-1]

    yield sem
    nc.clear_and_free_semaphores(taken)
    nc.all_engine_barrier()


class Order:

    def __init__(self, per, round_):
        self.per, self.round, self.k = per, round_, 0

    def next(self):
        self.k += 1
        assert self.k <= self.per
        return self.round * self.per + self.k


def past(n):
    return not (isinstance(n, int) and n <= 0)


def take_moments(nc, m, src, n0, count):
    for t in range(count):
        i = nc.vector.bn_stats(m.moments[:, bass.ds(n0 + t, 1), :].rearrange("p o d -> p (o d)"),
                               src[:, bass.ds(n0 + t, 1), :].rearrange("p o d -> p (o d)"))
    return i


def layer_stats(nc, name, m, W, stat, rstd, eps, second_moment=False):
    with ExitStack() as ctx:
        sem = ctx.enter_context(semaphores(nc))
        sb = lambda n, s: ctx.enter_context(nc.sbuf_tensor(f"{name}_{n}", s, f32))
        parts, root, apart = m.moments, sb("root", [P, NT]), sb("apart", [P, NT])
        order, shifted, rooted = (sem(f"{name}_{x}") for x in ("order", "shifted", "rooted"))
        block = ctx.enter_context(nc.Block())

        @block.vector
        def _(dve):
            mean, var = stat[:, :, 0], stat[:, :, 1]
            nc.vector.tensor_tensor(apart[:, :], parts[:, :, 1], parts[:, :, 4], ALU.subtract).then_inc(order, 1)
            nc.vector.tensor_tensor(mean, parts[:, :, 1], parts[:, :, 4], ALU.add).then_inc(order, 1)
            nc.vector.tensor_tensor(var, parts[:, :, 2], parts[:, :, 5], ALU.add).then_inc(order, 1)
            dve.wait_ge(order, 3)
            nc.vector.tensor_scalar(mean, mean, 0.5, None, ALU.mult).then_inc(order, 1)
            nc.vector.tensor_scalar(var, var, 1.0 / W, None, ALU.mult).then_inc(order, 1)
            nc.vector.scalar_tensor_tensor(out=apart[:, :], in0=apart[:, :], scalar=0.25, in1=apart[:, :],
                                           op0=ALU.mult, op1=ALU.mult).then_inc(order, 1)
            dve.wait_ge(order, 6)
            nc.vector.tensor_tensor(var, var, apart[:, :], ALU.add).then_inc(order, 1)
            dve.wait_ge(order, 7)
            if second_moment:
                nc.vector.tensor_tensor(root[:, :], mean, mean, ALU.mult).then_inc(order, 1)
                dve.wait_ge(order, 8)
                nc.vector.tensor_tensor(root[:, :], root[:, :], var, ALU.add).then_inc(order, 1)
                dve.wait_ge(order, 9)
                nc.vector.tensor_scalar(root[:, :], root[:, :], eps, None, ALU.add).then_inc(shifted, 1)
            else:
                nc.vector.tensor_scalar(root[:, :], var, eps, None, ALU.add).then_inc(shifted, 1)
            dve.wait_ge(rooted, 1)
            nc.vector.reciprocal(rstd[:, :], root[:, :])

        @block.scalar
        def _(act):
            act.wait_ge(shifted, 1)
            nc.scalar.activation(root[:, :], root[:, :], ACT.Sqrt).then_inc(rooted, 1)


def project(nc, kind, m, w):
    plain, cosine, queries, keys = (kind == k for k in ("plain", "cosine", "queries", "keys"))
    rope = queries or keys
    W = LAT if keys else D
    NQ = 1 if rope else 2
    has_v = not queries
    LAG = 2 if cosine else 1
    RING = 4
    with ExitStack() as ctx:
        sb = lambda n, s, d=f32: ctx.enter_context(nc.sbuf_tensor(f"{kind}_{n}", s, d))
        ps = lambda n, s, d=f32: ctx.enter_context(nc.psum_tensor(f"{kind}_{n}", s, d))
        new_sem = ctx.enter_context(semaphores(nc))
        sem = lambda n: new_sem(f"{kind}_{n}")
        src, stat, rstd = (m.lat, m.lat_stat, m.lat_rstd) if keys else (m.x, m.x_stat, m.x_rstd)
        xn = sb("xn", [P, 2, TT, W])
        qk = sb("qk", [P, RING, NQ, T])
        if plain:
            xT = [qk[:, u, 1, :] for u in range(RING)]
        else:
            x_turned = sb("xT", [W, 2, T])
            xT = [x_turned[:, u % 2, :] for u in range(RING)]
        rest = sb("rest", [P, 2, NQ, T])
        parts = sb("parts", [P, RING, NQ, 3, T], bf16)
        if has_v:
            vt = sb("vt", [P, RING, TT, H, VW])
            v_ready, v_taken = sem("v_ready"), sem("v_taken")
        turn = [ps(f"turn{u}", [P, 512]) for u in range(2)]
        weights_in, cleared = sem("weights_in"), sem("cleared")
        normed = sem("normed")
        turned = sem("turned")
        x_ready = sem("x_ready")
        q_ready = sem("q_ready")
        qk_ready = sem("qk_ready")
        high, left, middle, low = sem("high"), sem("left"), sem("middle"), sem("low")
        stored = [sem(f"stored{u}") for u in range(RING)]
        Q_COPIES = ((0, 3, 0, True), (3, 2, 1, True))
        COPIES = (Q_COPIES + ((5, 1, 2, False),) if queries else
                  ((6, 3, 0, False), (9, 2, 0, False), (11, 1, 0, False)) if keys else
                  Q_COPIES + ((5, 4, 2, False), (9, 2, 3, False), (11, 1, 3, False)))
        STORES = len(COPIES) + has_v
        ordered = sem("ordered")

        if plain or rope:
            wq = sb("wq", [W, D])
        if plain or keys:
            wv = sb("wv", [W, D])
            pv = ps("pv", [P, 512])
        if plain:
            pq = ps("pq", [P, 512])
            bv = sb("bv", [P, D])
            q_copied = sem("q_copied")
            loads = [(wq[:, :], w["watt"]), (wv[:, :], w["wvT"]), (bv[:, :], w["bv"].partition_broadcast(P))]
        if cosine:
            wqkv = sb("wqkv", [P, 3 * D])
            qkscale = sb("qkscale", [P, 2])
            square = sb("square", [P, 2, TT, 2 * D])
            norm = sb("norm", [P, 2, TT, 2, H])
            unit = sb("unit", [P, 2, TT, 2 * D])
            pqkv = [[ps(f"qkv{u}{t}", [P, 512]) for t in range(TT)] for u in range(2)]
            pturn = ps("pturn", [P, 512])
            squared, summed, rooted, shifted, inverted, unit_ready, unit_turned = (sem(x) for x in (
                "squared", "summed", "rooted", "shifted", "inverted", "unit_ready", "unit_turned"))
            loads = [(wqkv[:, :], w["wqkv"])] + [(qkscale[:, n:n + 1], w[x]) for n, x in enumerate(("qs", "ks"))]
        if rope:
            pq, pq2 = [ps(f"pq{u}", [P, 512]) for u in range(2)], [ps(f"pqr{u}", [P, 512]) for u in range(2)]
            wq2 = sb("wq2", [W, D])
            gain = sb("gain", [W, 1])
            cos_t, sin_t = sb("cos", [P, T]), sb("sin", [P, T])
            a1, a2 = sb("a1", [P, 2, T]), sb("a2", [P, 2, T])
            multiplied = sem("multiplied")
            loads = [(cos_t[:, :], w["cos"]), (sin_t[:, :], w["sin"])]
        if queries:
            rr = sb("rr", [P, NT])
            wd = sb("wd", [P, LAT])
            pl = ps("pl", [P, 512])
            lat_made, lat_kept = sem("lat_made"), sem("lat_kept")
            r_made, r_root = sem("r_made"), sem("r_root")
            loads += [(wq[:, :], w["wqT"]), (wq2[:, :], w["wqrT"]), (wd[:, :], w["wdT"]), (gain[:, :], w["n1"])]
        if keys:
            shift = sb("shift", [W, 1])
            loads += [(wq[:, :], w["wkT"]), (wq2[:, :], w["wkrT"]), (wv[:, :], w["wvT0"]),
                      (gain[:, :], w["lg"]), (shift[:, :], w["lb"])]
        N_LOADS = len(loads)
        block = ctx.enter_context(nc.Block())

        def steps(eng, step):
            for u in range(RING):
                step(0, u)
            with eng.Fori(1, B // RING - 1) as j:
                for u in range(RING):
                    step(j, u)
            for n in range(B - RING, B + LAG):
                step(n // RING, n % RING)

        def run(stage, j, u, d):
            j, u = j + (u + d) // RING, (u + d) % RING
            if not isinstance(j, int) or 0 <= j * RING + u < B:
                stage(j, u)

        @block.sync
        def _(sp):
            for dst, s in loads:
                sp.dma_start(dst, s).then_inc(weights_in, 16)

            def store(j, u):
                b = j * RING + u
                if has_v:
                    sp.wait_ge(v_taken, b + 1)
                    sp.dma_start(m.v_dram[bass.ds(b, 1), :, :, :].rearrange("o p t c -> (o p) t c"),
                                 vt[:, u, :, :, :].rearrange("p t h c -> p t (h c)")).then_inc(stored[u], 16)
                sp.wait_ge(low, b + 1)
                all_parts = parts[:, u, :, :, :].rearrange("p n k t -> p (n k) t")
                for row, count, part, repeated in COPIES:
                    dst = m.qk_dram[bass.ds(b, 1), row:row + count, :, :, :, :]\
                        .rearrange("o r d x p t -> (o d x p) r t")
                    some = (all_parts[:, part:part + 1, :].broadcast_to([P, count, T]) if repeated else
                            all_parts[:, part:part + count, :])
                    sp.dma_start(dst, some).then_inc(stored[u], 16)

            steps(sp, lambda j, u: run(store, j, u, -LAG))
            for u in range(RING):
                sp.wait_ge(stored[u], STORES * 16 * (B // RING))

        @block.gpsimd
        def _(pool):
            if has_v:
                for u in range(RING):
                    nc.gpsimd.memset(vt[:, u, :, :, :], 1.0).then_inc(cleared, 1)

            def rotated(j, u):
                b = j * RING + u
                if past(b - RING + 1):
                    pool.wait_ge(left, b - RING + 1)
                pool.wait_ge(multiplied, b * 2 + 2)
                nc.gpsimd.tensor_tensor(qk[:, u, 0, :], a1[:, u % 2, :], a2[:, u % 2, :], ALU.add).then_inc(qk_ready, 1)

            def add_bias(j, u):
                pool.wait_ge(normed, (j * RING + u) * TT + TT)
                two = m.x[:, bass.ds(j * (RING * TT) + u * TT, TT), :]
                bias = (m.out_bias if plain else m.proj_bias)[:, :]
                nc.gpsimd.tensor_tensor(two, two, bias.unsqueeze(1).broadcast_to([P, TT, D]), ALU.add)

            def lowest(j, u):
                b = j * RING + u
                pool.wait_ge(middle, b + 1)
                nc.gpsimd.tensor_tensor(parts[:, u, :, 2, :], rest[:, u % 2, :, :], parts[:, u, :, 1, :],
                                        ALU.subtract).then_inc(low, 1)

            def step(j, u):
                if rope:
                    run(rotated, j, u, 0)
                else:
                    run(add_bias, j, u, 0)
                run(lowest, j, u, -LAG)
            steps(pool, step)

        @block.vector
        def _(dve):
            if queries:
                nc.vector.tensor_tensor(rr[:, :], rstd[:, :], rstd[:, :], ALU.mult).then_inc(r_made, 1)
                dve.wait_ge(r_made, 1)
                nc.vector.tensor_tensor(rr[:, :], rr[:, :], stat[:, :, 1], ALU.mult).then_inc(r_made, 1)
                dve.wait_ge(r_made, 2)
                nc.vector.tensor_scalar(rr[:, :], rr[:, :], 1e-6, None, ALU.add).then_inc(r_made, 1)
                dve.wait_ge(r_root, 1)
                nc.vector.reciprocal(rr[:, :], rr[:, :]).then_inc(r_made, 1)
                dve.wait_ge(r_made, 4)

            def row_of(a, n):
                return a[:, bass.ds(n, 1), :].rearrange("p o d -> p (o d)")

            def normalize(j, u):
                b = j * RING + u
                n0 = j * (RING * TT) + u * TT
                if past(b - 1):
                    dve.wait_ge(turned, b - 1)
                for t in range(TT):
                    n = n0 + t
                    mean, inv = stat[:, bass.ds(n, 1), 0], rstd[:, bass.ds(n, 1)]
                    dst, row = row_of(m.y, n) if queries else xn[:, u % 2, t, :], row_of(src, n)
                    if plain:
                        dst = dst.rearrange("p (d x q) -> p d x q", x=2, d=HD)
                        row = row.rearrange("p (q x d) -> p d x q", x=2, d=HD)
                    nc.vector.tensor_scalar(dst, row, mean, inv, ALU.subtract, ALU.mult)\
                        .then_inc(ordered if queries else normed, 1)
                if queries:
                    for t in range(TT):
                        n = n0 + t
                        dve.wait_ge(ordered, b * TT + t + 1)
                        nc.vector.tensor_scalar(xn[:, u % 2, t, :], row_of(m.y, n), rr[:, bass.ds(n, 1)], None, ALU.mult)\
                            .then_inc(normed, 1)

            def multiplied_rope(j, u):
                b = j * RING + u
                if past(b - 1):
                    dve.wait_ge(qk_ready, b - 1)
                dve.wait_ge(q_ready, b + 1)
                nc.vector.tensor_tensor(a1[:, u % 2, :], pq[u % 2][:, 0:T], cos_t[:, :], ALU.mult).then_inc(multiplied, 1)
                nc.vector.tensor_tensor(a2[:, u % 2, :], pq2[u % 2][:, 0:T], sin_t[:, :], ALU.mult).then_inc(multiplied, 1)

            def keep_latent(j, u):
                dve.wait_ge(lat_made, j * RING + u + 1)
                n0 = j * (RING * TT) + u * TT
                nc.vector.tensor_copy(m.lat[:, bass.ds(n0, TT), :],
                                      pl[:, 0:TT * LAT].rearrange("p (t c) -> p t c", t=TT))
                for t in range(TT):
                    i = nc.vector.bn_stats(m.moments[:, bass.ds(n0 + t, 1), :].rearrange("p o d -> p (o d)"),
                                           pl[:, t * LAT:(t + 1) * LAT])
                i.then_inc(lat_kept, 1)

            def take_v(j, u):
                dve.wait_ge(v_ready, j * RING + u + 1)
                if past(j):
                    dve.wait_ge(stored[u], j * (STORES * 16))
                for t in range(TT):
                    v = pv[:, t * D:(t + 1) * D].rearrange("p (h c) -> p h c", h=H)
                    if plain:
                        i = nc.vector.tensor_tensor(vt[:, u, t, :, 0:HD], v, bv[:, :].rearrange("p (h c) -> p h c", h=H),
                                                    ALU.add)
                    else:
                        i = nc.vector.tensor_copy(vt[:, u, t, :, 0:HD], v)
                i.then_inc(v_taken, 1)

            def sum_squares(j, u):
                b = j * RING + u
                dve.wait_ge(squared, b + 1)
                if past(b - 1):
                    dve.wait_ge(unit_ready, (b - 1) * TT)
                nc.vector.tensor_reduce(norm[:, u % 2, :, :, :].rearrange("p t n h -> p (t n) h"),
                                        square[:, u % 2, :, :].rearrange("p t (n d g) -> p (t n) g d", n=2, d=HD),
                                        AX.X, ALU.add).then_inc(summed, 1)

            def to_unit(j, u):
                b = j * RING + u
                nn = norm[:, u % 2, :, :, :].rearrange("p t n h -> p (t n h)")
                dve.wait_ge(rooted, b + 1)
                nc.vector.tensor_scalar(nn, nn, 1e-8, None, ALU.add).then_inc(shifted, 1)
                dve.wait_ge(shifted, b + 1)
                nc.vector.reciprocal(nn, nn).then_inc(inverted, 1)
                dve.wait_ge(inverted, b + 1)
                if past(b - 1):
                    dve.wait_ge(unit_turned, b - 1)
                dve.wait_ge(v_taken, b + 1)
                for t in range(TT):
                    nc.vector.tensor_tensor(unit[:, u % 2, t, :].rearrange("p (n d g) -> p n d g", n=2, d=HD),
                                            pqkv[u % 2][t][:, 0:2 * D].rearrange("p (n d g) -> p n d g", n=2, d=HD),
                                            norm[:, u % 2, t, :, :].unsqueeze(2).broadcast_to([P, 2, HD, H]),
                                            ALU.mult).then_inc(unit_ready, 1)

            def subtract_high(j, u):
                b = j * RING + u
                dve.wait_ge(high, b + 1)
                if past(b - 1):
                    dve.wait_ge(low, b - 1)
                nc.vector.tensor_tensor(rest[:, u % 2, :, :], qk[:, u, :, :], parts[:, u, :, 0, :],
                                        ALU.subtract).then_inc(left, 1)

            dve.wait_ge(weights_in, 16 * N_LOADS)
            if plain or keys:
                dve.wait_ge(cleared, RING)
            normalize(0, 0)
            normalize(0, 1)

            def step(j, u):
                run(normalize, j, u, 2)
                if cosine:
                    run(to_unit, j, u, -1)
                if rope:
                    run(multiplied_rope, j, u, 0)
                if queries:
                    run(keep_latent, j, u, 0)
                run(subtract_high, j, u, -LAG)
                if plain or keys:
                    run(take_v, j, u, 0)
                if cosine:
                    run(sum_squares, j, u, 0)
            steps(dve, step)

        @block.tensor
        def _(pe):
            def turns(j, u):
                b = j * RING + u
                pe.wait_ge(normed, b * TT + TT)
                if past(b - 1):
                    pe.wait_ge(x_ready, b - 1)
                for t in range(TT):
                    if keys:
                        i = nc.tensor.matmul(turn[u % 2][0:W, t * P:(t + 1) * P], xn[:, u % 2, t, :], m.ident[:, :],
                                             start=True, stop=True)
                    else:
                        i = nc.tensor.transpose(turn[u % 2][0:W, t * P:(t + 1) * P], xn[:, u % 2, t, :], m.ident[:, :])
                i.then_inc(turned, 1)

            turns(0, 0)
            pe.wait_ge(weights_in, 16 * N_LOADS)

            def products(j, u):
                b = j * RING + u
                pe.wait_ge(x_ready, b + 1)
                if plain:
                    if past(b):
                        pe.wait_ge(q_copied, b)
                    nc.tensor.matmul(pq[:, 0:T], wq[:, :], xT[u], start=True, stop=True).then_inc(q_ready, 1)
                if rope:
                    if past(b - 1):
                        pe.wait_ge(multiplied, (b - 1) * 2)
                    nc.tensor.matmul(pq[u % 2][:, 0:T], wq[:, :], xT[u], start=True, stop=True)
                    nc.tensor.matmul(pq2[u % 2][:, 0:T], wq2[:, :], xT[u], start=True, stop=True).then_inc(q_ready, 1)
                if queries:
                    if past(b):
                        pe.wait_ge(lat_kept, b)
                    for t in range(TT):
                        i = nc.tensor.matmul(pl[:, t * LAT:(t + 1) * LAT], xT[u][:, t * P:(t + 1) * P], wd[:, :],
                                             start=True, stop=True)
                    i.then_inc(lat_made, 1)
                if plain or keys:
                    if past(b):
                        pe.wait_ge(v_taken, b)
                    for t in range(TT):
                        i = nc.tensor.matmul(pv[:, t * D:(t + 1) * D], xT[u][:, t * P:(t + 1) * P], wv[:, :],
                                             start=True, stop=True)
                    i.then_inc(v_ready, 1)
                if cosine:
                    if past(b - 1):
                        pe.wait_ge(unit_ready, (b - 1) * TT)
                        pe.wait_ge(v_taken, b - 1)
                    for t in range(TT):
                        i = nc.tensor.matmul(pqkv[u % 2][t][:, 0:3 * D], xT[u][:, t * P:(t + 1) * P], wqkv[:, :],
                                             start=True, stop=True)
                    i.then_inc(q_ready, 1)

            def turn_unit(j, u):
                b = j * RING + u
                pe.wait_ge(unit_ready, b * TT + TT)
                if past(b):
                    pe.wait_ge(qk_ready, b)
                for n in range(2):
                    for t in range(TT):
                        c = n * T + t * P
                        i = nc.tensor.transpose(pturn[:, c:c + P], unit[:, u % 2, t, n * D:(n + 1) * D], m.ident[:, :])
                i.then_inc(unit_turned, 1)

            def step(j, u):
                run(turns, j, u, 1)
                run(products, j, u, 0)
                if cosine:
                    run(turn_unit, j, u, -1)
            steps(pe, step)

        @block.scalar
        def _(act):
            if queries:
                act.wait_ge(r_made, 3)
                nc.scalar.activation(rr[:, :], rr[:, :], ACT.Sqrt).then_inc(r_root, 1)
            if not plain:
                act.wait_ge(weights_in, 16 * N_LOADS)

            def take(j, u):
                b = j * RING + u
                act.wait_ge(turned, b + 1)
                if plain:
                    if past(b - RING + 1):
                        act.wait_ge(v_ready, b - RING + 1)
                        act.wait_ge(left, b - RING + 1)
                elif past(b - 1):
                    act.wait_ge(lat_made if queries else q_ready if cosine else v_ready, b - 1)
                if rope:
                    nc.scalar.activation(xT[u], turn[u % 2][0:W, 0:T], ACT.Identity, scale=gain[:, :],
                                         bias=shift[:, :] if keys else 0.0).then_inc(x_ready, 1)
                else:
                    nc.scalar.activation(xT[u], turn[u % 2][0:W, 0:T], ACT.Copy).then_inc(x_ready, 1)

            def copy_q(j, u):
                b = j * RING + u
                act.wait_ge(q_ready, b + 1)
                if past(b - RING + 1):
                    act.wait_ge(left, b - RING + 1)
                nc.scalar.activation(qk[:, u, 0, :], pq[:, 0:T], ACT.Copy).then_inc(q_copied, 1)

            def squares(j, u):
                b = j * RING + u
                act.wait_ge(q_ready, b + 1)
                if past(b - 1):
                    act.wait_ge(summed, b - 1)
                for t in range(TT):
                    i = nc.scalar.activation(square[:, u % 2, t, :], pqkv[u % 2][t][:, 0:2 * D], ACT.Square)
                i.then_inc(squared, 1)
                if past(j):
                    act.wait_ge(stored[u], j * (STORES * 16))
                for t in range(TT):
                    i = nc.scalar.activation(vt[:, u, t, :, 0:HD], pqkv[u % 2][t][:, 2 * D:3 * D]
                                             .rearrange("p (h c) -> p h c", h=H), ACT.Copy)
                i.then_inc(v_taken, 1)

            def roots(j, u):
                nn = norm[:, u % 2, :, :, :].rearrange("p t n h -> p (t n h)")
                act.wait_ge(summed, j * RING + u + 1)
                nc.scalar.activation(nn, nn, ACT.Sqrt, scale=1.0 / HD).then_inc(rooted, 1)

            def scaled_unit(j, u):
                b = j * RING + u
                act.wait_ge(unit_turned, b + 1)
                for n in range(2):
                    i = nc.scalar.activation(qk[:, u, n, :], pturn[:, n * T:(n + 1) * T], ACT.Copy,
                                             scale=qkscale[:, n:n + 1])
                i.then_inc(qk_ready, 1)

            def split_high(j, u):
                b = j * RING + u
                if plain:
                    act.wait_ge(q_copied, b + 1)
                else:
                    act.wait_ge(qk_ready, b + 1)
                if past(j):
                    act.wait_ge(stored[u], j * (STORES * 16))
                nc.scalar.activation(parts[:, u, :, 0, :], qk[:, u, :, :], ACT.Copy).then_inc(high, 1)

            def split_middle(j, u):
                act.wait_ge(left, j * RING + u + 1)
                nc.scalar.activation(parts[:, u, :, 1, :], rest[:, u % 2, :, :], ACT.Copy).then_inc(middle, 1)

            take(0, 0)
            if cosine:
                act.wait_ge(cleared, RING)

            def step(j, u):
                if cosine:
                    run(roots, j, u, -1)
                    run(scaled_unit, j, u, -2)
                run(split_high, j, u, -LAG)
                run(take, j, u, 1)
                if cosine:
                    run(squares, j, u, 0)
                if plain:
                    run(copy_q, j, u, 0)
                run(split_middle, j, u, -LAG)
            steps(act, step)


def attend(nc, kind, m, w):
    causal = kind == "causal"
    RING = 4
    QUAD = 4
    SW = T + (P if causal else T)
    with ExitStack() as ctx:
        sb = lambda n, s, d=f32: ctx.enter_context(nc.sbuf_tensor(f"{kind}{m.serial}_{n}", s, d))
        ps = lambda n, s, d=f32: ctx.enter_context(nc.psum_tensor(f"{kind}{m.serial}_{n}", s, d))
        new_sem = ctx.enter_context(semaphores(nc))
        sem = lambda n: new_sem(f"{kind}{m.serial}_{n}")
        resid = m.y if causal else m.x
        qst, kst = m.qst, m.kst
        vst = sb("vst", [P, RING, TT, H // 2, VW])
        neg = sb("neg", [P, 2, TT, 2, UP])
        msp = sb("msp", [P, 2, TT, 2, 2, UP], bf16)
        mrow = sb("mrow", [2 * 2 * UP, 2, T], bf16)
        prob = sb("prob", [P, UP, 2, SW])
        usb = sb("usb", [P, 2, T])
        rec = sb("rec", [P, TT * H // 2])
        o = sb("o", [P, TT, D])
        oT = sb("oT", [P, T])
        wo = sb("wo", [P, D])
        ps_s = [ps(f"s{t}", [P, 512]) for t in range(2)]
        ps_st = [ps(f"st{t}", [P, 2, 512]) for t in range(2)]
        ps_u = ps("u", [P, 512])
        ps_m = ps("m", [P, 512])

        w_in = sem("w_in")
        stack_in = [sem(f"stack_in{k}") for k in range(RING)]
        mrow_in = [sem(f"mrow_in{k}") for k in range(RING)]
        s_ready, s_read = sem("s_ready"), sem("s_read")
        halved = sem("halved")
        msplit, mturned, mrow_ready = sem("msplit"), sem("mturned"), sem("mrow_ready")
        st_ready, exp_done = sem("st_ready"), sem("exp_done")
        pv_done, u_out = sem("pv_done"), sem("u_out")
        t_ready, inverted, t_read = sem("t_ready"), sem("inverted"), sem("t_read")
        ot_ready, ot_out = sem("ot_ready"), sem("ot_out")
        proj_ready, added = sem("proj_ready"), sem("added")
        cleared = sem("u_cleared")
        STACK_DMAS, MROW_DMAS = 4, 1
        block = ctx.enter_context(nc.Block())

        def steps(eng, step):
            for k in range(RING):
                step(0, k)
            with eng.Fori(1, UNITS // RING - 1) as j:
                for k in range(RING):
                    step(j, k)
            for k in range(RING):
                step(UNITS // RING - 1, k)
            for k in range(2):
                step(UNITS // RING, k)

        def has_unit(j, k, ahead):
            return not isinstance(j, int) or 0 <= j * RING + k + ahead < UNITS

        @block.sync
        def _(sp):
            sp.dma_start(wo[:, :], w["woT"]).then_inc(w_in, 16)

            def load(j, k):
                b, p0 = j * 2 + k // 2, UP * (k % 2)
                rows = m.qk_dram[bass.ds(b, 1), 0:6, :, :, p0:p0 + UP, :].rearrange("o r d x p t -> (o r d x) p t")
                sp.dma_start(qst[0:ROWS, k, :, :], rows).then_inc(stack_in[k], 16)
                for x in range(2):
                    rows = m.qk_dram[bass.ds(b, 1), 6:12, :, x, p0:p0 + UP, :].rearrange("o r d p t -> (o r d) p t")
                    sp.dma_start(kst[x:ROWS:2, k, x, :, :], rows).then_inc(stack_in[k], 16)
                h0 = (H // 2) * (k % 2)
                v = m.v_dram[bass.ds(b, 1), :, :, h0 * VW:(h0 + H // 2) * VW].rearrange("o p t c -> (o p) t c")
                sp.dma_start(vst[:, k, :, :, :].rearrange("p t h c -> p t (h c)"), v).then_inc(stack_in[k], 16)

            def bring_max(j, k):
                u = j * RING + k
                sp.wait_ge(mrow_ready, u + 1)
                sp.dma_start(qst[ROWS:ROWS + 4, k, :, :].rearrange("c p t -> c (p t)"), mrow[:, k % 2, :])\
                    .then_inc(mrow_in[k], 16)

            for k in range(3):
                load(0, k)
            bring_max(0, 0)

            def step(j, k):
                s = j * RING + k
                if has_unit(j, k, 3):
                    if past(s):
                        sp.wait_ge(pv_done, s * 2)
                    load(j + (k + 3) // RING, (k + 3) % RING)
                if has_unit(j, k, 1):
                    bring_max(j + (k + 1) // RING, (k + 1) % RING)
            steps(sp, step)

        def pass1_columns(t):
            return P if causal and t == 0 else T

        @block.tensor
        def _(pe):
            def scores1(j, k, p, tiles=range(TT)):
                u = j * RING + k
                if p == 0 and 0 in tiles:
                    pe.wait_ge(stack_in[k], (j + 1) * (STACK_DMAS * 16))
                for t in tiles:
                    c = pass1_columns(t)
                    n = (u * UP + p) * TT + t
                    if past(n - 1):
                        pe.wait_ge(s_read, n - 1)
                    q = qst[0:ROWS, k, p, t * P:(t + 1) * P]
                    out = ps_s[t][:, :].rearrange("p (x c) -> p x c", x=2)[:, :, 0:c]
                    i = nc.tensor.matmul(out, q, kst[0:ROWS, k, :, p, 0:c], start=True, stop=not causal)
                    if causal:
                        i = nc.tensor.matmul(out[:, :, c - P:c], m.ident16[:, :], m.mask_qk[:, :, :],
                                             start=False, stop=True)
                    i.then_inc(s_ready, 1)

            def turn_max(j, k):
                u = j * RING + k
                pe.wait_ge(msplit, u + 1)
                if past(u - 1):
                    pe.wait_ge(u_out, (u - 1) * 2)
                if not past(u - 1) and past(u):
                    pe.wait_ge(mrow_ready, 1)
                for t in range(TT):
                    i = nc.tensor.matmul(ps_u[0:4 * UP, T + t * P:T + (t + 1) * P],
                                         msp[:, k % 2, t, :, :, :].rearrange("p x r q -> p (x r q)"),
                                         m.ident16[:, :], start=True, stop=True)
                i.then_inc(mturned, 1)

            def scores2(j, k, p, x):
                u = j * RING + k
                if p == 0 and x == 0:
                    pe.wait_ge(mrow_in[k], (j + 1) * (MROW_DMAS * 16))
                n = u * UP + p
                if x == 0 and past(n - 1):
                    pe.wait_ge(exp_done, n - 1)
                for kt in range(TT):
                    q0 = P if causal and kt else 0
                    c0 = T * kt
                    key = kst[0:ROWS + 4, k, x, p, kt * P:(kt + 1) * P]
                    out = ps_st[p % 2][:, x, c0:c0 + T - q0]
                    i = nc.tensor.matmul(out, key, qst[0:ROWS + 4, k, p, q0:T], start=True, stop=not causal)
                    if causal:
                        i = nc.tensor.matmul(out[:, 0:P], m.ident16[:, :], m.mask_kq[:, :], start=False, stop=True)
                if x == 1:
                    i.then_inc(st_ready, 1)

            def values(j, k, qd):
                u = j * RING + k
                n = u * 2 + qd
                pe.wait_ge(exp_done, u * UP + 2 * qd + 2)
                if past(n):
                    pe.wait_ge(u_out, n)
                if qd == 0 and has_unit(j, k, 1):
                    pe.wait_ge(mrow_ready, u + 2)
                for kt in range(TT):
                    q0 = P if causal and kt else 0
                    for g in range(QUAD):
                        h = QUAD * qd + g
                        i = nc.tensor.matmul(ps_u[32 * g:32 * g + VW, q0:T], vst[:, k, kt, h, :],
                                             prob[:, h // 2, h % 2, T * kt:T * kt + T - q0],
                                             start=kt == 0, stop=kt == TT - 1, tile_position=(0, 32 * g))
                i.then_inc(pv_done, 1)

            def turn_values(j, k):
                pe.wait_ge(u_out, (j * RING + k) * 2 + 2)
                for t in range(TT):
                    for qd in range(2):
                        c = (t * 2 + qd) * P
                        i = nc.tensor.transpose(ps_m[:, c:c + P], usb[:, qd, t * P:(t + 1) * P], m.ident[:, :])
                i.then_inc(t_ready, 1)

            pe.wait_ge(cleared, 1)
            for p in range(UP):
                scores1(0, 0, p)
            for p in range(UP):
                scores1(0, 1, p)
            turn_max(0, 0)
            pe.wait_ge(w_in, 16)

            def step(j, k):
                s = j * RING + k
                jj, kk = (j, k - 1) if k else (j - 1, RING - 1)
                behind = past(s) and has_unit(j, k, -1)
                for p in range(UP):
                    for i in range(2):
                        if has_unit(j, k, 2):
                            scores1(j + (k + 2) // RING, (k + 2) % RING, p, [i])
                        if has_unit(j, k, 0):
                            scores2(j, k, p, i)
                    if p == 0 and behind:
                        values(jj, kk, 1)
                    if p == 1 and has_unit(j, k, 1):
                        turn_max(j + (k + 1) // RING, (k + 1) % RING)
                    if p == 1 and behind:
                        if k % 2 == 1 and past(s - 1):
                            pe.wait_ge(ot_out, j * 2 + (k - 1) // 2)
                        elif k % 2 == 0 and past(s - 2):
                            pe.wait_ge(added, j * 2 + (k - 2) // 2)
                        elif past(s - 1):
                            pe.wait_ge(t_read, 1)
                        turn_values(jj, kk)
                    if p == 2 and has_unit(j, k, 0):
                        values(j, k, 0)
                    if p == 3 and k % 2 == 0 and past(s):
                        pe.wait_ge(t_read, s)
                        for t in range(TT):
                            i = nc.tensor.transpose(ps_m[:, t * P:(t + 1) * P], o[:, t, :], m.ident[:, :])
                        i.then_inc(ot_ready, 1)
                    if p == 3 and k % 2 == 1 and past(s - 1):
                        if behind:
                            pe.wait_ge(t_read, s)
                        pe.wait_ge(ot_out, j * 2 + (k - 1) // 2)
                        for t in range(TT):
                            i = nc.tensor.matmul(ps_m[:, t * P:(t + 1) * P], oT[:, t * P:(t + 1) * P], wo[:, :],
                                                 start=True, stop=True)
                        i.then_inc(proj_ready, 1)
            steps(pe, step)

        @block.vector
        def _(dve):
            nc.vector.memset(ps_u[:, :], 0.0).then_inc(cleared, 1)

            def maxima(j, k, p, tiles=range(TT)):
                u = j * RING + k
                for t in tiles:
                    c = pass1_columns(t)
                    dve.wait_ge(s_ready, (u * UP + p) * TT + t + 1)
                    if p == 0 and t == 0 and past(u - 1):
                        dve.wait_ge(msplit, u - 1)
                    nc.vector.tensor_reduce(neg[:, k % 2, t, :, p],
                                            ps_s[t][:, :].rearrange("p (x c) -> p x c", x=2)[:, :, 0:c],
                                            AX.X, ALU.max, negate=True).then_inc(s_read, 1)

            def split_max(j, k, part):
                u = j * RING + k
                n_ = neg[:, k % 2, :, :, :].rearrange("p t x q -> p (t x) q")
                hi, mid = (msp[:, k % 2, :, :, r, :].rearrange("p t x q -> p (t x) q") for r in range(2))
                if part == 0:
                    dve.wait_ge(s_read, (u + 1) * (UP * TT))
                    if past(u - 1):
                        dve.wait_ge(mturned, u - 1)
                    nc.vector.tensor_copy(hi, n_).then_inc(halved, 1)
                else:
                    dve.wait_ge(halved, u + 1)
                    nc.vector.tensor_tensor(mid, n_, hi, ALU.subtract).then_inc(msplit, 1)

            def normalize(j, k, part):
                u = j * RING + k
                h0 = (H // 2) * (k % 2)
                tv = ps_m[:, :].rearrange("p (g c) -> p g c", c=32)
                if part == 0:
                    dve.wait_ge(t_ready, u + 1)
                    if past(u):
                        dve.wait_ge(t_read, u)
                    nc.vector.reciprocal(rec[:, :], tv[:, :, HD]).then_inc(inverted, 1)
                else:
                    dve.wait_ge(inverted, u + 1)
                    nc.vector.tensor_tensor(o[:, :, h0 * HD:(h0 + H // 2) * HD].rearrange("p t (g c) -> p t g c", c=HD),
                                            tv[:, :, 0:HD].rearrange("p (t g) c -> p t g c", t=TT),
                                            rec[:, :].rearrange("p (t g) -> p t g", t=TT).unsqueeze(3)
                                            .broadcast_to([P, TT, H // 2, HD]), ALU.mult).then_inc(t_read, 1)

            for k in range(2):
                for p in range(UP):
                    for t in range(TT):
                        maxima(0, k, p, [t])
                        if k == 1 and p == 0:
                            split_max(0, 0, t)

            def add_output(before, n0):
                dve.wait_ge(proj_ready, before + 1)
                x = resid[:, bass.ds(n0, TT), :]
                nc.vector.tensor_tensor(x, x, ps_m[:, 0:TT * D].rearrange("p (t c) -> p t c", t=TT),
                                        ALU.add).then_inc(added, 1)

            def step(j, k):
                s = j * RING + k
                jj, kk = (j, k - 1) if k else (j - 1, RING - 1)
                behind = past(s) and has_unit(j, k, -1)
                for p in range(UP):
                    for t in range(TT):
                        summed = k % 2 == 0 and past(s - 2)
                        if p == 2 and t == 0 and summed:
                            dve.wait_ge(added, j * 2 + (k - 4) // 2 + 1)
                        if has_unit(j, k, 2):
                            maxima(j + (k + 2) // RING, (k + 2) % RING, p, [t])
                        if p == 2 and t == 0 and summed:
                            take_moments(nc, m, resid, (j * 2 + (k - 4) // 2) * TT, TT)
                        if p == 0 and t == 1 and summed:
                            add_output(j * 2 + (k - 4) // 2, (j * 2 + (k - 4) // 2) * TT)
                        if p == 0 and has_unit(j, k, 1):
                            split_max(j + (k + 1) // RING, (k + 1) % RING, t)
                        if p == 2 and behind:
                            normalize(jj, kk, t)
            steps(dve, step)
            add_output(B - 1, (B - 1) * TT)
            dve.wait_ge(added, B)
            take_moments(nc, m, resid, (B - 1) * TT, TT)

        @block.scalar
        def _(act):
            def rows(j, k):
                u = j * RING + k
                act.wait_ge(mturned, u + 1)
                if past(u - 1):
                    act.wait_ge(mrow_in[(k - 2) % RING], (j + 1 - (k < 2)) * (MROW_DMAS * 16))
                nc.scalar.activation(mrow[:, k % 2, :], ps_u[0:4 * UP, T:2 * T], ACT.Copy).then_inc(mrow_ready, 1)

            def exps(j, k, p):
                n = (j * RING + k) * UP + p
                act.wait_ge(st_ready, n + 1)
                if p % 2 == 0 and past(n - UP + 1):
                    act.wait_ge(pv_done, (j * RING + k) * 2 + p // 2 - 1)
                nc.scalar.activation(prob[:, p, :, :], ps_st[p % 2][:, :, 0:SW], ACT.Exp, scale=SCALE)\
                    .then_inc(exp_done, 1)

            def keep_values(j, k, qd):
                n = (j * RING + k) * 2 + qd
                act.wait_ge(pv_done, n + 1)
                if past(j * RING + k):
                    act.wait_ge(t_ready, j * RING + k)
                nc.scalar.activation(usb[:, qd, :], ps_u[:, 0:T], ACT.Copy).then_inc(u_out, 1)

            rows(0, 0)

            def step(j, k):
                s = j * RING + k
                jj, kk = (j, k - 1) if k else (j - 1, RING - 1)
                if has_unit(j, k, 0):
                    exps(j, k, 0)
                if past(s) and has_unit(j, k, -1):
                    keep_values(jj, kk, 1)
                if has_unit(j, k, 0):
                    exps(j, k, 1)
                if has_unit(j, k, 1):
                    rows(j + (k + 1) // RING, (k + 1) % RING)
                if has_unit(j, k, 0):
                    exps(j, k, 2)
                    keep_values(j, k, 0)
                    exps(j, k, 3)
                if k % 2 == 0 and past(s):
                    act.wait_ge(ot_ready, j * 2 + k // 2)
                    nc.scalar.activation(oT[:, :], ps_m[:, 0:T], ACT.Copy).then_inc(ot_out, 1)
            steps(act, step)


def experts0(nc, m, w):
    G = 4
    N = G * P
    C = F0 // P
    GROUPS = NT // G
    with ExitStack() as ctx:
        sb = lambda n, s, d=f32: ctx.enter_context(nc.sbuf_tensor(f"e0_{n}", s, d))
        ps = lambda n, s, d=f32: ctx.enter_context(nc.psum_tensor(f"e0_{n}", s, d))
        new_sem = ctx.enter_context(semaphores(nc))
        sem = lambda n: new_sem(f"e0_{n}")
        w1, w2 = sb("w1", [P, E0, F0]), sb("w2", [P, E0, C, D])
        b1, b2 = sb("b1", [P, E0, C]), sb("b2", [P, E0])
        gw, gb, n2 = sb("gw", [P, E0]), sb("gb", [P, E0]), sb("n2", [P, 1])
        xn = sb("xn", [P, 2, G, D])
        xT = sb("xT", [P, 2, N])
        hid = sb("hid", [P, 4, N])
        yT = sb("yT", [P, 2, N])
        acc = sb("acc", [P, 2, G, D])
        lg, eq, one = sb("lg", [P, G, E0]), sb("eq", [P, G, E0]), sb("one", [P, 2, G, E0])
        top = sb("top", [P, G])
        turn, psl, pst = ps("turn", [P, 512]), ps("psl", [P, 512]), ps("pst", [P, 512])
        psh = [ps(f"h{i}", [P, 512]) for i in range(2)]
        psy = [ps(f"y{i}", [P, 512]) for i in range(2)]
        w_in, normed, turned, x_ready = sem("w_in"), sem("normed"), sem("turned"), sem("x_ready")
        lg_ready, order, chosen = sem("lg_ready"), sem("order"), sem("chosen")
        h_ready, h_act, h_dve = sem("h_ready"), sem("h_act"), sem("h_dve")
        y_done, y_out, t_ready, summed = (sem(x) for x in ("y_done", "y_out", "t_ready", "summed"))
        joined = sem("joined")
        K_ROWS = 8
        empty = sb("empty", [P, K_ROWS, ROW])
        empty_made, emptied = sem("empty_made"), sem("emptied")
        block = ctx.enter_context(nc.Block())
        loads = [(w1, w["w1"]), (w2, w["w2"]), (b1, w["b1"]), (b2, w["b2"]), (gw, w["gw"]), (n2, w["n2"])]
        EC = E0 * C

        def groups(eng, step):
            for u in range(2):
                step(0, u)
            with eng.Fori(1, GROUPS // 2 - 1) as j:
                for u in range(2):
                    step(j, u)
            for u in range(2):
                step(GROUPS // 2 - 1, u)
            step(GROUPS // 2, 0)

        def run(stage, j, u, q):
            k = u + q // EC
            j, u = j + k // 2, k % 2
            if not isinstance(j, int) or 0 <= j * 2 + u < GROUPS:
                stage(j, u, q % EC)

        @block.sync
        def _(sp):
            for dst, s in loads:
                sp.dma_start(dst[:], s).then_inc(w_in, 16)
            sp.dma_start(gb[:, :], w["gb"].partition_broadcast(P)).then_inc(w_in, 16)
            sp.wait_ge(empty_made, 2)
            n_rows = P * K_ROWS
            for n in range(SLOTS // n_rows):
                sp.dma_start(m.slots[n * n_rows:(n + 1) * n_rows, :].rearrange("(p k) d -> p (k d)", k=K_ROWS),
                             empty[:, :, :].rearrange("p k d -> p (k d)")).then_inc(emptied, 16)
            sp.wait_ge(emptied, 16 * (SLOTS // n_rows))

        @block.gpsimd
        def _(pool):
            def step(j, u):
                if isinstance(j, int) and j * 2 + u == GROUPS:
                    return
                pool.wait_ge(summed, (j * 2 + u) * E0 + E0)
                x = m.x[:, bass.ds(j * (2 * G) + u * G, G), :]
                nc.gpsimd.tensor_tensor(x, x, acc[:, u, :, :], ALU.add).then_inc(joined, 1)
            groups(pool, step)

        @block.vector
        def _(dve):
            def normalize(j, u, q=0):
                g = j * 2 + u
                if past(g - 1):
                    dve.wait_ge(turned, g - 1)
                for t in range(G):
                    n = j * (2 * G) + (u * G + t)
                    i = nc.vector.tensor_scalar(xn[:, u, t, :], m.y[:, bass.ds(n, 1), :].rearrange("p o d -> p (o d)"),
                                                m.y_rms[:, bass.ds(n, 1)], None, ALU.mult)
                i.then_inc(normed, 1)

            def choose(j, u, q=0):
                g = j * 2 + u
                o = Order(5, g)
                lgp = psl[:, 0:G * E0].rearrange("p (t e) -> p t e", e=E0)
                dve.wait_ge(lg_ready, g + 1)
                nc.vector.tensor_tensor(lg[:, :, :], lgp, gb[:, :].unsqueeze(1).broadcast_to([P, G, E0]),
                                        ALU.add).then_inc(order, 1)
                dve.wait_ge(order, o.next())
                nc.vector.tensor_reduce(top[:, :], lg[:, :, :], AX.X, ALU.max).then_inc(order, 1)
                dve.wait_ge(order, o.next())
                nc.vector.tensor_tensor(eq[:, :, :], lg[:, :, :], top[:, :].unsqueeze(2).broadcast_to([P, G, E0]),
                                        ALU.is_equal).then_inc(order, 1)
                dve.wait_ge(order, o.next())
                nc.vector.tensor_tensor(eq[:, :, :], eq[:, :, :], m.prior[:, 0:E0].unsqueeze(1)
                                        .broadcast_to([P, G, E0]), ALU.mult).then_inc(order, 1)
                dve.wait_ge(order, o.next())
                nc.vector.tensor_reduce(top[:, :], eq[:, :, :], AX.X, ALU.max).then_inc(order, 1)
                dve.wait_ge(order, o.next())
                nc.vector.tensor_tensor(one[:, u, :, :], eq[:, :, :], top[:, :].unsqueeze(2)
                                        .broadcast_to([P, G, E0]), ALU.is_equal).then_inc(chosen, 1)

            nc.vector.memset(empty[:, :, 0:NUMBER], 0.0).then_inc(empty_made, 1)
            nc.vector.memset(empty[:, :, NUMBER:ROW].bitcast(u32), NO_TOKEN).then_inc(empty_made, 1)
            normalize(0, 0)
            dve.wait_ge(w_in, 16 * (len(loads) + 1))
            choose(0, 0)

            def add_expert(j, u, q):
                g, e = j * 2 + u, q // C
                dve.wait_ge(t_ready, g * E0 + e + 1)
                dve.wait_ge(chosen, g + 1)
                if e:
                    dve.wait_ge(summed, g * E0 + e)
                elif past(g - 1):
                    dve.wait_ge(joined, g - 1)
                for t in range(G):
                    n = j * (2 * G) + (u * G + t)
                    base = acc[:, u, t, :] if e else m.y[:, bass.ds(n, 1), :].rearrange("p o d -> p (o d)")
                    i = nc.vector.scalar_tensor_tensor(out=acc[:, u, t, :], in0=pst[:, t * P:(t + 1) * P],
                                                       scalar=one[:, u, t, e:e + 1], in1=base,
                                                       op0=ALU.mult, op1=ALU.add)
                i.then_inc(summed, 1)

            def hidden(j, u, q):
                g = j * 2 + u
                dve.wait_ge(h_ready, g * EC + q + 1)
                if past(g * EC + q - 3):
                    dve.wait_ge(y_done, g * EC + q - 3)
                nc.vector.tensor_scalar(hid[:, q % 4, :], psh[q % 2][:, :], b1[:, q // C, q % C:q % C + 1], 0.0,
                                        ALU.add, ALU.max).then_inc(h_dve, 1)

            def moments(j, u, q):
                take_moments(nc, m, m.x, j * (2 * G) + u * G, G)

            def step(j, u):
                g = j * 2 + u
                for q in range(EC):
                    if q == 11 and past(g):
                        dve.wait_ge(joined, g)
                    if q % 2:
                        run(hidden, j, u, q)
                    if q == 11:
                        run(moments, j, u, q - EC)
                    if q == 8:
                        run(normalize, j, u, q + EC)
                    if q == 12:
                        run(choose, j, u, q + EC)
                    if q % C == C - 1:
                        run(add_expert, j, u, q - 7)
            groups(dve, step)

        @block.scalar
        def _(act):
            act.wait_ge(w_in, 16 * (len(loads) + 1))

            def take(j, u, q=0):
                g = j * 2 + u
                act.wait_ge(turned, g + 1)
                if past(g - 1):
                    act.wait_ge(h_ready, (g - 1) * EC)
                    act.wait_ge(lg_ready, g - 1)
                nc.scalar.activation(xT[:, u, :], turn[:, :], ACT.Copy, scale=n2[:, :]).then_inc(x_ready, 1)

            take(0, 0)

            def hidden(j, u, q):
                g = j * 2 + u
                act.wait_ge(h_ready, g * EC + q + 1)
                if past(g * EC + q - 3):
                    act.wait_ge(y_done, g * EC + q - 3)
                nc.scalar.activation(hid[:, q % 4, :], psh[q % 2][:, :], ACT.Relu,
                                     bias=b1[:, q // C, q % C:q % C + 1]).then_inc(h_act, 1)

            def keep_outputs(j, u, q):
                g, e = j * 2 + u, q // C
                act.wait_ge(y_done, g * EC + e * C + C)
                if past(g * E0 + e - 1):
                    act.wait_ge(t_ready, g * E0 + e - 1)
                nc.scalar.activation(yT[:, e % 2, :], psy[e % 2][:, :], ACT.Identity,
                                     bias=b2[:, e:e + 1]).then_inc(y_out, 1)

            def step(j, u):
                for q in range(EC):
                    if q % 2 == 0:
                        run(hidden, j, u, q)
                    if q == 9:
                        run(take, j, u, q + EC)
                    if q % C == 2:
                        run(keep_outputs, j, u, q - 6)
            groups(act, step)

        @block.tensor
        def _(pe):
            def turns(j, u, q=0):
                g = j * 2 + u
                pe.wait_ge(normed, g + 1)
                if past(g):
                    pe.wait_ge(x_ready, g)
                for t in range(G):
                    i = nc.tensor.transpose(turn[:, t * P:(t + 1) * P], xn[:, u, t, :], m.ident[:, :])
                i.then_inc(turned, 1)

            def logits(j, u, q=0):
                g = j * 2 + u
                pe.wait_ge(x_ready, g + 1)
                if past(g):
                    pe.wait_ge(chosen, g)
                for t in range(G):
                    i = nc.tensor.matmul(psl[:, t * E0:(t + 1) * E0], xT[:, u, t * P:(t + 1) * P], gw[:, :],
                                         start=True, stop=True)
                i.then_inc(lg_ready, 1)

            turns(0, 0)
            pe.wait_ge(w_in, 16 * (len(loads) + 1))
            logits(0, 0)

            def hidden(j, u, q):
                g = j * 2 + u
                if past(g * EC + q - 1):
                    pe.wait_ge(h_dve if q % 2 else h_act, g * (EC // 2) + q // 2)
                nc.tensor.matmul(psh[q % 2][:, :], w1[:, q // C, (q % C) * P:(q % C + 1) * P], xT[:, u, :],
                                 start=True, stop=True).then_inc(h_ready, 1)

            def outputs(j, u, q):
                g, e, c = j * 2 + u, q // C, q % C
                pe.wait_ge(h_dve if q % 2 else h_act, g * (EC // 2) + q // 2 + 1)
                if c == 0 and past(g * E0 + e - 1):
                    pe.wait_ge(y_out, g * E0 + e - 1)
                nc.tensor.matmul(psy[e % 2][:, :], w2[:, e, c, :], hid[:, q % 4, :],
                                 start=c == 0, stop=c == C - 1).then_inc(y_done, 1)

            def turn_outputs(j, u, q):
                g, e = j * 2 + u, q // C
                pe.wait_ge(y_out, g * E0 + e + 1)
                if past(g * E0 + e):
                    pe.wait_ge(summed, g * E0 + e)
                for t in range(G):
                    i = nc.tensor.transpose(pst[:, t * P:(t + 1) * P], yT[:, e % 2, t * P:(t + 1) * P], m.ident[:, :])
                i.then_inc(t_ready, 1)

            def step(j, u):
                for q in range(EC):
                    run(hidden, j, u, q)
                    run(outputs, j, u, q - 2)
                    if q == 8:
                        run(turns, j, u, q + EC)
                    if q == 11:
                        run(logits, j, u, q + EC)
                    if q % C == C - 1:
                        run(turn_outputs, j, u, q - 7)
            groups(pe, step)


def route1(nc, m, w, out):
    G, GROUPS = 4, NT // 4
    PARTS = 4
    PT = NT // PARTS
    with ExitStack() as ctx:
        sb = lambda n, s, d=f32: ctx.enter_context(nc.sbuf_tensor(f"r1_{n}", s, d))
        ps = lambda n, s, d=f32: ctx.enter_context(nc.psum_tensor(f"r1_{n}", s, d))
        new_sem = ctx.enter_context(semaphores(nc))
        sem = lambda n: new_sem(f"r1_{n}")
        gw = sb("gw", [P, E1])
        xn = sb("xn", [P, 2, G, D])
        xT = sb("xT", [P, 2, G * P])
        lg, ex, one = sb("lg", [P, NT, E1]), sb("ex", [P, NT, E1]), sb("one", [P, NT, E1])
        one16 = sb("one16", [P, NT, E1], bf16)
        tot = sb("tot", [P, NT, E1])
        inc = [sb(f"inc{c}", [P, E1, PT]) for c in range(PARTS)]
        mx, sm, esel = sb("mx", [P, NT]), sb("sm", [P, NT]), sb("esel", [P, NT])
        rank, keep, slot = sb("rank", [P, NT]), sb("keep", [P, NT]), sb("slot", [P, NT])
        onesf = sb("onesf", [P, PT])
        turn = [ps(f"turn{i}", [P, 512]) for i in range(2)]
        psl = [ps(f"l{i}", [P, 512]) for i in range(2)]
        ps_pre, ps_tot = ([ps(f"{n}{c}", [P, 512]) for c in range(2)] for n in ("ps_pre", "ps_tot"))
        w_in, normed, turned, x_ready, lg_ready, lg_kept = (sem(x) for x in ("w_in", "normed", "turned", "x_ready",
                                                                            "lg_ready", "lg_kept"))
        order, less, exped, counted, one_ready = (sem(x) for x in ("order", "less", "exped", "counted", "one_ready"))
        slot_ready, scattered, x_out, y_kept = (sem(x) for x in ("slot_ready", "scattered", "x_out", "y_kept"))
        block = ctx.enter_context(nc.Block())

        def groups(eng, step, c):
            first, end = c * GROUPS // PARTS // 2, (c + 1) * GROUPS // PARTS // 2
            for u in range(2):
                step(first, u)
            if end - first > 1:
                with eng.Fori(first + 1, end) as j:
                    for u in range(2):
                        step(j, u)
            for u in range(2):
                step(end, u)

        def run(stage, c, j, u, d):
            j, u = j + (u + d) // 2, (u + d) % 2
            if not isinstance(j, int) or c * GROUPS // PARTS <= j * 2 + u < (c + 1) * GROUPS // PARTS:
                stage(j, u)

        @block.sync
        def _(sp):
            sp.dma_start(gw[:, :], w["gw"]).then_inc(w_in, 16)
            view = out.rearrange("b (t p) d -> p (b t) d", p=P)
            for n in range(0, NT, PT):
                sp.dma_start(view[:, n:n + PT, :], m.x[:, n:n + PT, :]).then_inc(x_out, 16)
            sp.wait_ge(x_out, 16 * PARTS)

        @block.gpsimd
        def _(pool):
            for n in range(NT):
                if n % PT == 0:
                    pool.wait_ge(slot_ready, n // PT + 1)
                nc.gpsimd.indirect_dma_start(out=m.slots, out_offset=bass.IndirectOffsetOnAxis(
                    ap=m.to_slot[:, n:n + 1], axis=0), in_=m.rows[:, n, :], in_offset=None,
                    bounds_check=SLOTS - 1, oob_is_err=False).then_inc(scattered, 16)
            pool.wait_ge(scattered, 16 * NT)

        @block.scalar
        def _(act):
            def step(j, u):
                g = j * 2 + u
                act.wait_ge(turned, g + 1)
                if past(g - 1):
                    act.wait_ge(lg_ready, g - 1)
                nc.scalar.activation(xT[:, u, :], turn[u][:, :], ACT.Copy).then_inc(x_ready, 1)
                nc.scalar.activation(m.y[:, bass.ds(j * (2 * G) + u * G, G), :], xn[:, u, :, :], ACT.Copy)\
                    .then_inc(y_kept, 1)

            for c in range(PARTS):
                groups(act, lambda j, u: run(step, c, j, u, 0), c)
                part = slice(c * PT, (c + 1) * PT)
                act.wait_ge(less, c + 1)
                nc.scalar.activation(ex[:, part, :], lg[:, part, :], ACT.Exp).then_inc(exped, 1)

        @block.tensor
        def _(pe):
            pe.wait_ge(w_in, 16)

            def turns(j, u):
                g = j * 2 + u
                pe.wait_ge(normed, g + 1)
                if past(g - 1):
                    pe.wait_ge(x_ready, g - 1)
                for t in range(G):
                    i = nc.tensor.transpose(turn[u][:, t * P:(t + 1) * P], xn[:, u, t, :], m.ident[:, :])
                i.then_inc(turned, 1)

            def logits(j, u):
                g = j * 2 + u
                pe.wait_ge(x_ready, g + 1)
                if past(g - 1):
                    pe.wait_ge(lg_kept, g - 1)
                for t in range(G):
                    i = nc.tensor.matmul(psl[u][:, t * E1:(t + 1) * E1], xT[:, u, t * P:(t + 1) * P], gw[:, :],
                                         start=True, stop=True)
                i.then_inc(lg_ready, 1)

            for c in range(PARTS):
                def step(j, u):
                    run(turns, c, j, u, 0)
                    run(logits, c, j, u, -1)
                groups(pe, step, c)
                pe.wait_ge(one_ready, c + 1)
                rhs = one16[:, c * PT:(c + 1) * PT, :].rearrange("p n e -> p (n e)")
                nc.tensor.matmul(ps_pre[c % 2][:, 0:PT * E1], m.before[:, :], rhs, start=True, stop=True)
                nc.tensor.matmul(ps_tot[c % 2][:, 0:PT * E1], m.ones16[:, :], rhs, start=True, stop=True)\
                    .then_inc(counted, 1)

        @block.vector
        def _(dve):
            def normalize(j, u):
                g = j * 2 + u
                if past(g - 1):
                    dve.wait_ge(turned, g - 1)
                    dve.wait_ge(y_kept, g - 1)
                for t in range(G):
                    n = j * (2 * G) + (u * G + t)
                    row = m.x[:, bass.ds(n, 1), :].rearrange("p o d -> p (o d)")
                    mean, inv = m.x_stat[:, bass.ds(n, 1), 0], m.x_rstd[:, bass.ds(n, 1)]
                    i = nc.vector.tensor_scalar(xn[:, u, t, :], row, mean, inv, ALU.subtract, ALU.mult)
                i.then_inc(normed, 1)

            def keep_logits(j, u):
                dve.wait_ge(lg_ready, j * 2 + u + 1)
                nc.vector.tensor_copy(lg[:, bass.ds(j * (2 * G) + u * G, G), :],
                                      psl[u][:, 0:G * E1].rearrange("p (t e) -> p t e", e=E1)).then_inc(lg_kept, 1)

            nc.vector.memset(onesf[:, :], 1.0).then_inc(order, 1)

            def wide(a):
                return a.unsqueeze(2).broadcast_to([P, PT, E1])

            def flat(a):
                return a.unsqueeze(1).broadcast_to([P, PT, E1])

            o = Order(100, 0)
            o.next()
            for c in range(PARTS):
                def step(j, u):
                    run(normalize, c, j, u, 0)
                    run(keep_logits, c, j, u, -2)
                groups(dve, step, c)
                dve.wait_ge(lg_kept, (c + 1) * GROUPS // PARTS)

                part = slice(c * PT, (c + 1) * PT)
                lg_, ex_, one_, tot_ = (a[:, part, :] for a in (lg, ex, one, tot))
                mx_, sm_, esel_, rank_, keep_, slot_ = (a[:, part] for a in (mx, sm, esel, rank, keep, slot))
                gate_ = m.gate[:, part]

                def ordered(i):
                    i.then_inc(order, 1)
                    dve.wait_ge(order, o.next())

                ordered(nc.vector.tensor_reduce(mx_, lg_, AX.X, ALU.max))
                nc.vector.tensor_tensor(lg_, lg_, wide(mx_), ALU.subtract).then_inc(less, 1)
                dve.wait_ge(exped, c + 1)
                ordered(nc.vector.tensor_reduce(mx_, ex_, AX.X, ALU.max))
                ordered(nc.vector.tensor_tensor(one_, ex_, wide(mx_), ALU.is_equal))
                ordered(nc.vector.tensor_tensor(one_, one_, flat(m.prior[:, :]), ALU.mult))
                ordered(nc.vector.tensor_reduce(sm_, one_, AX.X, ALU.max))
                ordered(nc.vector.tensor_tensor(one_, one_, wide(sm_), ALU.is_equal))
                nc.vector.tensor_copy(one16[:, part, :], one_).then_inc(one_ready, 1)
                ordered(nc.vector.tensor_reduce(sm_, ex_, AX.X, ALU.add))
                ordered(nc.vector.reciprocal(sm_, sm_))
                ordered(nc.vector.tensor_tensor(gate_, mx_, sm_, ALU.mult))
                ordered(nc.vector.tensor_tensor(lg_, one_, flat(m.prior[:, :]), ALU.mult))
                ordered(nc.vector.tensor_reduce(esel_, lg_, AX.X, ALU.add))
                ordered(nc.vector.tensor_scalar(esel_, esel_, float(-CAP), float(E1 * CAP), ALU.mult, ALU.add))
                dve.wait_ge(counted, c + 1)
                ordered(nc.vector.tensor_copy(tot_.rearrange("p n e -> p (n e)"), ps_tot[c % 2][:, 0:PT * E1]))
                for e in range(E1):
                    start = inc[c - 1][:, e, PT - 1:PT] if c else 0.0
                    i = nc.vector.tensor_tensor_scan(inc[c][:, e, :], onesf[:, :], tot_[:, :, e], start,
                                                     ALU.mult, ALU.add)
                ordered(i)
                by_tile = inc[c][:, :, :].rearrange("p e n -> p n e")
                ordered(nc.vector.tensor_tensor(tot_, by_tile, tot_, ALU.subtract))
                ordered(nc.vector.tensor_tensor(tot_, tot_, ps_pre[c % 2][:, 0:PT * E1].rearrange("p (n e) -> p n e", e=E1),
                                                ALU.add))
                ordered(nc.vector.tensor_tensor(tot_, tot_, one_, ALU.mult))
                ordered(nc.vector.tensor_reduce(rank_, tot_, AX.X, ALU.add))
                ordered(nc.vector.tensor_tensor(slot_, esel_, rank_, ALU.add))
                ordered(nc.vector.tensor_scalar(keep_, rank_, float(CAP), None, ALU.is_lt))
                ordered(nc.vector.tensor_scalar(rank_, keep_, -1.0e6, 1.0e6, ALU.mult, ALU.add))
                ordered(nc.vector.tensor_tensor(rank_, rank_, slot_, ALU.add))
                dve.wait_ge(y_kept, (c + 1) * GROUPS // PARTS)
                nc.vector.tensor_copy(m.to_slot[:, part], rank_).then_inc(slot_ready, 1)


def experts1(nc, m, w, out):
    S = 2 * P
    BL = CAP // S
    C = F1 // P
    R = 2 * BL
    AHEAD = 5
    with ExitStack() as ctx:
        sb = lambda n, s, d=f32: ctx.enter_context(nc.sbuf_tensor(f"e1_{n}", s, d))
        ps = lambda n, s, d=f32: ctx.enter_context(nc.psum_tensor(f"e1_{n}", s, d))
        new_sem = ctx.enter_context(semaphores(nc))
        sem = lambda n: new_sem(f"e1_{n}")
        w1, w2 = sb("w1", [P, 2, F1]), sb("w2", [P, 2, C, D])
        b1, b2 = sb("b1", [P, 2, C]), sb("b2", [P, 2])
        tok = sb("tok", [P, R, 2, ROW])
        xT = sb("xT", [P, 2, S])
        hid = sb("hid", [P, 2, C, S])
        yT = sb("yT", [P, 2, S])
        res = sb("res", [P, R, 2, D])
        turn, psy, pst = ps("turn", [P, 512]), ps("y", [P, 512]), ps("t", [P, 512])
        psh = [ps(f"h{i}", [P, 512]) for i in range(4)]
        w_in = [sem(f"w_in{u}") for u in range(2)]
        tok_in = [sem(f"tok_in{r}") for r in range(R)]
        turned, x_ready, h_ready, h_act, h_dve = (sem(x) for x in ("turned", "x_ready", "h_ready", "h_act", "h_dve"))
        y_ready, y_out, t_ready, res_ready = (sem(x) for x in ("y_ready", "y_out", "t_ready", "res_ready"))
        sent = [sem(f"sent{r}") for r in range(R)]
        SENT = 2 * 16
        block = ctx.enter_context(nc.Block())
        slots = m.slots.rearrange("(b t p) d -> b p t d", t=2, p=P)
        out_rows = out.rearrange("b t d -> (b t) d")

        def experts(eng, step):
            def both(j):
                for u in range(2):
                    for r in range(BL):
                        step(j, u, r)
            both(0)
            with eng.Fori(1, E1 // 2 - 1) as j:
                both(j)
            both(E1 // 2 - 1)
            for r in range(2):
                step(E1 // 2, 0, r)

        def number(j, u, r):
            return j * (2 * BL) + (u * BL + r)

        def run(stage, j, u, r, d):
            k = u * BL + r + d
            j, u, r = j + k // (2 * BL), k // BL % 2, k % BL
            if not isinstance(j, int) or 0 <= number(j, u, r) < E1 * BL:
                stage(j, u, r)

        @block.gpsimd
        def _(pool):
            for i in range(E1 * BL):
                pool.wait_ge(res_ready, i + 1)
                for t in range(2):
                    nc.gpsimd.indirect_dma_start(out=out_rows, out_offset=bass.IndirectOffsetOnAxis(
                        ap=tok[:, i % R, t, NUMBER:ROW].bitcast(u32), axis=0), in_=res[:, i % R, t, :],
                        in_offset=None, bounds_check=B * T - 1, oob_is_err=False).then_inc(sent[i % R], 16)
            for place in range(R):
                pool.wait_ge(sent[place], SENT * (E1 // 2))

        @block.sync
        def _(sp):
            def weights(j, u):
                e = j * 2 + u
                sp.dma_start(w1[:, u, :], w["w1"][bass.ds(e, 1), :, :].rearrange("o d h -> (o d) h")).then_inc(w_in[u], 16)
                sp.dma_start(w2[:, u, :, :], w["w2"][bass.ds(e, 1), :, :].rearrange("o (c p) d -> (o p) c d", p=P))\
                    .then_inc(w_in[u], 16)
                sp.dma_start(b1[:, u, :], w["b1"][bass.ds(e, 1), :, :].rearrange("o p c -> (o p) c")).then_inc(w_in[u], 16)
                sp.dma_start(b2[:, u:u + 1], w["b2"][bass.ds(e, 1), :, :].rearrange("o p c -> (o p) c"))\
                    .then_inc(w_in[u], 16)

            for u in range(2):
                weights(0, u)

            def fetch(j, u, r):
                i, place = number(j, u, r), u * BL + r
                if past(j):
                    sp.wait_ge(sent[place], j * SENT)
                sp.dma_start(tok[:, place, :, :], slots[bass.ds(i, 1), :, :, :].rearrange("o p t d -> (o p) t d"))\
                    .then_inc(tok_in[place], 16)

            for d in range(AHEAD):
                run(fetch, 0, 0, 0, d)

            def step(j, u, r):
                run(fetch, j, u, r, AHEAD)
                if r == 2 and not (isinstance(j, int) and not 1 <= j * 2 + u < E1 - 1):
                    sp.wait_ge(y_out, (j * 2 + u) * BL)
                    weights(j + u, 1 - u)
            experts(sp, step)

        @block.scalar
        def _(act):
            def take(j, u, r):
                i = number(j, u, r)
                act.wait_ge(turned, i + 1)
                if past(i - 1):
                    act.wait_ge(h_ready, (i - 1) * 2)
                nc.scalar.activation(xT[:, (u * BL + r) % 2, :], turn[:, 0:S], ACT.Copy).then_inc(x_ready, 1)

            def hidden(j, u, r):
                i = number(j, u, r)
                v = (u * BL + r) % 2
                if r == 0:
                    act.wait_ge(w_in[u], (j + 1) * 64)
                act.wait_ge(h_ready, i * 2 + 1)
                if past(i - 1):
                    act.wait_ge(y_ready, i - 1)
                for c in (0, 1):
                    k = nc.scalar.activation(hid[:, v, c, :], psh[2 * v][:, c * S:(c + 1) * S], ACT.Relu,
                                             bias=b1[:, u, c:c + 1])
                k.then_inc(h_act, 1)

            def keep_outputs(j, u, r):
                i = number(j, u, r)
                v = (u * BL + r) % 2
                act.wait_ge(y_ready, i + 1)
                if past(i - 1):
                    act.wait_ge(t_ready, i - 1)
                nc.scalar.activation(yT[:, v, :], psy[:, 0:S], ACT.Identity, bias=b2[:, u:u + 1])\
                    .then_inc(y_out, 1)

            take(0, 0, 0)

            def step(j, u, r):
                run(hidden, j, u, r, 0)
                run(take, j, u, r, 1)
                run(keep_outputs, j, u, r, -1)
            experts(act, step)

        @block.vector
        def _(dve):
            def give(j, u, r):
                i = number(j, u, r)
                dve.wait_ge(t_ready, i + 1)
                place = u * BL + r
                if past(j):
                    dve.wait_ge(sent[place], j * SENT)
                for t in range(2):
                    k = nc.vector.scalar_tensor_tensor(out=res[:, place, t, :], in0=pst[:, t * P:(t + 1) * P],
                                                       scalar=tok[:, place, t, GATE:GATE + 1],
                                                       in1=tok[:, place, t, D:2 * D], op0=ALU.mult, op1=ALU.add)
                k.then_inc(res_ready, 1)

            def hidden(j, u, r):
                i = number(j, u, r)
                v = (u * BL + r) % 2
                if r == 0:
                    dve.wait_ge(w_in[u], (j + 1) * 64)
                dve.wait_ge(h_ready, i * 2 + 2)
                if past(i - 1):
                    dve.wait_ge(y_ready, i - 1)
                for c in (2, 3):
                    k = nc.vector.tensor_scalar(hid[:, v, c, :], psh[2 * v + 1][:, (c - 2) * S:(c - 1) * S],
                                                b1[:, u, c:c + 1], 0.0, ALU.add, ALU.max)
                k.then_inc(h_dve, 1)

            def step(j, u, r):
                run(hidden, j, u, r, 0)
                run(give, j, u, r, -2)
            experts(dve, step)

        @block.tensor
        def _(pe):
            def turns(j, u, r):
                i = number(j, u, r)
                pe.wait_ge(tok_in[u * BL + r], (j + 1) * 16)
                if past(i):
                    pe.wait_ge(x_ready, i)
                for t in range(2):
                    k = nc.tensor.transpose(turn[:, t * P:(t + 1) * P], tok[:, u * BL + r, t, 0:D], m.ident[:, :])
                k.then_inc(turned, 1)

            def hidden(j, u, r):
                i = number(j, u, r)
                v = (u * BL + r) % 2
                if r == 0:
                    pe.wait_ge(w_in[u], (j + 1) * 64)
                pe.wait_ge(x_ready, i + 1)
                for c in range(C):
                    if c % 2 == 0 and past(i - 1):
                        pe.wait_ge(h_dve if c else h_act, i - 1)
                    k = nc.tensor.matmul(psh[2 * v + c // 2][:, (c % 2) * S:(c % 2 + 1) * S],
                                         w1[:, u, c * P:(c + 1) * P], xT[:, v, :], start=True, stop=True)
                    if c % 2:
                        k.then_inc(h_ready, 1)

            def outputs(j, u, r):
                i = number(j, u, r)
                v = (u * BL + r) % 2
                pe.wait_ge(h_act, i + 1)
                if past(i):
                    pe.wait_ge(y_out, i)
                for c in range(C):
                    if c == 2:
                        pe.wait_ge(h_dve, i + 1)
                    k = nc.tensor.matmul(psy[:, 0:S], w2[:, u, c, :], hid[:, v, c, :], start=c == 0, stop=c == C - 1)
                k.then_inc(y_ready, 1)

            def turn_outputs(j, u, r):
                i = number(j, u, r)
                v = (u * BL + r) % 2
                pe.wait_ge(y_out, i + 1)
                if past(i):
                    pe.wait_ge(res_ready, i)
                for t in range(2):
                    k = nc.tensor.transpose(pst[:, t * P:(t + 1) * P], yT[:, v, t * P:(t + 1) * P], m.ident[:, :])
                k.then_inc(t_ready, 1)

            turns(0, 0, 0)

            def step(j, u, r):
                run(hidden, j, u, r, 0)
                run(turn_outputs, j, u, r, -2)
                run(turns, j, u, r, 1)
                run(outputs, j, u, r, -1)
            experts(pe, step)


class Kept:
    pass


def two_layers(nc, x, a, out):
    with ExitStack() as ctx:
        m = Kept()
        sb = lambda n, s, d=f32: ctx.enter_context(nc.sbuf_tensor(f"kept_{n}", s, d))
        dram = lambda n, s, d=f32: nc.dram_tensor(n, s, d, kind="Internal").ap()
        m.rows = sb("rows", [P, NT, ROW])
        m.y, m.x, m.gate = m.rows[:, :, 0:D], m.rows[:, :, D:2 * D], m.rows[:, :, GATE]
        number = m.rows[:, :, NUMBER].bitcast(u32)
        m.lat = sb("lat", [P, NT, LAT])
        m.x_stat, m.x_rstd = sb("x_stat", [P, NT, 2]), sb("x_rstd", [P, NT])
        m.moments = sb("moments", [P, NT, 6])
        m.lat_stat, m.lat_rstd = sb("lat_stat", [P, NT, 2]), sb("lat_rstd", [P, NT])
        m.y_stat, m.y_rms = sb("y_stat", [P, NT, 2]), sb("y_rms", [P, NT])
        m.qst, m.kst = sb("qst", [P, 4, UP, T], bf16), sb("kst", [P, 4, 2, UP, T], bf16)
        m.ident, m.ident16 = sb("ident", [P, P]), sb("ident16", [P, P], bf16)
        m.mask_qk, m.mask_kq = sb("mask_qk", [P, 2, P], bf16), sb("mask_kq", [P, P], bf16)
        m.before, m.ones16 = sb("before", [P, P], bf16), sb("ones16", [P, P], bf16)
        m.prior = sb("prior", [P, E1])
        m.proj_bias = sb("proj_bias", [P, D])
        m.out_bias = sb("out_bias", [P, D])
        m.to_slot = sb("to_slot", [P, NT], u32)
        m.qk_dram = dram("qk_stacks", (B, 12, HD, 2, PAIRS, T), bf16)
        m.v_dram = dram("v_rows", (B, P, TT, H * VW))
        m.slots = dram("slots", (SLOTS, ROW))
        m.serial = 0

        with ExitStack() as c:
            sem = c.enter_context(semaphores(nc))
            PIECES = 8
            x_in = [sem(f"x_in{n}") for n in range(PIECES)]
            bias_in, filled, made = sem("bias_in"), sem("filled"), sem("made")
            block = c.enter_context(nc.Block())

            @block.sync
            def _(sp):
                view = x.rearrange("b (t p) d -> p (b t) d", p=P)
                K = NT // PIECES
                for n in range(PIECES):
                    sp.dma_start(m.x[:, n * K:(n + 1) * K, :], view[:, n * K:(n + 1) * K, :]).then_inc(x_in[n], 16)
                sp.dma_start(m.proj_bias[:, :], a["L1_attn_bproj"].partition_broadcast(P)).then_inc(bias_in, 16)
                sp.dma_start(m.out_bias[:, :], a["L0_attn_out_b"].partition_broadcast(P)).then_inc(bias_in, 16)
                sp.wait_ge(bias_in, 32)

            @block.vector
            def _(dve):
                nc.vector.memset(m.ones16[:, :], 1.0)
                for n in range(PIECES):
                    dve.wait_ge(x_in[n], 16)
                    take_moments(nc, m, m.x, n * (NT // PIECES), NT // PIECES)

            @block.gpsimd
            def _(pool):
                p = nc.gpsimd
                n = 0

                def fill(tile, value):
                    p.memset(tile, value).then_inc(filled, 1)

                p.iota(number, pattern=[[P, NT]], base=0, channel_multiplier=1)
                kst = m.kst[:, :, :, :, :]
                fill(m.ident[:, :], 0.0)
                fill(m.ident16[:, :], 0.0)
                fill(m.mask_qk[:, :, :], 0.0)
                fill(m.mask_kq[:, :], 0.0)
                fill(m.before[:, :], 1.0)
                fill(kst, 0.0)
                for e in range(E1):
                    fill(m.prior[:, e:e + 1], float(E1 - e))
                pool.wait_ge(filled, 6 + E1)
                for t in (m.ident, m.ident16):
                    p.affine_select(out=t[:, :], in_=t[:, :], compare_op=ALU.not_equal, fill=1.0, base=0,
                                    pattern=[[-1, P]], channel_multiplier=1)
                p.affine_select(out=m.mask_qk[:, :, :], in_=m.mask_qk[:, :, :], compare_op=ALU.is_ge, fill=MASKED,
                                base=0, pattern=[[0, 2], [-1, P]], channel_multiplier=1)
                p.affine_select(out=m.mask_kq[:, :], in_=m.mask_kq[:, :], compare_op=ALU.is_ge, fill=MASKED,
                                base=0, pattern=[[1, P]], channel_multiplier=-1)
                p.affine_select(out=m.before[:, :], in_=m.before[:, :], compare_op=ALU.is_gt, fill=0.0,
                                base=0, pattern=[[1, P]], channel_multiplier=-1)
                for x_ in range(2):
                    for r in range(2):
                        part = m.kst[:, :, x_, :, :].rearrange("p k q t -> p k (q t)")
                        n += 1
                        p.affine_select(out=part, in_=part, compare_op=ALU.not_equal, fill=1.0,
                                        base=-(ROWS + 2 * x_ + r), pattern=[[0, 4], [0, UP * T]],
                                        channel_multiplier=1).then_inc(made, 1)
                        pool.wait_ge(made, n)

        layer_stats(nc, "first", m, D, m.x_stat, m.x_rstd, 1e-5)
        m.serial = 1
        project(nc, "plain", m, dict(watt=a["watt"], wvT=a["wvT"], bv=a["L0_attn_wv_b"]))
        attend(nc, "plain", m, dict(woT=a["outT"]))
        layer_stats(nc, "second", m, D, m.x_stat, m.x_rstd, 1e-5)
        project(nc, "queries", m, dict(cos=a["cos"], sin=a["sin"], wqT=a["wqT"], wqrT=a["wqrT"], wdT=a["wdkvT"],
                                       n1=a["n1"]))
        layer_stats(nc, "latent", m, LAT, m.lat_stat, m.lat_rstd, 1e-5)
        project(nc, "keys", m, dict(cos=a["cos"], sin=a["sin"], wkT=a["wukT"], wkrT=a["wukrT"], wvT0=a["wuvT"],
                                    lg=a["ln_g"], lb=a["ln_b"]))
        m.serial = 2
        attend(nc, "causal", m, dict(woT=a["woT"]))
        layer_stats(nc, "third", m, D, m.y_stat, m.y_rms, 1e-6, second_moment=True)
        experts0(nc, m, dict(w1=a["w1T"], w2=a["w2T"], b1=a["b1T"], b2=a["b2T"], gw=a["gwT"], gb=a["L0_ffn_gate_b"],
                             n2=a["n2"]))
        layer_stats(nc, "fourth", m, D, m.x_stat, m.x_rstd, 1e-5)
        project(nc, "cosine", m, dict(wqkv=a["L1_attn_Wqkv"], qs=a["q_scale"], ks=a["k_scale"]))
        m.serial = 3
        attend(nc, "plain", m, dict(woT=a["L1_attn_Wproj"]))
        layer_stats(nc, "fifth", m, D, m.x_stat, m.x_rstd, 1e-5)
        route1(nc, m, dict(gw=a["gate1T"]), out)
        experts1(nc, m, dict(w1=a["L1_ffn_w1"], w2=a["L1_ffn_w2"], b1=a["b11T"], b2=a["b21T"]), out)


def rope_tables():
    half = HD // 2
    inv = (np.float32(1.0) / np.float32(10000.0) ** (np.arange(half, dtype=np.float32) / np.float32(half)))
    ang = np.arange(T, dtype=np.float32)[:, None] * inv[None, :].astype(np.float32)
    sin, cos = np.sin(ang).T, np.cos(ang).T
    return (np.ascontiguousarray(np.tile(np.concatenate([cos, cos]), (H, 1)), np.float32),
            np.ascontiguousarray(np.tile(np.concatenate([-sin, sin]), (H, 1)), np.float32))


def kernel(**inputs):
    import concourse.bacc as bacc
    from concourse.bass_utils import run_bass_kernel_spmd as run

    i = {k: np.asarray(v) for k, v in inputs.items()}
    swap = np.arange(D).reshape(H, 2, HD // 2)[:, ::-1].reshape(D)
    order = np.arange(D).reshape(PAIRS, 2, HD).transpose(2, 1, 0).reshape(D)
    cos, sin = (t[order] for t in rope_tables())
    blocks = np.zeros((D, D), np.float32)
    for h in range(H):
        blocks[HD * h:HD * h + HD, HD * h:HD * h + HD] = i["L0_attn_w_att_val"][h]
    wqkv = np.concatenate([i["L1_attn_Wqkv"][:, :D][:, order], i["L1_attn_Wqkv"][:, D:2 * D][:, order],
                           i["L1_attn_Wqkv"][:, 2 * D:]], 1)
    arrays = {
        "watt": blocks[order][:, order],
        "wvT": i["L0_attn_wv_w"].T[order], "L0_attn_wv_b": i["L0_attn_wv_b"],
        "outT": i["L0_attn_out_w"].T, "L0_attn_out_b": i["L0_attn_out_b"],
        "cos": cos, "sin": sin,
        "wqT": i["L0_ffn_Wq"].T[:, order], "wqrT": i["L0_ffn_Wq"][swap].T[:, order], "wdkvT": i["L0_ffn_Wdkv"].T,
        "wukT": i["L0_ffn_Wuk"].T[:, order], "wukrT": i["L0_ffn_Wuk"][swap].T[:, order], "wuvT": i["L0_ffn_Wuv"].T,
        "woT": i["L0_ffn_Wo"].T,
        "n1": i["L0_ffn_norm1_w"].reshape(D, 1), "n2": i["L0_ffn_norm2_w"].reshape(D, 1),
        "ln_g": i["L0_ffn_ln_g"].reshape(LAT, 1), "ln_b": i["L0_ffn_ln_b"].reshape(LAT, 1),
        "gwT": i["L0_ffn_gate_w"].T, "L0_ffn_gate_b": i["L0_ffn_gate_b"],
        "w1T": i["L0_ffn_W1"].transpose(2, 0, 1),
        "b1T": i["L0_ffn_b1"].reshape(E0, F0 // P, P).transpose(2, 0, 1),
        "w2T": i["L0_ffn_W2"].reshape(E0, D, F0 // P, P).transpose(3, 0, 2, 1),
        "b2T": i["L0_ffn_b2"].T,
        "L1_attn_Wqkv": wqkv, "L1_attn_Wproj": i["L1_attn_Wproj"], "L1_attn_bproj": i["L1_attn_bproj"],
        "q_scale": i["L1_attn_q_scale"][order % HD].reshape(D, 1), "k_scale": i["L1_attn_k_scale"][order % HD].reshape(D, 1),
        "gate1T": i["L1_ffn_gate_w"].T,
        "L1_ffn_w1": i["L1_ffn_w1"], "L1_ffn_w2": i["L1_ffn_w2"],
        "b11T": i["L1_ffn_b1"].reshape(E1, F1 // P, P).transpose(0, 2, 1),
        "b21T": i["L1_ffn_b2"].reshape(E1, D, 1),
    }
    nc = bacc.Bacc("TRN2", target_bir_lowering=False, num_devices=1)
    feeds, aps = {"x": np.ascontiguousarray(i["L0_attn_x"])}, {}
    x = nc.dram_tensor("x", (B, T, D), f32, kind="ExternalInput").ap()
    for name, v in arrays.items():
        feeds["w_" + name] = np.ascontiguousarray(v)
        aps[name] = nc.dram_tensor("w_" + name, v.shape, f32, kind="ExternalInput").ap()
    out = nc.dram_tensor("out", (B, T, D), f32, kind="ExternalOutput").ap()
    two_layers(nc, x, aps, out)
    r = run(nc, [feeds], core_ids=[0])
    return r.results[0]["out"]
```
